# Optimizing a Trainium2 kernel written in Bass

```python
import numpy as np
import jax
import jax.numpy as jnp

def _softmax(x, axis=-1):
    return jax.nn.softmax(x, axis=axis)

def _gelu(x):
    return jax.nn.gelu(x, approximate=True)

def _silu(x):
    return jax.nn.silu(x)

def _sigmoid(x):
    return jax.nn.sigmoid(x)

def _layernorm(x, axis=-1, eps=1e-05):
    m = jnp.mean(x, axis=axis, keepdims=True)
    v = jnp.var(x, axis=axis, keepdims=True)
    return (x - m) / jnp.sqrt(v + eps)

def _scatter_add(tgt, idx, src, axis=0):
    return tgt.at[idx].add(src)

def _segment_sum(src, seg, n):
    return jax.ops.segment_sum(src, seg, n)
kernel_name = 'mk_adaln_attn_ffn_d1_seqx_r4_7dde50'

def setup_inputs(seed: int=0):
    np.random.seed(seed)
    _w = jnp.asarray

    def _rec_inputs():
        import jax
        import jax.numpy as jnp
        _rk = jax.random.key(seed)
        x = -0.000125 + 0.9999 * jax.random.normal(jax.random.fold_in(_rk, 1), (4, 512, 512), jnp.float32)
        _lenS = 512 - jax.random.randint(jax.random.fold_in(_rk, 7), (4,), 0, max(1, 512 // 4) + 1, jnp.int32)
        _lenS2 = 512 - jax.random.randint(jax.random.fold_in(_rk, 8), (4,), 0, max(1, 512 // 4) + 1, jnp.int32)
        fside_BxSxS_0 = -1.52775e-05 + 0.999936 * jax.random.normal(jax.random.fold_in(_rk, 11), (4, 512, 512), jnp.float32)
        cond_512 = -5.03954e-05 + 1.00559 * jax.random.normal(jax.random.fold_in(_rk, 12), (4, 128), jnp.float32)
        return (x, fside_BxSxS_0, cond_512)
    x, fside_BxSxS_0, cond_512 = _rec_inputs()

    def _L0_cond_setup():
        import jax, jax.numpy as jnp
        from jax import lax
        import numpy as np
        B, T, C, TD = (8, 512, 512, 128)

        def _bi_wkv(r, k, v, w, u, time_emb):
            tf = jax.nn.sigmoid(jnp.sum(time_emb, axis=-1))[:, None, None]
            decay = jnp.exp(-jnp.exp(w.astype(jnp.float32)))[None, :] * (0.5 + 0.5 * tf[:, :, 0])
            kf = k.astype(jnp.float32)
            vf = v.astype(jnp.float32)
            ek = jnp.exp(jnp.minimum(kf, 30.0))
            ekv = ek * vf

            def step(carry, x):
                a, b = carry
                ekv_t, ek_t = x
                a = a * decay + ekv_t
                b = b * decay + ek_t
                return ((a, b), (a, b))
            ekv_t = jnp.swapaxes(ekv, 0, 1)
            ek_t = jnp.swapaxes(ek, 0, 1)
            init = (jnp.zeros_like(decay), jnp.zeros_like(decay))
            _, (nf, df) = lax.scan(step, init, (ekv_t, ek_t))
            _, (nb, db) = lax.scan(step, init, (ekv_t, ek_t), reverse=True)
            nf = jnp.swapaxes(nf, 0, 1)
            df = jnp.swapaxes(df, 0, 1)
            nb = jnp.swapaxes(nb, 0, 1)
            db = jnp.swapaxes(db, 0, 1)
            euk = jnp.exp(jnp.minimum(u.astype(jnp.float32)[None, None, :] + kf, 30.0))
            num = nf + nb - ekv + euk * vf
            den = df + db - ek + euk
            base = jax.nn.sigmoid(r.astype(jnp.float32)) * (num / jnp.maximum(den, 1e-08))
            out = base * (0.8 + 0.2 * tf)
            return out.astype(r.dtype)
        key = jax.random.key(seed)
        ks = jax.random.split(key, 6)
        return {'r': jax.random.normal(ks[0], (B, T, C), dtype=jnp.float32), 'k': jax.random.normal(ks[1], (B, T, C), dtype=jnp.float32), 'v': jax.random.normal(ks[2], (B, T, C), dtype=jnp.float32), 'w': jax.random.normal(ks[3], (C,), dtype=jnp.float32), 'u': jax.random.normal(ks[4], (C,), dtype=jnp.float32), 'time_emb': jax.random.normal(ks[5], (B, TD), dtype=jnp.float32)}
    _L0_cond_all = _L0_cond_setup()
    _L0_cond_in = {k: v for k, v in _L0_cond_all.items() if k in ('w', 'u')}
    del _L0_cond_all

    def _L0_attn_setup():
        import jax, jax.numpy as jnp
        import numpy as np
        N_HEADS = 16
        D_HEAD = 128
        D_MODEL = 512
        MAXLEN = 512
        key = jax.random.key(seed)
        ks = jax.random.split(key, 9)
        b, t = (2, 512)
        hd = N_HEADS * D_HEAD
        init = 0.02
        return {'x': jax.random.normal(ks[0], (b, t, D_MODEL), dtype=jnp.float32), 'Wq': jax.random.normal(ks[1], (D_MODEL, hd), dtype=jnp.float32) * init, 'bq': jnp.zeros((hd,), dtype=jnp.float32), 'Wk': jax.random.normal(ks[2], (D_MODEL, hd), dtype=jnp.float32) * init, 'bk': jnp.zeros((hd,), dtype=jnp.float32), 'Wv': jax.random.normal(ks[3], (D_MODEL, hd), dtype=jnp.float32) * init, 'bv': jnp.zeros((hd,), dtype=jnp.float32), 'Wo': jax.random.normal(ks[4], (hd, D_MODEL), dtype=jnp.float32) * init, 'bo': jnp.zeros((D_MODEL,), dtype=jnp.float32)}
    _L0_attn_all = _L0_attn_setup()
    _L0_attn_in = {k: v for k, v in _L0_attn_all.items() if k in ('Wq', 'bq', 'Wk', 'bk', 'Wv', 'bv', 'Wo', 'bo')}
    del _L0_attn_all

    def _L0_cond2_setup():
        import jax, jax.numpy as jnp
        from jax import lax
        import numpy as np
        B, T, C, TD = (8, 512, 512, 128)

        def _bi_wkv(r, k, v, w, u, time_emb):
            tf = jax.nn.sigmoid(jnp.sum(time_emb, axis=-1))[:, None, None]
            decay = jnp.exp(-jnp.exp(w.astype(jnp.float32)))[None, :] * (0.5 + 0.5 * tf[:, :, 0])
            kf = k.astype(jnp.float32)
            vf = v.astype(jnp.float32)
            ek = jnp.exp(jnp.minimum(kf, 30.0))
            ekv = ek * vf

            def step(carry, x):
                a, b = carry
                ekv_t, ek_t = x
                a = a * decay + ekv_t
                b = b * decay + ek_t
                return ((a, b), (a, b))
            ekv_t = jnp.swapaxes(ekv, 0, 1)
            ek_t = jnp.swapaxes(ek, 0, 1)
            init = (jnp.zeros_like(decay), jnp.zeros_like(decay))
            _, (nf, df) = lax.scan(step, init, (ekv_t, ek_t))
            _, (nb, db) = lax.scan(step, init, (ekv_t, ek_t), reverse=True)
            nf = jnp.swapaxes(nf, 0, 1)
            df = jnp.swapaxes(df, 0, 1)
            nb = jnp.swapaxes(nb, 0, 1)
            db = jnp.swapaxes(db, 0, 1)
            euk = jnp.exp(jnp.minimum(u.astype(jnp.float32)[None, None, :] + kf, 30.0))
            num = nf + nb - ekv + euk * vf
            den = df + db - ek + euk
            base = jax.nn.sigmoid(r.astype(jnp.float32)) * (num / jnp.maximum(den, 1e-08))
            out = base * (0.8 + 0.2 * tf)
            return out.astype(r.dtype)
        key = jax.random.key(seed)
        ks = jax.random.split(key, 6)
        return {'r': jax.random.normal(ks[0], (B, T, C), dtype=jnp.float32), 'k': jax.random.normal(ks[1], (B, T, C), dtype=jnp.float32), 'v': jax.random.normal(ks[2], (B, T, C), dtype=jnp.float32), 'w': jax.random.normal(ks[3], (C,), dtype=jnp.float32), 'u': jax.random.normal(ks[4], (C,), dtype=jnp.float32), 'time_emb': jax.random.normal(ks[5], (B, TD), dtype=jnp.float32)}
    _L0_cond2_all = _L0_cond2_setup()
    _L0_cond2_in = {k: v for k, v in _L0_cond2_all.items() if k in ('w', 'u')}
    del _L0_cond2_all

    def _L0_ffn_setup():
        import jax, jax.numpy as jnp
        import numpy as np
        NUM_EXPERTS = 32
        TOP_K = 6
        N_GROUPS = 4
        N_LIMITED_GROUPS = 2
        key = jax.random.key(seed)
        ks = jax.random.split(key, 8)
        H, M = (512, 352)
        SH = 2 * M
        s = 0.02
        return {'hidden_states': jax.random.normal(ks[0], (4, 512, H), jnp.float32), 'gate_w': jax.random.normal(ks[1], (H, NUM_EXPERTS), jnp.float32) * s, 'w_gate': jax.random.normal(ks[2], (NUM_EXPERTS, H, M), jnp.float32) * s, 'w_up': jax.random.normal(ks[3], (NUM_EXPERTS, H, M), jnp.float32) * s, 'w_down': jax.random.normal(ks[4], (NUM_EXPERTS, M, H), jnp.float32) * s, 'sw_gate': jax.random.normal(ks[5], (H, SH), jnp.float32) * s, 'sw_up': jax.random.normal(ks[6], (H, SH), jnp.float32) * s, 'sw_down': jax.random.normal(ks[7], (SH, H), jnp.float32) * s}
    _L0_ffn_all = _L0_ffn_setup()
    _L0_ffn_in = {k: v for k, v in _L0_ffn_all.items() if k in ('gate_w', 'w_gate', 'w_up', 'w_down', 'sw_gate', 'sw_up', 'sw_down')}
    del _L0_ffn_all
    return {'x': x, 'fside_BxSxS_0': fside_BxSxS_0, 'cond_512': cond_512, 'L0_cond_w': _L0_cond_in['w'], 'L0_cond_u': _L0_cond_in['u'], 'L0_attn_Wq': _L0_attn_in['Wq'], 'L0_attn_bq': _L0_attn_in['bq'], 'L0_attn_Wk': _L0_attn_in['Wk'], 'L0_attn_bk': _L0_attn_in['bk'], 'L0_attn_Wv': _L0_attn_in['Wv'], 'L0_attn_bv': _L0_attn_in['bv'], 'L0_attn_Wo': _L0_attn_in['Wo'], 'L0_attn_bo': _L0_attn_in['bo'], 'L0_cond2_w': _L0_cond2_in['w'], 'L0_cond2_u': _L0_cond2_in['u'], 'L0_ffn_gate_w': _L0_ffn_in['gate_w'], 'L0_ffn_w_gate': _L0_ffn_in['w_gate'], 'L0_ffn_w_up': _L0_ffn_in['w_up'], 'L0_ffn_w_down': _L0_ffn_in['w_down'], 'L0_ffn_sw_gate': _L0_ffn_in['sw_gate'], 'L0_ffn_sw_up': _L0_ffn_in['sw_up'], 'L0_ffn_sw_down': _L0_ffn_in['sw_down']}

def reference(x, fside_BxSxS_0, cond_512, L0_cond_w, L0_cond_u, L0_attn_Wq, L0_attn_bq, L0_attn_Wk, L0_attn_bk, L0_attn_Wv, L0_attn_bv, L0_attn_Wo, L0_attn_bo, L0_cond2_w, L0_cond2_u, L0_ffn_gate_w, L0_ffn_w_gate, L0_ffn_w_up, L0_ffn_w_down, L0_ffn_sw_gate, L0_ffn_sw_up, L0_ffn_sw_down):
    import jax
    import jax.numpy as jnp

    def _L0_cond_ref(r, k, v, w, u, time_emb):
        import jax, jax.numpy as jnp
        from jax import lax
        import numpy as np
        B, T, C, TD = (8, 512, 512, 128)

        def _bi_wkv(r, k, v, w, u, time_emb):
            tf = jax.nn.sigmoid(jnp.sum(time_emb, axis=-1))[:, None, None]
            decay = jnp.exp(-jnp.exp(w.astype(jnp.float32)))[None, :] * (0.5 + 0.5 * tf[:, :, 0])
            kf = k.astype(jnp.float32)
            vf = v.astype(jnp.float32)
            ek = jnp.exp(jnp.minimum(kf, 30.0))
            ekv = ek * vf

            def step(carry, x):
                a, b = carry
                ekv_t, ek_t = x
                a = a * decay + ekv_t
                b = b * decay + ek_t
                return ((a, b), (a, b))
            ekv_t = jnp.swapaxes(ekv, 0, 1)
            ek_t = jnp.swapaxes(ek, 0, 1)
            init = (jnp.zeros_like(decay), jnp.zeros_like(decay))
            _, (nf, df) = lax.scan(step, init, (ekv_t, ek_t))
            _, (nb, db) = lax.scan(step, init, (ekv_t, ek_t), reverse=True)
            nf = jnp.swapaxes(nf, 0, 1)
            df = jnp.swapaxes(df, 0, 1)
            nb = jnp.swapaxes(nb, 0, 1)
            db = jnp.swapaxes(db, 0, 1)
            euk = jnp.exp(jnp.minimum(u.astype(jnp.float32)[None, None, :] + kf, 30.0))
            num = nf + nb - ekv + euk * vf
            den = df + db - ek + euk
            base = jax.nn.sigmoid(r.astype(jnp.float32)) * (num / jnp.maximum(den, 1e-08))
            out = base * (0.8 + 0.2 * tf)
            return out.astype(r.dtype)
        return _bi_wkv(r, k, v, w, u, time_emb)

    def _L0_attn_ref(x, Wq, bq, Wk, bk, Wv, bv, Wo, bo):
        import jax, jax.numpy as jnp
        import numpy as np
        N_HEADS = 16
        D_HEAD = 128
        D_MODEL = 512
        MAXLEN = 512
        b, t, _ = x.shape
        h, dh = (N_HEADS, D_HEAD)
        scale = 1.0 / np.sqrt(dh).astype(np.float32)
        q = (x @ Wq + bq).reshape(b, h, t, dh)
        k = (x @ Wk + bk).reshape(b, t, h, dh).transpose(0, 2, 3, 1)
        v = (x @ Wv + bv).reshape(b, t, h, dh).transpose(0, 2, 1, 3)
        logits = jnp.einsum('bhtd,bhds->bhts', q, k) * scale
        mask = jnp.triu(jnp.full((t, t), -jnp.inf, dtype=x.dtype), k=1)
        weights = jax.nn.softmax(logits + mask, axis=-1)
        out = jnp.einsum('bhts,bhsd->bhtd', weights, v)
        out = out.transpose(0, 2, 1, 3).reshape(b, t, h * dh)
        return out @ Wo + bo

    def _L0_cond2_ref(r, k, v, w, u, time_emb):
        import jax, jax.numpy as jnp
        from jax import lax
        import numpy as np
        B, T, C, TD = (8, 512, 512, 128)

        def _bi_wkv(r, k, v, w, u, time_emb):
            tf = jax.nn.sigmoid(jnp.sum(time_emb, axis=-1))[:, None, None]
            decay = jnp.exp(-jnp.exp(w.astype(jnp.float32)))[None, :] * (0.5 + 0.5 * tf[:, :, 0])
            kf = k.astype(jnp.float32)
            vf = v.astype(jnp.float32)
            ek = jnp.exp(jnp.minimum(kf, 30.0))
            ekv = ek * vf

            def step(carry, x):
                a, b = carry
                ekv_t, ek_t = x
                a = a * decay + ekv_t
                b = b * decay + ek_t
                return ((a, b), (a, b))
            ekv_t = jnp.swapaxes(ekv, 0, 1)
            ek_t = jnp.swapaxes(ek, 0, 1)
            init = (jnp.zeros_like(decay), jnp.zeros_like(decay))
            _, (nf, df) = lax.scan(step, init, (ekv_t, ek_t))
            _, (nb, db) = lax.scan(step, init, (ekv_t, ek_t), reverse=True)
            nf = jnp.swapaxes(nf, 0, 1)
            df = jnp.swapaxes(df, 0, 1)
            nb = jnp.swapaxes(nb, 0, 1)
            db = jnp.swapaxes(db, 0, 1)
            euk = jnp.exp(jnp.minimum(u.astype(jnp.float32)[None, None, :] + kf, 30.0))
            num = nf + nb - ekv + euk * vf
            den = df + db - ek + euk
            base = jax.nn.sigmoid(r.astype(jnp.float32)) * (num / jnp.maximum(den, 1e-08))
            out = base * (0.8 + 0.2 * tf)
            return out.astype(r.dtype)
        return _bi_wkv(r, k, v, w, u, time_emb)

    def _L0_ffn_ref(hidden_states, gate_w, w_gate, w_up, w_down, sw_gate, sw_up, sw_down):
        import jax, jax.numpy as jnp
        import numpy as np
        NUM_EXPERTS = 32
        TOP_K = 6
        N_GROUPS = 4
        N_LIMITED_GROUPS = 2
        B, S, H = hidden_states.shape
        E, K = (NUM_EXPERTS, TOP_K)
        x = hidden_states.reshape(-1, H)
        T = x.shape[0]
        scores = jax.nn.sigmoid(x @ gate_w)
        original_scores = scores
        epg = E // N_GROUPS
        sg = scores.reshape(T, N_GROUPS, epg)
        group_scores = jnp.max(sg, axis=-1)
        _, top_groups = jax.lax.top_k(group_scores, N_LIMITED_GROUPS)
        mask = jnp.ones((T, N_GROUPS), dtype=bool)
        mask = mask.at[jnp.arange(T)[:, None], top_groups].set(False)
        sg = jnp.where(mask[:, :, None], -jnp.inf, sg)
        masked_scores = sg.reshape(T, E)
        _, selected_experts = jax.lax.top_k(masked_scores, K)
        weights = jnp.take_along_axis(original_scores, selected_experts, axis=-1)
        weights = weights / jnp.sum(weights, axis=-1, keepdims=True)
        sel_flat = selected_experts.ravel()
        x_exp = jnp.repeat(x, K, axis=0)
        sort_idx = jnp.argsort(sel_flat)
        xs = x_exp[sort_idx]
        group_sizes = jnp.bincount(sel_flat, length=E).astype(jnp.int32)
        g = jax.lax.ragged_dot(xs, w_gate, group_sizes)
        u = jax.lax.ragged_dot(xs, w_up, group_sizes)
        d = jax.lax.ragged_dot(jax.nn.silu(g) * u, w_down, group_sizes)
        unsort_idx = jnp.argsort(sort_idx)
        out = d[unsort_idx].reshape(T, K, H)
        expert_out = jnp.sum(out * weights[..., None], axis=1)
        shared = jax.nn.silu(x @ sw_gate) * (x @ sw_up) @ sw_down
        return (expert_out + shared).reshape(B, S, H)
    x = x + _L0_attn_ref(_L0_cond_ref(x, fside_BxSxS_0, fside_BxSxS_0, L0_cond_w, L0_cond_u, cond_512), L0_attn_Wq, L0_attn_bq, L0_attn_Wk, L0_attn_bk, L0_attn_Wv, L0_attn_bv, L0_attn_Wo, L0_attn_bo)
    x = x + _L0_ffn_ref(_L0_cond2_ref(x, fside_BxSxS_0, fside_BxSxS_0, L0_cond2_w, L0_cond2_u, cond_512), L0_ffn_gate_w, L0_ffn_w_gate, L0_ffn_w_up, L0_ffn_w_down, L0_ffn_sw_gate, L0_ffn_sw_up, L0_ffn_sw_down)
    return x

_drawn_inputs = setup_inputs


def setup_inputs(seed=0):
    import zlib

    import numpy as np

    out = dict(_drawn_inputs(seed))
    spreads = {'L0_attn_bq': (0.0, 0.8),
     'L0_attn_bk': (0.0, 0.8),
     'L0_attn_bv': (0.0, 0.1),
     'L0_attn_bo': (0.0, 0.1)}
    factors = {'cond_512': 3.857,
     'L0_cond_u': 4.407,
     'L0_attn_Wq': 8.0,
     'L0_attn_Wk': 8.0,
     'L0_cond2_w': 7.951,
     'L0_cond2_u': 8.0,
     'L0_ffn_gate_w': 8.0,
     'L0_ffn_w_gate': 8.0,
     'L0_ffn_w_up': 8.0,
     'L0_ffn_w_down': 8.0,
     'L0_ffn_sw_gate': 4.965,
     'L0_ffn_sw_up': 4.987,
     'L0_ffn_sw_down': 4.932}
    for name, (base, spread) in spreads.items():
        noise = np.random.default_rng([zlib.crc32(name.encode()), seed]).standard_normal(out[name].shape)
        drawn = base * np.exp(spread * noise) if base else spread * noise
        out[name] = jnp.asarray(drawn.astype(out[name].dtype))
    for name, factor in factors.items():
        out[name] = (out[name] * factor).astype(out[name].dtype)
    return out
```

```python
import numpy as np
import concourse.bass as bass
from concourse import mybir
from contextlib import ExitStack

F32 = mybir.dt.float32
F32R = mybir.dt.float32r
BF16 = mybir.dt.bfloat16
I32 = mybir.dt.int32
U32 = mybir.dt.uint32
ALU = mybir.AluOpType
ACT = mybir.ActivationFunctionType
AX = mybir.AxisListType

P = 128
B, S, C = 4, 512, 512
KC = C // P
TC = S // P
T = B * S
NT = T // P
H, D = 16, 128
HG = 4
NG = H // HG
TD = 128
E, M = 32, 352
SH = 2 * M
NGRP, GSEL, TOPK = 4, 2, 6
EPG = E // NGRP
MCH = [(0, 128), (128, 128), (256, 96)]
SCH = [(128 * i, min(128, SH - 128 * i)) for i in range(-(-SH // P))]
NBLK = (T * TOPK + E * P - 1) // P
NBLK_ROOM = NBLK + 3
SCALE = 1.0 / float(np.sqrt(np.float32(D)))
NEG = -1.0e30
V_BQ, V_BK, V_BV, V_W1, V_W2, V_U1, V_U2, V_BO, V_N = 0, 16, 32, 48, 52, 56, 60, 64, 68


CREDIT = 2


def done(n):
    return n + (1 + CREDIT)


def pipeline(eng, total, unroll, depth, step):
    ahead = -(-depth // unroll) * unroll

    def peeled(n):
        def tile(k):
            m = n - k
            return (m, m % 2, m // 2, m % unroll) if 0 <= m < total else None
        return tile

    def looped(i, u):
        def tile(k):
            m = u - k
            return unroll * i + m, m % 2, (unroll // 2) * i + m // 2, m % unroll
        return tile

    for n in range(ahead):
        step(peeled(n))
    with eng.Fori(ahead // unroll, total // unroll) as i:
        for u in range(unroll):
            step(looped(i, u))
    for n in range(total // unroll * unroll, total + depth):
        step(peeled(n))


def chunk(tensor, n):
    return tensor[:].rearrange("p b k s -> p (b k) s")[:, bass.ds(n, 1), :].rearrange("p o s -> p (o s)")


class GateMath:

    def __init__(self, nc, ctx, name):
        sb = lambda n: ctx.enter_context(nc.sbuf_tensor(f"{name}_{n}", [P, 2, S], F32))
        sem = lambda n: ctx.enter_context(nc.semaphore(f"{name}_{n}"))
        self.nc = nc
        self.kt = sb("kt")
        self.ek, self.eu = sb("ek"), sb("eu")
        self.ekv, self.dl, self.dk = sb("ekv"), sb("dl"), sb("dk")
        self.nf, self.df = sb("nf"), sb("df")
        self.nb, self.db = sb("nb"), sb("db")
        self.min_done = sem("min_done")
        self.exp_done = sem("exp_done")
        self.ekv_done = sem("ekv_done")
        self.dl_done = sem("dl_done")
        self.dk_done = sem("dk_done")
        self.scan_done = sem("scan_done")
        self.sum_done = sem("sum_done")
        self.frac_done = sem("frac_done")

    def minima(self, dve, n, p, ucol):
        dve.wait_ge(self.scan_done, done(n - 2))
        dve.wait_ge(self.dl_done, done(n - 2))
        self.nc.vector.tensor_scalar(self.ek[:, p, :], self.kt[:, p, :], 30.0, None, ALU.min)
        self.nc.vector.tensor_scalar(self.eu[:, p, :], self.kt[:, p, :], ucol, 30.0, ALU.add, ALU.min).then_inc(self.min_done, 1)

    def exponentials(self, act, n, p):
        act.wait_ge(self.min_done, done(n))
        self.nc.scalar.activation(self.ek[:, p, :], self.ek[:, p, :], ACT.Exp)
        self.nc.scalar.activation(self.eu[:, p, :], self.eu[:, p, :], ACT.Exp).then_inc(self.exp_done, 1)

    def products(self, pool, n, p):
        pool.wait_ge(self.exp_done, done(n))
        pool.wait_ge(self.scan_done, done(n - 2))
        pool.wait_ge(self.frac_done, done(n - 2))
        self.nc.gpsimd.tensor_tensor(self.ekv[:, p, :], self.ek[:, p, :], self.kt[:, p, :], ALU.mult).then_inc(self.ekv_done, 1)
        self.nc.gpsimd.tensor_tensor(self.dl[:, p, :], self.eu[:, p, :], self.ek[:, p, :],
                                     ALU.subtract).then_inc(self.dl_done, 1)
        pool.wait_ge(self.dl_done, done(n))
        self.nc.gpsimd.tensor_tensor(self.dk[:, p, :], self.dl[:, p, :], self.kt[:, p, :], ALU.mult).then_inc(self.dk_done, 1)

    def scans(self, dve, n, p, decay, used):
        dve.wait_ge(used, done(n - 2))
        dve.wait_ge(self.ekv_done, done(n))
        dec = decay.broadcast_to([P, S])
        for f, b, src in ((self.nf, self.nb, self.ekv), (self.df, self.db, self.ek)):
            self.nc.vector.tensor_tensor_scan(f[:, p, :], dec, src[:, p, :], 0.0, ALU.mult, ALU.add)
            last = self.nc.vector.tensor_tensor_scan(b[:, p, ::-1], dec, src[:, p, ::-1], 0.0, ALU.mult, ALU.add)
        last.then_inc(self.scan_done, 1)

    def fraction(self, pool, n, p):
        tt = self.nc.gpsimd.tensor_tensor
        pool.wait_ge(self.scan_done, done(n))
        pool.wait_ge(self.dk_done, done(n))
        tt(self.nb[:, p, :], self.nf[:, p, :], self.nb[:, p, :], ALU.add)
        tt(self.db[:, p, :], self.df[:, p, :], self.db[:, p, :], ALU.add).then_inc(self.sum_done, 1)
        pool.wait_ge(self.sum_done, done(n))
        tt(self.nf[:, p, :], self.nb[:, p, :], self.dk[:, p, :], ALU.add)
        tt(self.df[:, p, :], self.db[:, p, :], self.dl[:, p, :], ALU.add).then_inc(self.frac_done, 1)

    def credit_dve(self, dve):
        dve.sem_inc(self.min_done, CREDIT)
        dve.sem_inc(self.scan_done, CREDIT)

    def credit_act(self, act):
        act.sem_inc(self.exp_done, CREDIT)

    def credit_pool(self, pool):
        for s in (self.ekv_done, self.dl_done, self.dk_done, self.sum_done, self.frac_done):
            pool.sem_inc(s, CREDIT)


def first_gate(nc, keep, dr, x, fs, cond, w1, u1, bq, bk, bv, bo, w2, u2):
    xT, ident, cols, bqs, par1, par2 = (keep[k] for k in ("xT", "ident", "cols", "bqs", "par1", "par2"))
    cTh, cTl, kT = keep["cTh"], keep["cTl"], keep["kT"]
    with ExitStack() as ctx:
        sb = lambda n, s, d=F32: ctx.enter_context(nc.sbuf_tensor(n, s, d))
        sem = lambda n: ctx.enter_context(nc.semaphore(n))
        kin = sb("kin", [P, TC, C])
        xin = sb("xin", [P, TC, C])
        rows = sb("rows", [V_N, P])
        te = sb("te", [P, B, TD])
        small = sb("small", [P, 64])
        cur = sb("cur1", [P, 2, 3])
        ex = sb("ex", [P, 2, S])
        rec = sb("rec1", [P, 2, S])
        cc_out = sb("c_out", [P, 2, S])
        psk = [ctx.enter_context(nc.psum_tensor(f"psk{i}", [P, S], F32)) for i in range(2)]
        psx = [ctx.enter_context(nc.psum_tensor(f"psx{i}", [P, S], F32)) for i in range(2)]
        psv = ctx.enter_context(nc.psum_tensor("psv", [P, V_N], F32))
        g = GateMath(nc, ctx, "g1")
        k_in, x_in, v_in, te_in, c_out_sem = (sem(n) for n in ("k_in", "x_in", "v_in", "te_in", "cT_stored"))
        ident_zero, ident_done, v_T, cols_done = (sem(n) for n in ("ident_zero", "ident_done", "v_T", "cols_done"))
        k_T, x_T = sem("k_T"), sem("x_T")
        kt_done, x_done = sem("kt_done"), sem("x_done")
        t_chain, s_chain = sem("time_steps"), sem("decay_steps")
        cur_done, par_done = sem("cur_done1"), sem("par_done")
        max_done, den_done, rec_done, c_done, hi_done, lo_done = (sem(n) for n in ("max1_done", "den1_done", "rec1_done", "c_done", "c_hi", "c_lo"))
        block = ctx.enter_context(nc.Block())
        vec = [(V_BQ, bq, 16), (V_BK, bk, 16), (V_BV, bv, 16), (V_W1, w1, 4), (V_W2, w2, 4), (V_U1, u1, 4),
               (V_U2, u2, 4), (V_BO, bo, 4)]

        @block.sync
        def _(sp):
            for at, v, n in vec:
                sp.dma_start(rows[at:at + n, :], v.rearrange("(r p) -> r p", p=P)).then_inc(v_in, 16)
            sp.dma_start(te[:], cond.partition_broadcast(P)).then_inc(te_in, 16)
            with sp.Fori(0, B) as b:
                sp.wait_ge(k_T, KC * b + CREDIT)
                sp.dma_start(kin[:], fs[bass.ds(b, 1)].rearrange("o (t p) c -> p (o t) c", p=P)).then_inc(k_in, 16)
                sp.wait_ge(x_T, KC * b + CREDIT)
                sp.dma_start(xin[:], x[bass.ds(b, 1)].rearrange("o (t p) c -> p (o t) c", p=P)).then_inc(x_in, 16)
            with sp.Fori(0, B) as b:
                sp.wait_ge(lo_done, KC * b + (KC + CREDIT))
                for h, part in enumerate((cTh, cTl)):
                    dst = dr["cT"][bass.ds(b, 1), :, h * KC * S:(h + 1) * KC * S].rearrange("o p n -> p (o n)")
                    src = part[:, bass.ds(b, 1), :, :].rearrange("p o k s -> p (o k s)").bitcast(F32)
                    sp.dma_start(dst, src).then_inc(c_out_sem, 16)
            sp.wait_ge(c_out_sem, 16 * 2 * B)

        @block.gpsimd
        def _(pool):
            g.credit_pool(pool)
            nc.gpsimd.memset(ident[:], 0.0).then_inc(ident_zero, 1)
            pool.wait_ge(ident_zero, 1)
            nc.gpsimd.affine_select(out=ident[:], in_=ident[:], compare_op=ALU.not_equal, fill=1.0, base=0,
                                    pattern=[[-1, P]], channel_multiplier=1).then_inc(ident_done, 1)

            def step(tile):
                if t := tile(0):
                    g.products(pool, t[0], t[1])
                if t := tile(1):
                    g.fraction(pool, t[0], t[1])

            pipeline(pool, B * KC, KC, 1, step)

        @block.tensor
        def _(pe):
            pe.sem_inc(k_T, CREDIT)
            pe.sem_inc(x_T, CREDIT)
            pe.wait_ge(ident_done, 1)
            pe.wait_ge(v_in, 16 * len(vec))
            nc.tensor.transpose(psv[:], rows[:], ident[0:V_N, 0:V_N]).then_inc(v_T, 1)
            with pe.Fori(0, B) as b:
                for i in range(KC):
                    n = KC * b + i
                    if i == 0:
                        pe.wait_ge(k_in, 16 * b + 16)
                        pe.wait_ge(x_in, 16 * b + 16)
                    pe.wait_ge(kt_done, done(n - 2))
                    for t in range(TC):
                        last = nc.tensor.transpose(psk[i % 2][:, t * P:(t + 1) * P], kin[:, t, i * P:(i + 1) * P], ident[:])
                    last.then_inc(k_T, 1)
                    pe.wait_ge(x_done, done(n - 2))
                    for t in range(TC):
                        last = nc.tensor.transpose(psx[i % 2][:, t * P:(t + 1) * P], xin[:, t, i * P:(i + 1) * P], ident[:])
                    last.then_inc(x_T, 1)

        @block.scalar
        def _(act):
            g.credit_act(act)
            for s in (kt_done, x_done, hi_done):
                act.sem_inc(s, CREDIT)
            act.wait_ge(v_T, 1)
            nc.scalar.activation(cols[:], psv[:], ACT.Copy).then_inc(cols_done, 1)
            act.wait_ge(cols_done, 1)
            nc.scalar.activation(small[:, 0:8], cols[:, V_W1:V_W1 + 8], ACT.Exp).then_inc(s_chain, 1)
            act.wait_ge(s_chain, 1)
            nc.scalar.activation(small[:, 8:16], small[:, 0:8], ACT.Exp, scale=-1.0).then_inc(s_chain, 1)
            act.wait_ge(t_chain, 1)
            nc.scalar.activation(small[:, 20:24], small[:, 16:20], ACT.Exp, scale=-1.0).then_inc(s_chain, 1)

            def step(tile):
                if t := tile(0):
                    n, p = t[:2]
                    act.wait_ge(k_T, done(n))
                    act.wait_ge(g.dk_done, done(n - 2))
                    nc.scalar.activation(g.kt[:, p, :], psk[p][:], ACT.Copy)
                    nc.scalar.activation(chunk(kT, n), psk[p][:], ACT.Copy).then_inc(kt_done, 1)
                    act.wait_ge(x_T, done(n))
                    nc.scalar.activation(chunk(xT, n), psx[p][:], ACT.Copy)
                    act.wait_ge(den_done, done(n - 2))
                    nc.scalar.activation(ex[:, p, :], psx[p][:], ACT.Exp, scale=-1.0).then_inc(x_done, 1)
                    g.exponentials(act, n, p)
                if t := tile(2):
                    n, p = t[:2]
                    act.wait_ge(c_done, done(n))
                    nc.scalar.activation(chunk(cTh, n), cc_out[:, p, :], ACT.Copy).then_inc(hi_done, 1)

            pipeline(act, B * KC, KC, 2, step)

        @block.vector
        def _(dve):
            g.credit_dve(dve)
            for s in (cur_done, max_done, den_done, rec_done, c_done, lo_done):
                dve.sem_inc(s, CREDIT)
            dve.wait_ge(te_in, 16)
            nc.vector.tensor_reduce(small[:, 16:20], te[:], AX.X, ALU.add).then_inc(t_chain, 1)
            dve.wait_ge(s_chain, 3)
            nc.vector.tensor_scalar(small[:, 24:28], small[:, 20:24], 1.0, None, ALU.add).then_inc(t_chain, 1)
            dve.wait_ge(t_chain, 2)
            nc.vector.reciprocal(small[:, 28:32], small[:, 24:28]).then_inc(t_chain, 1)
            dve.wait_ge(t_chain, 3)
            nc.vector.tensor_scalar(small[:, 32:36], small[:, 28:32], 0.5, 0.5, ALU.mult, ALU.add)
            nc.vector.tensor_scalar(small[:, 36:40], small[:, 28:32], 0.2, 0.8, ALU.mult, ALU.add).then_inc(t_chain, 1)
            dve.wait_ge(t_chain, 4)
            for l, par in enumerate((par1, par2)):
                nc.vector.tensor_tensor(par[:, :, :, 0], small[:, 32:36].unsqueeze(2).broadcast_to([P, B, KC]),
                                        small[:, 8 + 4 * l:12 + 4 * l].unsqueeze(1).broadcast_to([P, B, KC]), ALU.mult)
                u_row = (V_U1, V_U2)[l]
                nc.vector.tensor_copy(par[:, :, :, 1], cols[:, u_row:u_row + KC].unsqueeze(1).broadcast_to([P, B, KC]))
                nc.vector.tensor_copy(par[:, :, :, 2], small[:, 36:40].unsqueeze(2).broadcast_to([P, B, KC]))
            nc.vector.tensor_scalar(bqs[:], cols[:, V_BQ:V_BQ + H], SCALE, None, ALU.mult).then_inc(par_done, 1)
            dve.wait_ge(par_done, 1)

            def step(tile):
                if t := tile(0):
                    n, p, _, i = t
                    dve.wait_ge(kt_done, done(n))
                    g.minima(dve, n, p, cols[:, V_U1 + i:V_U1 + i + 1])
                if t := tile(1):
                    n, p = t[:2]
                    dve.wait_ge(c_done, done(n - 2))
                    nc.vector.tensor_copy(cur[:, p, :], chunk(par1, n)).then_inc(cur_done, 1)
                    dve.wait_ge(cur_done, done(n))
                    g.scans(dve, n, p, cur[:, p, 0:1], c_done)
                if t := tile(3):
                    n, p = t[:2]
                    dve.wait_ge(hi_done, done(n))
                    nc.vector.tensor_tensor(chunk(cTl, n), cc_out[:, p, :], chunk(cTh, n).bitcast(F32),
                                            ALU.subtract).then_inc(lo_done, 1)
                if t := tile(2):
                    n, p = t[:2]
                    dve.wait_ge(g.frac_done, done(n))
                    nc.vector.tensor_scalar(g.db[:, p, :], g.df[:, p, :], 1e-8, None, ALU.max).then_inc(max_done, 1)
                    dve.wait_ge(max_done, done(n))
                    dve.wait_ge(x_done, done(n))
                    nc.vector.scalar_tensor_tensor(out=g.df[:, p, :], in0=ex[:, p, :], scalar=1.0,
                                                   in1=g.db[:, p, :], op0=ALU.add, op1=ALU.mult).then_inc(den_done, 1)
                    dve.wait_ge(den_done, done(n))
                    nc.vector.reciprocal(rec[:, p, :], g.df[:, p, :]).then_inc(rec_done, 1)
                    dve.wait_ge(rec_done, done(n))
                    dve.wait_ge(lo_done, done(n - 2))
                    nc.vector.scalar_tensor_tensor(out=cc_out[:, p, :], in0=g.nf[:, p, :], scalar=cur[:, p, 2:3],
                                                   in1=rec[:, p, :], op0=ALU.mult, op1=ALU.mult).then_inc(c_done, 1)

            pipeline(dve, B * KC, KC, 3, step)


def queries_and_second_gate(nc, keep, dr, wq):
    cTh, cTl, kT, par2, bqs, cols = (keep[k] for k in ("cTh", "cTl", "kT", "par2", "bqs", "cols"))
    with ExitStack() as ctx:
        sb = lambda n, s, d=F32: ctx.enter_context(nc.sbuf_tensor(n, s, d))
        sem = lambda n: ctx.enter_context(nc.semaphore(n))
        wraw = sb("wq_raw", [P, 2, KC, P])
        wh = sb("wq_high", [P, 2, KC, P], F32R)
        wl = sb("wq_low", [P, 2, KC, P], F32R)
        qo = sb("q_out", [P, 2, B, S])
        cur = sb("cur2", [P, 2, 3])
        bqc = sb("bq_cur", [P, 2])
        rec = sb("rec2", [P, 2, S])
        fo = sb("f_out", [P, 2, S])
        psq = [ctx.enter_context(nc.psum_tensor(f"psq{i}", [P, S], F32)) for i in range(B)]
        g = GateMath(nc, ctx, "g2")
        wq_in = [sem("wq_in0"), sem("wq_in1")]
        q_out = [sem("q_stored0"), sem("q_stored1")]
        f_out = [sem("f_stored0"), sem("f_stored1")]
        wh_done, wl_done = sem("wq_high_done"), sem("wq_low_done")
        q_done = sem("q_done")
        q_ev = sem("q_left_psum")
        kt_done, cur_done, max_done, rec_done, f_done = (
            sem(n) for n in ("kt2_done", "cur2_done", "max2_done", "rec2_done", "f_done"))
        block = ctx.enter_context(nc.Block())

        @block.sync
        def _(sp):
            def step(tile):
                if t := tile(0):
                    n, p = t[:2]
                    sp.wait_ge(wl_done, done(n - 2))
                    sp.dma_start(wraw[:, p, :, :], wq[:, bass.ds(P * n, P)].rearrange("(k p) m -> p k m", p=P)).then_inc(wq_in[p], 16)
                if t := tile(2):
                    n, p = t[:2]
                    sp.wait_ge(q_ev, B * n + 2 * B)
                    for b in range(B):
                        sp.dma_start(dr["q"][b, :, :, bass.ds(P * n, P)].rearrange("g p m -> p g m"),
                                     qo[:, p, b, :].rearrange("p (g m) -> p g m", g=NG)).then_inc(q_out[p], 16)
                    sp.wait_ge(f_done, done(n))
                    sp.dma_start(dr["f2"][bass.ds(n, 1)].rearrange("o p s -> p (o s)"), fo[:, p, :]).then_inc(f_out[p], 16)

            pipeline(sp, H, 2, 2, step)
            for p in range(2):
                sp.wait_ge(q_out[p], 16 * B * H // 2)
                sp.wait_ge(f_out[p], 16 * H // 2)

        @block.gpsimd
        def _(pool):
            g.credit_pool(pool)

            def step(tile):
                if t := tile(0):
                    g.products(pool, t[0], t[1])
                if t := tile(1):
                    g.fraction(pool, t[0], t[1])

            pipeline(pool, B * KC, 2, 1, step)

        @block.tensor
        def _(pe):
            pe.sem_inc(q_done, B)

            def step(tile):
                n, p = tile(0)[:2]
                pe.wait_ge(wl_done, done(n))
                for b in range(B):
                    pe.wait_ge(q_ev, B * n + (b + 1))
                    i = 0
                    for a, m in ((wh, cTh), (wh, cTl), (wl, cTh)):
                        for k in range(KC):
                            last = nc.tensor.matmul(psq[b][:], a[:, p, k, :], m[:, b, k, :], start=i == 0, stop=i == 3 * KC - 1)
                            i += 1
                    last.then_inc(q_done, 1)

            pipeline(pe, H, 2, 0, step)

        @block.scalar
        def _(act):
            g.credit_act(act)
            act.sem_inc(wh_done, CREDIT)
            act.sem_inc(q_ev, B)

            def step(tile):
                if t := tile(0):
                    n, p, half = t[:3]
                    act.wait_ge(wq_in[p], 16 * half + 16)
                    act.wait_ge(q_done, B * n)
                    nc.scalar.activation(wh[:, p, :, :], wraw[:, p, :, :], ACT.Copy).then_inc(wh_done, 1)
                    g.exponentials(act, n, p)
                if t := tile(1):
                    n, p, half = t[:3]
                    act.wait_ge(q_out[p], 16 * B * half)
                    act.wait_ge(kt_done, done(n))
                    for b in range(B):
                        act.wait_ge(q_done, B * n + (B + b + 1))
                        nc.scalar.activation(qo[:, p, b, :], psq[b][:], ACT.Identity, bias=bqc[:, p:p + 1],
                                             scale=SCALE).then_inc(q_ev, 1)

            pipeline(act, H, 2, 1, step)

        @block.vector
        def _(dve):
            g.credit_dve(dve)
            for s in (kt_done, wl_done, cur_done, max_done, rec_done, f_done):
                dve.sem_inc(s, CREDIT)

            def step(tile):
                if t := tile(0):
                    n, p, _, i = t
                    dve.wait_ge(wh_done, done(n))
                    nc.vector.tensor_tensor(wl[:, p, :, :], wraw[:, p, :, :], wh[:, p, :, :].bitcast(F32),
                                            ALU.subtract).then_inc(wl_done, 1)
                    dve.wait_ge(g.dk_done, done(n - 2))
                    dve.wait_ge(q_ev, B * n)
                    nc.vector.tensor_scalar(bqc[:, p:p + 1], bqs[:, bass.ds(n, 1)], 1.0, None, ALU.mult)
                    nc.vector.tensor_scalar(g.kt[:, p, :], chunk(kT, n), 1.0, None, ALU.mult).then_inc(kt_done, 1)
                    dve.wait_ge(kt_done, done(n))
                    g.minima(dve, n, p, cols[:, V_U2 + i:V_U2 + i + 1])
                if t := tile(1):
                    n, p = t[:2]
                    dve.wait_ge(f_done, done(n - 2))
                    nc.vector.tensor_copy(cur[:, p, :], chunk(par2, n)).then_inc(cur_done, 1)
                    dve.wait_ge(cur_done, done(n))
                    g.scans(dve, n, p, cur[:, p, 0:1], f_done)
                if t := tile(2):
                    n, p, half = t[:3]
                    dve.wait_ge(g.frac_done, done(n))
                    nc.vector.tensor_scalar(g.db[:, p, :], g.df[:, p, :], 1e-8, None, ALU.max).then_inc(max_done, 1)
                    dve.wait_ge(max_done, done(n))
                    nc.vector.reciprocal(rec[:, p, :], g.db[:, p, :]).then_inc(rec_done, 1)
                    dve.wait_ge(rec_done, done(n))
                    dve.wait_ge(f_out[p], 16 * half)
                    nc.vector.scalar_tensor_tensor(out=fo[:, p, :], in0=g.nf[:, p, :], scalar=cur[:, p, 2:3],
                                                   in1=rec[:, p, :], op0=ALU.mult, op1=ALU.mult).then_inc(f_done, 1)

            pipeline(dve, H, 4, 2, step)


S_BANKS = ((0, 2), (3,), (1,))
P_AT = [0, 128, 384, 768]
P_N = 1280
T_BANKS = ((0,), (1, 3), (2,))
T_AT = {0: 0, 1: 512, 3: 896, 2: 1024}
PE_ORDER = "K0 K1 S0 V0 K2 S1 V1 T0 V2 S2 V3 A0 K3 T1 S3 T2 A1 T3 A2 A3 O0 O1 O2 O3".split()
ACT_ORDER = [e for e in PE_ORDER if e[0] != "O"]
DVE_ORDER = "K0 K1 M0 V0 N0 K2 M1 V1 N1 T0 V2 M2 V3 N2 A0 K3 T1 M3 T2 N3 A1 T3 A2 A3 O0 O1 O2 O3".split()
PROJ = [e for e in PE_ORDER if e[0] in "KVO"]
NPROJ = len(PROJ)


def split_products(nc, out, highs_lows, start, stop):
    terms = [(a, b) for (ah, al), (bh, bl) in highs_lows for a, b in ((ah, bh), (ah, bl), (al, bh))]
    for i, (a, b) in enumerate(terms):
        last = nc.tensor.matmul(out, a, b, start=start and i == 0, stop=stop and i == len(terms) - 1)
    return last


def attention(nc, keep, dr, wk, wv, wo):
    xT, ident, cols = keep["xT"], keep["ident"], keep["cols"]
    with ExitStack() as ctx:
        sb = lambda n, s, d=F32: ctx.enter_context(nc.sbuf_tensor(n, s, d))
        sem = lambda n: ctx.enter_context(nc.semaphore(n))
        ps = lambda n: ctx.enter_context(nc.psum_tensor(n, [P, S], F32))
        wraw = sb("w_raw", [P, KC, HG * D])
        wsplit = {w: (sb(f"w{w}_high", [P, KC, HG * D], F32R), sb(f"w{w}_low", [P, KC, HG * D], F32R)) for w in "kvo"}
        cT = sb("cT", [P, 2, KC, S], F32R)
        qraw = sb("q_raw", [P, H, P])
        qh, ql = sb("q_high", [P, HG, S], F32R), sb("q_low", [P, HG, S], F32R)
        kh, kl = sb("k_high", [P, 2, S], F32R), sb("k_low", [P, 2, S], F32R)
        vh, vl = sb("v_high", [P, TC, HG * D], F32R), sb("v_low", [P, TC, HG * D], F32R)
        prob = sb("prob", [P, 2, P_N])
        pth, ptl = sb("pT_high", [P, 2, P_N], F32R), sb("pT_low", [P, 2, P_N], F32R)
        oth, otl = sb("oT_high", [P, HG, S], F32R), sb("oT_low", [P, HG, S], F32R)
        nmax, rsum, rinv = sb("neg_max", [P, 2, TC]), sb("row_sum", [P, 2, TC]), sb("row_inv", [P, 2, TC])
        bias = sb("bias_kv", [P, 2 * HG])
        identb, maskb = sb("ident_b", [P, P], BF16), sb("mask_b", [P, P], BF16)
        zero = sb("zero_row", [P, C])
        pj = [ps("proj0"), ps("proj1")]
        pss = [ps(f"scores{i}") for i in range(3)]
        pst = [ps("weights_T0"), ps("weights_T1")]
        psa = ps("average_T")
        w_in, w_lo = sem("w_in"), sem("w_split")
        cT_in, q_in, q_hi, q_lo = sem("cT_in"), sem("q_in"), sem("q_high_done"), sem("q_split")
        w_hi = sem("w_high_done")
        mask0, mask_done, zero_done, filled = sem("mask_zero"), sem("mask_done"), sem("zero_done"), sem("slots_filled")
        proj_mm, proj_hi, proj_ev = sem("proj_mm"), sem("proj_high"), sem("proj_left")
        s_mm, s_max, s_exp, s_rec, s_norm = (sem(n) for n in ("scores_mm", "max_done", "exp_done", "rinv_done", "norm_done"))
        t_mm, t_hi, t_lo = sem("pT_mm"), sem("pT_high_done"), sem("pT_low_done")
        a_mm, a_hi, a_lo = sem("avg_mm"), sem("oT_high_done"), sem("oT_low_done")
        bias_done = sem("bias_done")
        pool_steps = sem("pool_steps")
        block = ctx.enter_context(nc.Block())
        NIT = NG * B
        FILL = NBLK_ROOM * P // NIT
        FP = 104
        assert FILL * NIT == NBLK_ROOM * P and FILL % FP == 0

        def v_proj(it, e):
            return NPROJ * it + (PROJ.index(e) + 3)

        def v_head(it, h):
            return HG * it + (h + 1 + HG)

        def v_bank(it, h, x):
            return 3 * HG * it + (3 * h + x + 1 + 3 * HG)

        @block.sync
        def _(sp):
            sp.wait_ge(zero_done, 1)
            with sp.Fori(0, NG) as g:
                cs = bass.ds(HG * D * g, HG * D)
                for i, src in enumerate((wk[:, cs].rearrange("(k p) m -> p k m", p=P),
                                         wv[:, cs].rearrange("(k p) m -> p k m", p=P),
                                         wo[cs, :].rearrange("(k p) m -> p k m", p=P))):
                    sp.wait_ge(w_lo, 3 * g + (i + 1))
                    sp.dma_start(wraw[:], src).then_inc(w_in, 16)
                with sp.Fori(0, B) as b:
                    it = B * g + b
                    sp.wait_ge(proj_mm, v_proj(it - 1, "K3") + (NPROJ - 2))
                    sp.dma_start(cT[:].rearrange("p a k s -> p (a k s)").bitcast(F32),
                                 dr["cT"][bass.ds(b, 1)].rearrange("o p n -> p (o n)")).then_inc(cT_in, 16)
                    sp.wait_ge(q_lo, it + 1)
                    sp.dma_start(qraw[:], dr["q"][bass.ds(b, 1), bass.ds(g, 1)]
                                 .rearrange("o u p (j t) -> p (o u j) t", j=H)).then_inc(q_in, 16)
                    sp.dma_start(dr["xs"][bass.ds(FILL * it, FILL), :].rearrange("(p r) c -> p r c", p=FP),
                                 zero[0:FP, :].unsqueeze(1).broadcast_to([FP, FILL // FP, C])).then_inc(filled, 16)
            sp.wait_ge(filled, 16 * NIT)

        @block.gpsimd
        def _(pool):
            nc.gpsimd.memset(zero[:], 0.0).then_inc(zero_done, 1)
            nc.gpsimd.memset(identb[:], 0.0).then_inc(mask0, 1)
            nc.gpsimd.memset(maskb[:], 0.0).then_inc(mask0, 1)
            pool.wait_ge(mask0, 2)
            nc.gpsimd.affine_select(out=identb[:], in_=identb[:], compare_op=ALU.not_equal, fill=1.0, base=0,
                                    pattern=[[-1, P]], channel_multiplier=1).then_inc(mask_done, 1)
            nc.gpsimd.affine_select(out=maskb[:], in_=maskb[:], compare_op=ALU.is_ge, fill=NEG, base=0,
                                    pattern=[[-1, P]], channel_multiplier=1).then_inc(mask_done, 1)
            pool.sem_inc(w_lo, 1)
            pool.sem_inc(q_lo, 1)

            def split_weights(g, i, w):
                pool.wait_ge(w_in, 48 * g + 16 * (i + 1))
                pool.wait_ge(proj_mm, proj_used(g, w))
                pool.sem_inc(pool_steps, 1)
                nc.gpsimd.tensor_scalar(wsplit[w][0][:], wraw[:], 1.0, 1.0, ALU.mult, ALU.mult).then_inc(w_hi, 1)
                pool.wait_ge(w_hi, 3 * g + (i + 1))
                nc.gpsimd.tensor_tensor(wsplit[w][1][:], wraw[:], wsplit[w][0][:].bitcast(F32), ALU.subtract).then_inc(w_lo, 1)

            def proj_used(g, w):
                last = {"k": "K3", "v": "V3", "o": "O3"}[w]
                return v_proj(B * g - 1, last) + (NPROJ - 2)

            def split_queries(it):
                pool.wait_ge(q_in, 16 * it + 16)
                pool.wait_ge(s_mm, v_bank(it - 1, HG - 1, 2))
                src = qraw[:].rearrange("p j t -> p t j")
                dst = lambda t: t[:].rearrange("p h (t j) -> p (h t) j", j=H)
                pool.sem_inc(pool_steps, 1)
                nc.gpsimd.tensor_scalar(dst(qh), src, 1.0, 1.0, ALU.mult, ALU.mult).then_inc(q_hi, 1)
                pool.wait_ge(q_hi, it + 1)
                nc.gpsimd.tensor_tensor(dst(ql), src, dst(qh).bitcast(F32), ALU.subtract).then_inc(q_lo, 1)

            with pool.Fori(0, NG) as g:
                split_weights(g, 0, "k")
                split_weights(g, 1, "v")
                split_queries(B * g)
                split_weights(g, 2, "o")
                with pool.Fori(1, B) as b:
                    split_queries(B * g + b)

        @block.tensor
        def _(pe):
            pe.sem_inc(proj_mm, NPROJ)
            pe.sem_inc(s_mm, 3 * HG)
            pe.sem_inc(t_mm, 3 * HG)
            pe.sem_inc(a_mm, HG)
            pe.wait_ge(mask_done, 2)
            with pe.Fori(0, NG) as g, pe.Fori(0, B) as b:
                it = B * g + b
                for e in PE_ORDER:
                    kind, h = e[0], int(e[1])
                    if kind in "KVO":
                        out = pj[PROJ.index(e) % 2]
                        pe.wait_ge(proj_ev, v_proj(it, e) - 2)
                    if e == "K0":
                        pe.wait_ge(cT_in, 16 * it + 16)
                        pe.wait_ge(w_lo, 3 * g + 2)
                    if e == "V0":
                        pe.wait_ge(w_lo, 3 * g + 3)
                    if e == "O0":
                        pe.wait_ge(w_lo, 3 * g + 4)
                    if kind == "K":
                        ws = slice(h * D, (h + 1) * D)
                        split_products(nc, out[:], [((wsplit["k"][0][:, k, ws], wsplit["k"][1][:, k, ws]),
                                                     (cT[:, 0, k, :], cT[:, 1, k, :])) for k in range(KC)],
                                       True, True).then_inc(proj_mm, 1)
                    elif kind == "V":
                        ts = slice(h * P, (h + 1) * P)
                        split_products(nc, out[:], [((cT[:, 0, k, ts], cT[:, 1, k, ts]),
                                                     (wsplit["v"][0][:, k, :], wsplit["v"][1][:, k, :])) for k in range(KC)],
                                       True, True).then_inc(proj_mm, 1)
                    elif kind == "O":
                        if h == 0:
                            pe.wait_ge(a_lo, v_head(it, HG - 1))
                        cs = slice(h * P, (h + 1) * P)
                        split_products(nc, out[:], [((wsplit["o"][0][:, k, cs], wsplit["o"][1][:, k, cs]),
                                                     (oth[:, k, :], otl[:, k, :])) for k in range(HG)],
                                       True, True).then_inc(proj_mm, 1)
                    elif kind == "S":
                        if h == 0:
                            pe.wait_ge(q_lo, it + 2)
                        pe.wait_ge(proj_ev, v_proj(it, f"K{h}"))
                        for x, tiles in enumerate(S_BANKS):
                            pe.wait_ge(s_exp, v_bank(it, h - 1, x))
                            at = 0
                            for i in tiles:
                                n, ts = (i + 1) * P, slice(i * P, (i + 1) * P)
                                acc, kk = pss[x][:, at:at + n], slice(0, n)
                                nc.tensor.matmul(acc, qh[:, h, ts], kh[:, h % 2, kk], start=True, stop=False)
                                nc.tensor.matmul(acc[:, n - P:n], identb[:], maskb[:], start=False, stop=False)
                                nc.tensor.matmul(acc, qh[:, h, ts], kl[:, h % 2, kk], start=False, stop=False)
                                last = nc.tensor.matmul(acc, ql[:, h, ts], kh[:, h % 2, kk], start=False, stop=True)
                                at += n
                            last.then_inc(s_mm, 1)
                    elif kind == "T":
                        pe.wait_ge(s_norm, v_head(it, h))
                        for x, tiles in enumerate(T_BANKS):
                            turn = 3 * h + x
                            pe.wait_ge(t_lo, v_bank(it, h, x - 2))
                            at = 0
                            for j in tiles:
                                for i in range(j, TC):
                                    last = nc.tensor.transpose(pst[turn % 2][:, at:at + P],
                                                               prob[:, h % 2, P_AT[i] + j * P:P_AT[i] + (j + 1) * P], ident[:])
                                    at += P
                            last.then_inc(t_mm, 1)
                    elif kind == "A":
                        if h == 0:
                            pe.wait_ge(proj_ev, v_proj(it, "V3"))
                        pe.wait_ge(t_lo, v_bank(it, h, 2))
                        pe.wait_ge(a_lo, v_head(it, h - 1))
                        for j in range(TC):
                            n, ds = (TC - j) * P, slice(h * D, (h + 1) * D)
                            pt = slice(T_AT[j], T_AT[j] + n)
                            last = split_products(nc, psa[:, j * P:], [((vh[:, j, ds], vl[:, j, ds]),
                                                                        (pth[:, h % 2, pt], ptl[:, h % 2, pt]))],
                                                  j == 0, j == TC - 1)
                        last.then_inc(a_mm, 1)

        @block.scalar
        def _(act):
            act.sem_inc(s_exp, 3 * HG)
            act.sem_inc(t_hi, 3 * HG)
            act.sem_inc(a_hi, HG)
            with act.Fori(0, NG) as g, act.Fori(0, B) as b:
                it = B * g + b
                for e in ACT_ORDER:
                    kind, h = e[0], int(e[1])
                    if kind == "K":
                        if h == 0:
                            act.wait_ge(bias_done, it + 1)
                        act.wait_ge(s_mm, v_bank(it, h - 2, 2))
                        act.wait_ge(proj_mm, v_proj(it, e) + (NPROJ - 2))
                        nc.scalar.activation(kh[:, h % 2, :], pj[PROJ.index(e) % 2][:], ACT.Identity,
                                             bias=bias[:, h:h + 1]).then_inc(proj_hi, 1)
                    elif kind == "V":
                        if h == 0:
                            act.wait_ge(a_mm, v_head(it - 1, HG - 1))
                        act.wait_ge(proj_mm, v_proj(it, e) + (NPROJ - 2))
                        nc.scalar.activation(vh[:, h, :], pj[PROJ.index(e) % 2][:], ACT.Copy).then_inc(proj_hi, 1)
                    elif kind == "S":
                        act.wait_ge(t_mm, v_bank(it, h - 2, 2))
                        act.wait_ge(s_norm, v_head(it, h - 2))
                        for x, tiles in enumerate(S_BANKS):
                            act.wait_ge(s_max, v_bank(it, h, x))
                            at = 0
                            for i in tiles:
                                n = (i + 1) * P
                                last = nc.scalar.activation(prob[:, h % 2, P_AT[i]:P_AT[i] + n], pss[x][:, at:at + n], ACT.Exp,
                                                            bias=nmax[:, h % 2, i:i + 1], accum_out=rsum[:, h % 2, i:i + 1])
                                at += n
                            last.then_inc(s_exp, 1)
                    elif kind == "T":
                        act.wait_ge(a_mm, v_head(it, h - 2))
                        for x, tiles in enumerate(T_BANKS):
                            at, n = T_AT[tiles[0]], sum((TC - j) * P for j in tiles)
                            act.wait_ge(t_mm, v_bank(it, h, x))
                            nc.scalar.activation(pth[:, h % 2, at:at + n], pst[(3 * h + x) % 2][:, 0:n], ACT.Copy).then_inc(t_hi, 1)
                    elif kind == "A":
                        if h == 0:
                            act.wait_ge(proj_mm, v_proj(it - 1, "O3") + (NPROJ - 2))
                        act.wait_ge(a_mm, v_head(it, h))
                        nc.scalar.activation(oth[:, h, :], psa[:], ACT.Identity, bias=bias[:, HG + h:HG + h + 1]).then_inc(a_hi, 1)

        @block.vector
        def _(dve):
            dve.sem_inc(proj_ev, 2)
            dve.sem_inc(s_max, 3 * HG)
            dve.sem_inc(s_norm, HG)
            dve.sem_inc(t_lo, 3 * HG)
            dve.sem_inc(a_lo, HG)
            with dve.Fori(0, NG) as g, dve.Fori(0, B) as b:
                it = B * g + b
                dve.wait_ge(a_lo, v_head(it - 1, HG - 1))
                nc.vector.tensor_scalar(bias[:, 0:HG], cols[:, bass.ds(HG * g + V_BK, HG)], 1.0, None, ALU.mult)
                nc.vector.tensor_scalar(bias[:, HG:], cols[:, bass.ds(HG * g + V_BV, HG)], 1.0, None, ALU.mult).then_inc(bias_done, 1)
                dve.wait_ge(bias_done, it + 1)
                for e in DVE_ORDER:
                    kind, h = e[0], int(e[1])
                    if kind in "KVO":
                        bank = pj[PROJ.index(e) % 2]
                    if kind in "KV":
                        kv = [x for x in PROJ if x[0] != "O"]
                        dve.wait_ge(proj_hi, len(kv) * it + (kv.index(e) + 1))
                    if kind == "K":
                        nc.vector.scalar_tensor_tensor(out=kl[:, h % 2, :], in0=bank[:], scalar=bias[:, h:h + 1],
                                                       in1=kh[:, h % 2, :].bitcast(F32), op0=ALU.add,
                                                       op1=ALU.subtract).then_inc(proj_ev, 1)
                    elif kind == "V":
                        nc.vector.tensor_tensor(vl[:, h, :], bank[:], vh[:, h, :].bitcast(F32), ALU.subtract).then_inc(proj_ev, 1)
                    elif kind == "O":
                        dve.wait_ge(proj_mm, v_proj(it, e) + (NPROJ - 2))
                        acc = xT[:, bass.ds(b, 1), h, :].rearrange("p o s -> p (o s)")
                        nc.vector.tensor_tensor(acc, bank[:], acc, ALU.add).then_inc(proj_ev, 1)
                    elif kind == "M":
                        dve.wait_ge(s_exp, v_bank(it, h - 2, 2))
                        for x, tiles in enumerate(S_BANKS):
                            dve.wait_ge(s_mm, v_bank(it, h, x))
                            at = 0
                            for i in tiles:
                                last = nc.vector.tensor_reduce(nmax[:, h % 2, i:i + 1], pss[x][:, at:at + (i + 1) * P], AX.X,
                                                               ALU.max, negate=True)
                                at += (i + 1) * P
                            last.then_inc(s_max, 1)
                    elif kind == "N":
                        dve.wait_ge(s_norm, v_head(it, h - 2))
                        dve.wait_ge(s_exp, v_bank(it, h, 2))
                        nc.vector.reciprocal(rinv[:, h % 2, :], rsum[:, h % 2, :]).then_inc(s_rec, 1)
                        dve.wait_ge(s_rec, HG * it + (h + 1))
                        for i in range(TC):
                            w = prob[:, h % 2, P_AT[i]:P_AT[i] + (i + 1) * P]
                            last = nc.vector.tensor_scalar(w, w, rinv[:, h % 2, i:i + 1], None, ALU.mult)
                        last.then_inc(s_norm, 1)
                    elif kind == "T":
                        for x, tiles in enumerate(T_BANKS):
                            at, n = T_AT[tiles[0]], sum((TC - j) * P for j in tiles)
                            dve.wait_ge(t_hi, v_bank(it, h, x))
                            nc.vector.tensor_tensor(ptl[:, h % 2, at:at + n], pst[(3 * h + x) % 2][:, 0:n],
                                                    pth[:, h % 2, at:at + n].bitcast(F32), ALU.subtract).then_inc(t_lo, 1)
                    elif kind == "A":
                        dve.wait_ge(a_hi, v_head(it, h))
                        nc.vector.scalar_tensor_tensor(out=otl[:, h, :], in0=psa[:], scalar=bias[:, HG + h:HG + h + 1],
                                                       in1=oth[:, h, :].bitcast(F32), op0=ALU.add,
                                                       op1=ALU.subtract).then_inc(a_lo, 1)


POOL_ITEMS = 3


def route_and_shared_up(nc, keep, dr, gate_w, sw_gate, sw_up):
    xT, ident, cols, hsh, wts, slot, tab, blocks = (
        keep[k] for k in ("xT", "ident", "cols", "hsh", "wts", "slot", "tab", "blocks"))
    with ExitStack() as ctx:
        sb = lambda n, s, d=F32: ctx.enter_context(nc.sbuf_tensor(n, s, d))
        sem = lambda n: ctx.enter_context(nc.semaphore(n))
        ps = lambda n, s=(P, S): ctx.enter_context(nc.psum_tensor(n, list(s), F32))
        x2h, x2l = sb("x2_high", [P, B, KC, S], F32R), sb("x2_low", [P, B, KC, S], F32R)
        gw = sb("gate_raw", [P, KC, E])
        gwh, gwl = sb("gate_high", [P, KC, E], F32R), sb("gate_low", [P, KC, E], F32R)
        wraw = sb("sw_raw", [P, 2, 2, KC, P])
        wh, wl = sb("sw_high", [P, 2, 2, KC, P], F32R), sb("sw_low", [P, 2, 2, KC, P], F32R)
        sc = sb("scores", [P, NT, E])
        identb, onesb, before = sb("identb4", [P, P], BF16), sb("onesb", [P, P], BF16), sb("before", [P, P], BF16)
        iota_e, iota_g, iota_q, iota_p = sb("iota_e", [P, E]), sb("iota_g", [P, NGRP]), sb("iota_q", [P, NT]), sb("iota_p", [P, 1])
        sg, us = sb("silu_g", [P, 2, S]), sb("up_out", [P, 2, S])
        with ExitStack() as first:
            sf = lambda n, s, d=F32: first.enter_context(nc.sbuf_tensor(n, s, d))
            f2 = sf("f2", [P, KC, S])
            x2 = sf("x2", [P, KC, S])
            tok = sf("x2_tok", [P, TC, C])
        lt = us[0:E, 0, :]
        with ExitStack() as second:
            sf = lambda n, s, d=F32: second.enter_context(nc.sbuf_tensor(n, s, d))
            gm = sf("group_max", [P, NT, 8])
            gv, gi = sf("group_top", [P, NT, 8]), sf("group_at", [P, NT, 8], U32)
            gif = sf("group_at_f", [P, NT, GSEL])
            gk, gk1 = sf("group_kept", [P, 2, NT, NGRP]), sf("group_off", [P, NT, NGRP])
            wv, ei = sf("expert_top", [P, NT, 8]), sf("expert_at", [P, NT, 8], U32)
            eif, wsum, winv = sf("expert_at_f", [P, NT, 8]), sf("weight_sum", [P, NT]), sf("weight_inv", [P, NT])
            oh = sf("one_hot", [P, TOPK, NT * E])
            chosen = sf("chosen", [P, NT * E], BF16)
            more, nb, incl, base = sf("more", [P, E, NT]), sf("n_blocks", [P, E]), sf("blocks_to", [P, E]), sf("base", [P, E])
            pos, slotf = sf("position", [P, NT, E]), sf("slot_f", [P, TOPK, NT])
            eb, ebb, ebi = sf("block_expert", [P, 2]), sf("block_expert_b", [P, 1], BF16), sf("block_expert_i", [1, 2, P], I32)
            ones_e = sf("ones_e", [P, E])
        with ExitStack() as third:
            sf = lambda n, s, d=F32: third.enter_context(nc.sbuf_tensor(n, s, d))
            stage, sidx = sf("row_stage", [P, 2, C]), sf("slot_stage", [P, 2, 8], I32)
        psl, pslg, psr = ps("logits_ps", (E, S)), ps("scores_ps", (P, TC * E)), ps("route_ps")
        pst = ps("tok_ps")
        psg, psu = [ps("gate_ps0"), ps("gate_ps1")], [ps("up_ps0"), ps("up_ps1")]
        gw_in, gw_hi, gw_lo, consts, masks = sem("gate_in"), sem("gate_hi"), sem("gate_lo"), sem("iotas"), sem("masks")
        f2_in, sg_done, x2_done, x2_hi, x2_lo, x1_done = (sem(n) for n in ("f2_in", "sig_done", "x2_done", "x2_hi", "x2_lo", "x1_done"))
        l_mm, l_ev, l_T, sc_done = sem("logits_mm"), sem("logits_left"), sem("logits_T_done"), sem("scores_done")
        tok_T, tok_ev, tok_st = sem("tok_T"), sem("tok_left"), sem("tok_stored")
        act_steps = sem("act_steps")
        w_in, w_hi, w_lo = [sem("sw_in0"), sem("sw_in1")], sem("sw_hi"), sem("sw_lo")
        u_mm, s_done, h_pool, h_dve = sem("up_mm"), sem("silu_done"), sem("hidden_pool"), sem("hidden_dve")
        pool_steps, pe_steps = sem("pool_steps4"), sem("pe_steps4")
        r, chosen_done, pos_mm, row_done, row_mm, slot_done = (
            sem(n) for n in ("route_steps", "chosen_done", "pos_mm", "row_done", "row_mm", "slot_done"))
        st_in, sidx_done, sent = [sem("stage_in0"), sem("stage_in1")], sem("slot_stage_done"), [sem("sent0"), sem("sent1")]
        block = ctx.enter_context(nc.Block())

        def wait_hidden(eng, m, i, p):
            if m < POOL_ITEMS:
                eng.wait_ge(h_pool, B * m + 2 * i + (p + 1))
            else:
                eng.wait_ge(h_pool, B * POOL_ITEMS + 2)
                eng.wait_ge(h_dve, B * (m - POOL_ITEMS) + 2 * i + (p + 1))

        @block.sync
        def _(sp):
            sp.sem_inc(tok_st, 16)
            sp.dma_start(gw[:], gate_w.rearrange("(k p) e -> p k e", p=P)).then_inc(gw_in, 16)
            def load_shared(m):
                at, n = SCH[m]
                if m >= 2:
                    sp.wait_ge(w_lo, m - 1)
                for i, w in enumerate((sw_gate, sw_up)):
                    sp.dma_start(wraw[:, m % 2, i, :, 0:n], w[:, at:at + n].rearrange("(k p) m -> p k m", p=P)).then_inc(w_in[m % 2], 16)

            load_shared(0)
            load_shared(1)
            with sp.Fori(0, B) as b:
                sp.wait_ge(x2_done, b + 1)
                sp.dma_start(f2[:], dr["f2"][bass.ds(KC * b, KC)].rearrange("k p s -> p k s")).then_inc(f2_in, 16)
                sp.wait_ge(tok_ev, TC * b + (TC + 1))
                sp.dma_start(dr["x2"][bass.ds(S * b, S), :].rearrange("(t p) c -> p t c", p=P), tok[:]).then_inc(tok_st, 16)
            for m in range(2, len(SCH)):
                load_shared(m)
            sp.wait_ge(tok_st, 16 * B + 16)
            sp.wait_ge(slot_done, 1)

            def stage_rows(i, first):
                for p in range(2):
                    if not first:
                        sp.wait_ge(sent[p], 16 * TOPK * i)
                    sp.dma_start(stage[:, p, :], dr["x2"][bass.ds(2 * P * i + p * P, P), :]).then_inc(st_in[p], 16)

            stage_rows(0, True)
            with sp.Fori(1, NT // 2) as i:
                stage_rows(i, False)
            for p in range(2):
                sp.wait_ge(sent[p], 16 * TOPK * NT // 2)

        @block.gpsimd
        def _(pool):
            nc.gpsimd.memset(identb[:], 0.0).then_inc(masks, 1)
            nc.gpsimd.memset(onesb[:], 1.0).then_inc(masks, 1)
            pool.wait_ge(masks, 2)
            nc.gpsimd.affine_select(out=identb[:], in_=identb[:], compare_op=ALU.not_equal, fill=1.0, base=0,
                                    pattern=[[-1, P]], channel_multiplier=1).then_inc(consts, 1)
            nc.gpsimd.affine_select(out=before[:], in_=onesb[:], compare_op=ALU.is_ge, fill=0.0, base=-1,
                                    pattern=[[1, P]], channel_multiplier=-1).then_inc(consts, 1)
            for tile, pattern, cm in ((iota_e, [[1, E]], 0), (iota_g, [[1, NGRP]], 0), (iota_q, [[P, NT]], 0), (iota_p, [[0, 1]], 1)):
                nc.gpsimd.iota(tile[:], pattern=pattern, base=0, channel_multiplier=cm,
                               allow_small_or_imprecise_dtypes=True).then_inc(consts, 1)
            pool.sem_inc(h_pool, 2)
            for m in range(POOL_ITEMS):
                with pool.Fori(0, B // 2) as i:
                    for p in range(2):
                        pool.wait_ge(s_done, B * m + 2 * i + (p + 1))
                        pool.sem_inc(pool_steps, 1)
                        nc.gpsimd.tensor_tensor(hsh[:, m, bass.ds(2 * S * i + p * S, S)], sg[:, p, :], us[:, p, :],
                                                ALU.mult).then_inc(h_pool, 1)
            pool.wait_ge(slot_done, 1)

            def send_rows(i, first):
                for p in range(2):
                    if not first:
                        pool.wait_ge(sent[p], 16 * TOPK * i)
                    pool.sem_inc(pool_steps, 1)
                    nc.gpsimd.tensor_copy(sidx[:, p, :], slot[:, bass.ds(2 * i + p, 1), :].rearrange("p o k -> p (o k)")).then_inc(sidx_done, 1)
                    pool.wait_ge(sidx_done, 2 * i + (p + 1))
                    pool.wait_ge(st_in[p], 16 * i + 16)
                    pool.sem_inc(pool_steps, 1)
                    for k in range(TOPK):
                        pool.indirect_dma_start(dr["xs"], bass.IndirectOffsetOnAxis(ap=sidx[:, p, k:k + 1], axis=0),
                                                stage[:, p, :], None).then_inc(sent[p], 16)

            send_rows(0, True)
            with pool.Fori(1, NT // 2) as i:
                send_rows(i, False)

        @block.tensor
        def _(pe):
            pe.sem_inc(tok_T, TC)
            pe.sem_inc(l_T, 1)
            with pe.Fori(0, B) as b:
                pe.wait_ge(gw_lo, 1)
                pe.wait_ge(x2_lo, b + 2)
                pe.wait_ge(l_ev, b + 1)
                both = lambda k: [t[:, bass.ds(b, 1), k, :].rearrange("p o s -> p (o s)") for t in (x2h, x2l)]
                split_products(nc, psl[:], [((gwh[:, k, :], gwl[:, k, :]), both(k)) for k in range(KC)],
                               True, True).then_inc(l_mm, 1)
                for t in range(TC):
                    pe.wait_ge(tok_ev, TC * b + (t + 1))
                    for k in range(KC):
                        last = nc.tensor.transpose(pst[:, k * P:(k + 1) * P], x2[:, k, t * P:(t + 1) * P], ident[:])
                    last.then_inc(tok_T, 1)
                pe.wait_ge(l_ev, b + 2)
                pe.wait_ge(sc_done, b + 1)
                pe.sem_inc(pe_steps, 1)
                for t in range(TC):
                    last = nc.tensor.transpose(pslg[:, t * E:(t + 1) * E], lt[:, t * P:(t + 1) * P], ident[0:E, 0:E])
                last.then_inc(l_T, 1)

            for m, (at, n) in enumerate(SCH):
                pe.wait_ge(w_lo, m + 1)
                with pe.Fori(0, B // 2) as i:
                    for p in range(2):
                        b = 2 * i + p
                        both = lambda k: [t[:, bass.ds(b, 1), k, :].rearrange("p o s -> p (o s)") for t in (x2h, x2l)]
                        wait_hidden(pe, m, i, p)
                        for j, bank in enumerate((psg[p], psu[p])):
                            last = split_products(nc, bank[0:n, :], [((wh[:, m % 2, j, k, 0:n], wl[:, m % 2, j, k, 0:n]), both(k))
                                                                     for k in range(KC)], True, True)
                        last.then_inc(u_mm, 1)
                if m == 1:
                    pe.wait_ge(chosen_done, 1)
                    pe.wait_ge(sc_done, B + 1)
                    nc.tensor.matmul(psr[:], before[:], chosen[:], start=True, stop=False)
                    for j in range(NT - 1):
                        rest = NT - 1 - j
                        rhs = chosen[:, j * E:(j + 1) * E].unsqueeze(1).broadcast_to([P, rest, E])
                        nc.tensor.matmul(psr[:, (j + 1) * E:], onesb[:], rhs, start=False, stop=j == NT - 2)
                    for j in range(NT):
                        last = nc.tensor.matmul(pslg[:, 0:E], onesb[:], chosen[:, j * E:(j + 1) * E], start=j == 0, stop=j == NT - 1)
                    last.then_inc(pos_mm, 1)
                if m == 3:
                    pe.wait_ge(row_done, 1)
                    nc.tensor.matmul(psl[0:1, 0:P], ebb[:], identb[:], start=True, stop=True).then_inc(row_mm, 1)

        @block.scalar
        def _(act):
            act.wait_ge(gw_in, 16)
            nc.scalar.activation(gwh[:], gw[:], ACT.Copy).then_inc(gw_hi, 1)
            act.sem_inc(l_ev, 1)
            act.sem_inc(sc_done, 1)

            def split_high(m):
                n = SCH[m][1]
                act.wait_ge(w_in[m % 2], 32 * (m // 2 + 1))
                if m >= 2:
                    act.wait_ge(u_mm, B * (m - 1))
                nc.scalar.activation(wh[:, m % 2, :, :, 0:n], wraw[:, m % 2, :, :, 0:n], ACT.Copy).then_inc(w_hi, 1)

            split_high(0)
            with act.Fori(0, B) as b:
                act.wait_ge(tok_T, TC * b + TC)
                act.wait_ge(x2_lo, b + 1)
                act.sem_inc(act_steps, 1)
                for k in range(KC):
                    last = nc.scalar.activation(x2[:, k, :], xT[:, bass.ds(b, 1), k, :].rearrange("p o s -> p (o s)"), ACT.Sigmoid,
                                                bias=cols[:, V_BO + k:V_BO + k + 1])
                last.then_inc(sg_done, 1)
                act.wait_ge(x2_done, b + 2)
                act.sem_inc(act_steps, 1)
                nc.scalar.activation(x2h[:, bass.ds(b, 1), :, :].rearrange("p o k s -> p (o k s)"),
                                     x2[:].rearrange("p k s -> p (k s)"), ACT.Copy).then_inc(x2_hi, 1)
                act.wait_ge(l_mm, b + 1)
                act.wait_ge(l_T, b + 1)
                nc.scalar.activation(lt, psl[:], ACT.Copy).then_inc(l_ev, 1)
                act.wait_ge(l_T, b + 2)
                act.sem_inc(act_steps, 1)
                nc.scalar.activation(sc[:, bass.ds(TC * b, TC), :].rearrange("p t e -> p (t e)"), pslg[:], ACT.Sigmoid).then_inc(sc_done, 1)
            for m, (at, n) in enumerate(SCH):
                if m + 1 < len(SCH):
                    split_high(m + 1)
                with act.Fori(0, B // 2) as i:
                    for p in range(2):
                        wait_hidden(act, m, i, p)
                        act.wait_ge(u_mm, B * m + 2 * i + (p + 1))
                        last = nc.scalar.activation(sg[0:n, p, :], psg[p][0:n, :], ACT.Silu)
                        if m < POOL_ITEMS:
                            last = nc.scalar.activation(us[0:n, p, :], psu[p][0:n, :], ACT.Copy)
                        last.then_inc(s_done, 1)

        @block.vector
        def _(dve):
            step = [0]

            def then(ins):
                step[0] += 1
                ins.then_inc(r, 1)
                dve.wait_ge(r, step[0])

            tt, ts, red = nc.vector.tensor_tensor, nc.vector.tensor_scalar, nc.vector.tensor_reduce
            dve.sem_inc(x2_done, 1)
            dve.sem_inc(x2_lo, 1)
            dve.sem_inc(tok_ev, 1)
            dve.sem_inc(h_dve, 2)
            dve.wait_ge(gw_hi, 1)
            tt(gwl[:], gw[:], gwh[:].bitcast(F32), ALU.subtract).then_inc(gw_lo, 1)

            def split_low(m):
                n = SCH[m][1]
                dve.wait_ge(w_hi, m + 1)
                for j in range(2):
                    last = tt(wl[:, m % 2, j, :, 0:n], wraw[:, m % 2, j, :, 0:n], wh[:, m % 2, j, :, 0:n].bitcast(F32), ALU.subtract)
                last.then_inc(w_lo, 1)

            split_low(0)
            with dve.Fori(0, B) as b:
                dve.wait_ge(sg_done, b + 1)
                for k in range(KC):
                    x1 = xT[:, bass.ds(b, 1), k, :].rearrange("p o s -> p (o s)")
                    ts(x1, x1, cols[:, V_BO + k:V_BO + k + 1], None, ALU.add)
                dve.wait_ge(f2_in, 16 * b + 16)
                tt(x2[:], x2[:], f2[:], ALU.mult).then_inc(x2_done, 1)
                dve.wait_ge(x2_hi, b + 1)
                tt(x2l[:, bass.ds(b, 1), :, :].rearrange("p o k s -> p (o k s)"), x2[:].rearrange("p k s -> p (k s)"),
                   x2h[:, bass.ds(b, 1), :, :].rearrange("p o k s -> p (o k s)").bitcast(F32), ALU.subtract).then_inc(x2_lo, 1)
                dve.wait_ge(tok_st, 16 * b + 16)
                for t in range(TC):
                    dve.wait_ge(tok_T, TC * b + (TC + t + 1))
                    nc.vector.tensor_copy(tok[:, t, :], pst[:]).then_inc(tok_ev, 1)

            dve.wait_ge(tok_st, 16 * B + 16)
            dve.wait_ge(l_T, B + 1)
            dve.wait_ge(sc_done, B + 1)
            dve.wait_ge(consts, 6)
            then(nc.vector.memset(gm[:], -1.0))
            then(red(gm[:, :, 0:NGRP], sc[:].rearrange("p t (g e) -> p t g e", g=NGRP), AX.X, ALU.max))
            for t in range(NT):
                last = nc.vector.max(gv[:, t, :], gm[:, t, :])
            then(last)
            for t in range(NT):
                last = nc.vector.max_index(gi[:, t, :], gv[:, t, :], gm[:, t, :])
            then(last)
            then(nc.vector.tensor_copy(gif[:], gi[:, :, 0:GSEL]))
            for c in range(GSEL):
                last = tt(gk[:, c, :, :], gif[:, :, c:c + 1].broadcast_to([P, NT, NGRP]),
                          iota_g[:].unsqueeze(1).broadcast_to([P, NT, NGRP]), ALU.is_equal)
            then(last)
            then(tt(gk[:, 0, :, :], gk[:, 0, :, :], gk[:, 1, :, :], ALU.add))
            then(ts(gk1[:], gk[:, 0, :, :], -1.0, None, ALU.add))
            spread = lambda g: g.rearrange("p t g -> p (t g)").unsqueeze(2).broadcast_to([P, NT * NGRP, EPG])
            sc3 = sc[:].rearrange("p t (g e) -> p (t g) e", g=NGRP)
            then(tt(sc3, sc3, spread(gk[:, 0, :, :]), ALU.mult))
            then(tt(sc3, sc3, spread(gk1[:]), ALU.add))
            for t in range(NT):
                last = nc.vector.max(wv[:, t, :], sc[:, t, :])
            then(last)
            for t in range(NT):
                last = nc.vector.max_index(ei[:, t, :], wv[:, t, :], sc[:, t, :])
            then(last)
            nc.vector.tensor_copy(eif[:], ei[:])
            then(red(wsum[:], wv[:, :, 0:TOPK], AX.X, ALU.add))
            then(nc.vector.reciprocal(winv[:], wsum[:]))
            tt(wts[:], wv[:], winv[:].unsqueeze(2).broadcast_to([P, NT, 8]), ALU.mult)
            for k in range(TOPK):
                last = tt(oh[:, k, :].rearrange("p (t e) -> p t e", e=E), eif[:, :, k:k + 1].broadcast_to([P, NT, E]),
                          iota_e[:].unsqueeze(1).broadcast_to([P, NT, E]), ALU.is_equal)
            then(last)
            with nc.allow_low_precision(reason="zeros and ones"):
                red(chosen[:], oh[:].rearrange("p k n -> p n k"), AX.X, ALU.add).then_inc(chosen_done, 1)
            split_low(1)
            split_low(2)
            dve.wait_ge(pos_mm, 1)
            then(tt(more[:], pslg[:, 0:E].unsqueeze(2).broadcast_to([P, E, NT]), iota_q[:].unsqueeze(1).broadcast_to([P, E, NT]), ALU.is_gt))
            then(red(nb[:], more[:], AX.X, ALU.add))
            nc.vector.memset(ones_e[:], 1.0)
            then(ts(nb[:], nb[:], 1.0, None, ALU.max))
            then(nc.vector.tensor_tensor_scan(incl[:], ones_e[:], nb[:], 0.0, ALU.mult, ALU.add))
            then(tt(base[:], incl[:], nb[:], ALU.subtract))
            then(ts(base[:], base[:], float(P), None, ALU.mult))
            then(tt(pos[:], psr[:].rearrange("p (t e) -> p t e", e=E), base[:].unsqueeze(1).broadcast_to([P, NT, E]), ALU.add))
            then(tt(oh[:], oh[:], pos[:].rearrange("p t e -> p (t e)").unsqueeze(1).broadcast_to([P, TOPK, NT * E]), ALU.mult))
            then(red(slotf[:].rearrange("p k t -> p (k t)"), oh[:].rearrange("p k (t e) -> p (k t) e", e=E), AX.X, ALU.add))
            nc.vector.memset(slot[:], 0)
            then(ts(more[:, :, 0], incl[:], iota_p[:, 0:1], None, ALU.is_le))
            nc.vector.tensor_copy(slot[:, :, 0:TOPK], slotf[:].rearrange("p k t -> p t k")).then_inc(slot_done, 1)
            then(red(eb[:, 0:1], more[:, :, 0], AX.X, ALU.add))
            then(ts(ebb[:], eb[:, 0:1], float(E - 1), None, ALU.min))
            dve.sem_inc(row_done, 1)
            split_low(3)
            nc.vector.tensor_copy(blocks[:], incl[0:1, :])
            for m in range(POOL_ITEMS, len(SCH)):
                if m == 4:
                    dve.wait_ge(row_mm, 1)
                    then(nc.vector.tensor_copy(ebi[:, 0, :], psl[0:1, 0:P]))
                    then(ts(ebi[:, 1, :], ebi[:, 0, :], 1, None, ALU.bitwise_and))
                    tab2 = tab[:].rearrange("o (b c) -> o b c", c=2)
                    ts(tab2[:, :, 0], psl[0:1, 0:P], 2.0, None, ALU.add)
                    nc.vector.tensor_copy(tab2[:, :, 1], ebi[:, 1, :])
                n = SCH[m][1]
                if 3 < m + 1 < len(SCH):
                    split_low(m + 1)
                with dve.Fori(0, B // 2) as i:
                    for p in range(2):
                        dve.wait_ge(s_done, B * m + 2 * i + (p + 1))
                        tt(hsh[0:n, m, bass.ds(2 * S * i + p * S, S)], sg[0:n, p, :], psu[p][0:n, :], ALU.mult).then_inc(h_dve, 1)


W_UP, W_DOWN, W_N = KC * M, 2 * KC * M, 2 * KC * M + len(MCH) * C


def experts(nc, keep, dr, w_gate, w_up, w_down):
    ident, tab, blocks = keep["ident"], keep["tab"], keep["blocks"]
    with ExitStack() as ctx:
        sb = lambda n, s, d=F32: ctx.enter_context(nc.sbuf_tensor(n, s, d))
        sem = lambda n: ctx.enter_context(nc.semaphore(n))
        ps = lambda n, s=S: ctx.enter_context(nc.psum_tensor(n, [P, s], F32))
        raw = sb("we_raw", [P, W_N])
        wh, wl = sb("we_high", [P, 2, W_N], F32R), sb("we_low", [P, 2, W_N], F32R)
        xg = sb("rows_in", [P, 2, C])
        xth, xtl = sb("xT_high", [P, 2, KC, P], F32R), sb("xT_low", [P, 2, KC, P], F32R)
        sg, hb = sb("silu_e", [P, M]), sb("hidden_e", [P, M])
        hth, htl = sb("hT_high", [P, len(MCH), P], F32R), sb("hT_low", [P, len(MCH), P], F32R)
        yb = sb("rows_out", [P, 2, C])
        psx, psg, psu, psh = ps("xT_ps"), ps("gate_e", M), ps("up_e", M), ps("hT_ps", len(MCH) * P)
        psy = [ps("down_e0"), ps("down_e1")]
        w_in, w_hi, w_ready, pad = sem("we_in"), sem("we_high_done"), sem("we_ready"), sem("we_pad")
        xg_in, y_out = [sem("rows_in0"), sem("rows_in1")], [sem("rows_out0"), sem("rows_out1")]
        x_T, x_hi, x_lo = sem("x_T_e"), sem("x_hi_e"), sem("x_lo_e")
        gu_mm, s_done, h_done = sem("gate_up_mm"), sem("silu_e_done"), sem("hidden_e_done")
        h_T, h_hi, h_lo = sem("h_T_e"), sem("h_hi_e"), sem("h_lo_e")
        d_mm, y_ev, pool_steps = sem("down_mm"), sem("rows_left"), sem("pool_steps5")
        block = ctx.enter_context(nc.Block())

        @block.sync
        def _(sp):
            with sp.Fori(0, E) as e:
                sp.wait_ge(pad, 1)
                sp.wait_ge(w_ready, e + 1)
                one = lambda w: w[bass.ds(e, 1)]
                for at, w in ((0, w_gate), (W_UP, w_up)):
                    sp.dma_start(raw[:, at:at + W_UP].rearrange("p (k m) -> p k m", k=KC),
                                 one(w).rearrange("o (k p) m -> p (o k) m", p=P)).then_inc(w_in, 16)
                sp.dma_start(raw[:, W_DOWN:W_DOWN + 2 * C].rearrange("p (k c) -> p k c", k=2),
                             one(w_down)[:, 0:2 * P, :].rearrange("o (k p) c -> p (o k) c", p=P)).then_inc(w_in, 16)
                sp.dma_start(raw[0:M - 2 * P, W_DOWN + 2 * C:], one(w_down)[:, 2 * P:, :].rearrange("o p c -> p (o c)")).then_inc(w_in, 16)

        @block.gpsimd
        def _(pool):
            pool.sem_inc(w_ready, 1)
            nc.gpsimd.memset(raw[M - 2 * P:, W_DOWN + 2 * C:], 0.0).then_inc(pad, 1)

            def split(e, p, free):
                if free is not None:
                    used = pool.value_load(blocks[0:1, bass.ds(free, 1)], min_val=1, max_val=NBLK)
                    pool.wait_ge(d_mm, used + CREDIT)
                pool.wait_ge(w_in, 64 * e + 64)
                pool.sem_inc(pool_steps, 1)
                nc.gpsimd.tensor_scalar(wh[:, p, :], raw[:], 1.0, 1.0, ALU.mult, ALU.mult).then_inc(w_hi, 1)
                pool.wait_ge(w_hi, e + 1)
                nc.gpsimd.tensor_tensor(wl[:, p, :], raw[:], wh[:, p, :].bitcast(F32), ALU.subtract).then_inc(w_ready, 1)

            split(0, 0, None)
            split(1, 1, None)
            with pool.Fori(1, E // 2) as i:
                for p in range(2):
                    split(2 * i + p, p, 2 * i + (p - 2))

        @block.tensor
        def _(pe):
            for s in (x_T, gu_mm, h_T, d_mm):
                pe.sem_inc(s, CREDIT)

            def step(tile):
                if t := tile(2):
                    n, p = t[:2]
                    pe.wait_ge(h_done, done(n))
                    pe.wait_ge(h_lo, done(n - 1))
                    for c, (at, w) in enumerate(MCH):
                        last = nc.tensor.transpose(psh[0:w, c * P:(c + 1) * P], hb[:, at:at + w], ident[:])
                    last.then_inc(h_T, 1)
                if t := tile(0):
                    n, p, half = t[:3]
                    pe.wait_ge(x_lo, done(n - 1))
                    pe.wait_ge(xg_in[p], 16 * half + 16)
                    for k in range(KC):
                        last = nc.tensor.transpose(psx[:, k * P:(k + 1) * P], xg[:, p, k * P:(k + 1) * P], ident[:])
                    last.then_inc(x_T, 1)
                if t := tile(1):
                    n, p = t[:2]
                    expert = pe.value_load(tab[0:1, bass.ds(2 * n, 1)], min_val=2, max_val=E + 1)
                    buf = pe.value_load(tab[0:1, bass.ds(2 * n + 1, 1)], min_val=0, max_val=1)
                    pe.wait_ge(w_ready, expert)
                    pe.wait_ge(x_lo, done(n))
                    pe.wait_ge(h_done, done(n - 1))
                    for bank, at in ((psg, 0), (psu, W_UP)):
                        part = lambda w, k: w[:, bass.ds(buf, 1), at + k * M:at + (k + 1) * M].rearrange("p o m -> p (o m)")
                        last = split_products(nc, bank[:], [((xth[:, p, k, :], xtl[:, p, k, :]), (part(wh, k), part(wl, k)))
                                                            for k in range(KC)], True, True)
                    last.then_inc(gu_mm, 1)
                if t := tile(2):
                    n, p = t[:2]
                    buf = pe.value_load(tab[0:1, bass.ds(2 * n + 1, 1)], min_val=0, max_val=1)
                    pe.wait_ge(h_lo, done(n))
                    pe.wait_ge(y_ev, done(n - 2))
                    part = lambda w, c: w[0:MCH[c][1], bass.ds(buf, 1), W_DOWN + c * C:W_DOWN + (c + 1) * C].rearrange("p o m -> p (o m)")
                    split_products(nc, psy[p][:], [((hth[0:w, c, :], htl[0:w, c, :]), (part(wh, c), part(wl, c)))
                                                   for c, (at, w) in enumerate(MCH)], True, True).then_inc(d_mm, 1)

            pipeline(pe, NBLK, 2, 2, step)

        @block.scalar
        def _(act):
            for s in (x_hi, s_done, h_hi, y_ev):
                act.sem_inc(s, CREDIT)

            def load(n, p):
                act.dma_start(xg[:, p, :], dr["xs"][bass.ds(P * n, P), :]).then_inc(xg_in[p], 16)

            load(0, 0)
            load(1, 1)

            def step(tile):
                if t := tile(2):
                    n, p = t[:2]
                    act.wait_ge(h_T, done(n))
                    act.wait_ge(d_mm, done(n - 1))
                    nc.scalar.activation(hth[:, 0:2, :], psh[:, 0:2 * P].rearrange("p (c t) -> p c t", c=2), ACT.Copy)
                    nc.scalar.activation(hth[0:M - 2 * P, 2, :], psh[0:M - 2 * P, 2 * P:], ACT.Copy).then_inc(h_hi, 1)
                if t := tile(0):
                    n, p = t[:2]
                    act.wait_ge(x_T, done(n))
                    act.wait_ge(gu_mm, done(n - 2))
                    nc.scalar.activation(xth[:, p, :, :], psx[:].rearrange("p (k t) -> p k t", k=KC), ACT.Copy).then_inc(x_hi, 1)
                    load(n + 2, p)
                if t := tile(1):
                    n, p = t[:2]
                    act.wait_ge(gu_mm, done(n))
                    act.wait_ge(h_done, done(n - 1))
                    nc.scalar.activation(sg[:], psg[:], ACT.Silu).then_inc(s_done, 1)
                if t := tile(2):
                    n, p, half = t[:3]
                    act.wait_ge(y_out[p], 16 * half)
                    act.wait_ge(d_mm, done(n))
                    nc.scalar.activation(yb[:, p, :], psy[p][:], ACT.Copy).then_inc(y_ev, 1)
                    act.wait_ge(y_ev, done(n))
                    act.dma_start(dr["ys"][bass.ds(P * n, P), :], yb[:, p, :]).then_inc(y_out[p], 16)

            pipeline(act, NBLK, 2, 2, step)
            for p in range(2):
                act.wait_ge(y_out[p], 16 * ((NBLK + 1 - p) // 2))
                act.wait_ge(xg_in[p], 16 * ((NBLK + 3 - p) // 2))

        @block.vector
        def _(dve):
            for s in (x_lo, h_done, h_lo):
                dve.sem_inc(s, CREDIT)

            def step(tile):
                if t := tile(2):
                    n, p = t[:2]
                    dve.wait_ge(h_hi, done(n))
                    nc.vector.tensor_tensor(htl[:, 0:2, :], psh[:, 0:2 * P].rearrange("p (c t) -> p c t", c=2),
                                            hth[:, 0:2, :].bitcast(F32), ALU.subtract)
                    nc.vector.tensor_tensor(htl[0:M - 2 * P, 2, :], psh[0:M - 2 * P, 2 * P:],
                                            hth[0:M - 2 * P, 2, :].bitcast(F32), ALU.subtract).then_inc(h_lo, 1)
                if t := tile(0):
                    n, p = t[:2]
                    dve.wait_ge(x_hi, done(n))
                    nc.vector.tensor_tensor(xtl[:, p, :, :], psx[:].rearrange("p (k t) -> p k t", k=KC),
                                            xth[:, p, :, :].bitcast(F32), ALU.subtract).then_inc(x_lo, 1)
                if t := tile(1):
                    n, p = t[:2]
                    dve.wait_ge(s_done, done(n))
                    dve.wait_ge(h_T, done(n - 1))
                    nc.vector.tensor_tensor(hb[:], sg[:], psu[:], ALU.mult).then_inc(h_done, 1)

            pipeline(dve, NBLK, 2, 2, step)


def combine(nc, keep, dr, sw_down, out):
    xT, ident, hsh, wts, slot = (keep[k] for k in ("xT", "ident", "hsh", "wts", "slot"))
    NS = len(SCH)
    with ExitStack() as ctx:
        sb = lambda n, s, d=F32: ctx.enter_context(nc.sbuf_tensor(n, s, d))
        sem = lambda n: ctx.enter_context(nc.semaphore(n))
        raw, wh, wl = sb("sd_raw", [P, NS, C]), sb("sd_high", [P, NS, C], F32R), sb("sd_low", [P, NS, C], F32R)
        hh, hl = sb("h_high", [P, 2, NS, P], F32R), sb("h_low", [P, 2, NS, P], F32R)
        xc = sb("x1_tile", [P, 2, KC, P])
        wt = sb("wts_tile", [P, 2, 8])
        sidx = sb("slot_tile", [P, 2, 8], I32)
        yk = sb("expert_rows", [P, 2, TOPK, C])
        acc, ob = sb("acc", [P, 2, C]), sb("out_rows", [P, 2, C])
        pso = [ctx.enter_context(nc.psum_tensor(f"out_ps{i}", [P, S], F32)) for i in range(2)]
        w_in, w_hi, w_lo = sem("sd_in"), sem("sd_hi"), sem("sd_lo")
        hi, lo, x_c, o_mm = sem("h_hi6"), sem("h_lo6"), sem("x1_copied"), sem("out_mm")
        idx_done, y_in, acc_done, o_done, o_out = (sem("slot6"), [sem("y_in0"), sem("y_in1")], sem("acc_steps"), sem("out_done"),
                                                   [sem("out0"), sem("out1")])
        pool_steps, act_steps = sem("pool_steps6"), sem("act_steps6")
        block = ctx.enter_context(nc.Block())
        tail = SCH[-1][1]

        def loop(eng, step):
            with eng.Fori(0, B) as b:
                for t in range(TC):
                    step(TC * b + t, t % 2, (TC // 2) * b + t // 2, b, t)

        @block.sync
        def _(sp):
            for p in range(2):
                sp.sem_inc(o_out[p], 16)
            sp.dma_start(raw[:, 0:NS - 1, :], sw_down[0:(NS - 1) * P, :].rearrange("(k p) c -> p k c", p=P)).then_inc(w_in, 16)
            sp.dma_start(raw[0:tail, NS - 1, :], sw_down[(NS - 1) * P:, :]).then_inc(w_in, 16)

            def step(n, p, half, b, t):
                sp.wait_ge(o_done, done(n))
                sp.dma_start(out[bass.ds(b, 1), t * P:(t + 1) * P, :].rearrange("o p c -> p (o c)"), ob[:, p, :]).then_inc(o_out[p], 16)

            loop(sp, step)
            for p in range(2):
                sp.wait_ge(o_out[p], 16 * NT // 2 + 16)

        @block.gpsimd
        def _(pool):
            def step(n, p, half, b, t):
                pool.wait_ge(o_done, done(n - 2))
                if not (isinstance(half, int) and half == 0):
                    pool.wait_ge(y_in[p], 16 * TOPK * half)
                pool.sem_inc(pool_steps, 1)
                nc.gpsimd.tensor_copy(sidx[:, p, :], slot[:, bass.ds(n, 1), :].rearrange("p o k -> p (o k)")).then_inc(idx_done, 1)
                pool.wait_ge(idx_done, n + 1)
                pool.sem_inc(pool_steps, 1)
                for k in range(TOPK):
                    pool.indirect_dma_start(yk[:, p, k, :], None, dr["ys"],
                                            bass.IndirectOffsetOnAxis(ap=sidx[:, p, k:k + 1], axis=0)).then_inc(y_in[p], 16)

            for t in range(TC):
                step(t, t % 2, t // 2, 0, t)
            with pool.Fori(1, B) as b:
                for t in range(TC):
                    step(TC * b + t, t % 2, (TC // 2) * b + t // 2, b, t)

        @block.tensor
        def _(pe):
            pe.sem_inc(o_mm, CREDIT)
            pe.wait_ge(w_lo, 1)

            def step(n, p, half, b, t):
                pe.wait_ge(lo, done(n))
                pe.wait_ge(o_done, done(n - 2))
                parts = [((hh[0:w, p, c, :], hl[0:w, p, c, :]), (wh[0:w, c, :], wl[0:w, c, :])) for c, (at, w) in enumerate(SCH)]
                split_products(nc, pso[p][:], parts[:1], True, False)
                pe.wait_ge(x_c, done(n))
                for k in range(KC):
                    nc.tensor.matmul(pso[p][:, k * P:(k + 1) * P], xc[:, p, k, :], ident[:], start=False, stop=False)
                split_products(nc, pso[p][:], parts[1:], False, True).then_inc(o_mm, 1)

            loop(pe, step)

        @block.scalar
        def _(act):
            act.sem_inc(hi, CREDIT)
            act.sem_inc(x_c, CREDIT)
            act.wait_ge(w_in, 32)
            nc.scalar.activation(wh[:, 0:NS - 1, :], raw[:, 0:NS - 1, :], ACT.Copy)
            nc.scalar.activation(wh[0:tail, NS - 1, :], raw[0:tail, NS - 1, :], ACT.Copy).then_inc(w_hi, 1)

            def step(n, p, half, b, t):
                act.wait_ge(o_mm, done(n - 2))
                act.sem_inc(act_steps, 1)
                ts = bass.ds(S * b + t * P, P)
                nc.scalar.activation(hh[:, p, 0:NS - 1, :], hsh[:, 0:NS - 1, ts], ACT.Copy)
                nc.scalar.activation(hh[0:tail, p, NS - 1, :], hsh[0:tail, NS - 1, ts], ACT.Copy).then_inc(hi, 1)
                nc.scalar.activation(xc[:, p, :, :], xT[:, bass.ds(b, 1), :, t * P:(t + 1) * P].rearrange("p o k s -> p (o k) s"),
                                     ACT.Copy).then_inc(x_c, 1)

            loop(act, step)

        @block.vector
        def _(dve):
            dve.sem_inc(lo, CREDIT)
            dve.sem_inc(o_done, CREDIT)
            dve.wait_ge(w_hi, 1)
            nc.vector.tensor_tensor(wl[:, 0:NS - 1, :], raw[:, 0:NS - 1, :], wh[:, 0:NS - 1, :].bitcast(F32), ALU.subtract)
            nc.vector.tensor_tensor(wl[0:tail, NS - 1, :], raw[0:tail, NS - 1, :], wh[0:tail, NS - 1, :].bitcast(F32),
                                    ALU.subtract).then_inc(w_lo, 1)

            def step(n, p, half, b, t):
                dve.wait_ge(hi, done(n))
                ts = bass.ds(S * b + t * P, P)
                nc.vector.tensor_tensor(hl[:, p, 0:NS - 1, :], hsh[:, 0:NS - 1, ts], hh[:, p, 0:NS - 1, :].bitcast(F32), ALU.subtract)
                nc.vector.tensor_tensor(hl[0:tail, p, NS - 1, :], hsh[0:tail, NS - 1, ts], hh[0:tail, p, NS - 1, :].bitcast(F32),
                                        ALU.subtract).then_inc(lo, 1)
                dve.wait_ge(o_done, done(n - 2))
                dve.wait_ge(o_out[p], 16 * half + 16)
                nc.vector.tensor_scalar(wt[:, p, :], wts[:, bass.ds(n, 1), :].rearrange("p o k -> p (o k)"), 1.0, None,
                                        ALU.mult).then_inc(acc_done, 1)
                dve.wait_ge(y_in[p], 16 * TOPK * half + 16 * TOPK)
                dve.wait_ge(o_mm, done(n))
                for k in range(TOPK):
                    dve.wait_ge(acc_done, TOPK * n + (k + 1))
                    last = k == TOPK - 1
                    nc.vector.scalar_tensor_tensor(out=(ob if last else acc)[:, p, :], in0=yk[:, p, k, :], scalar=wt[:, p, k:k + 1],
                                                   in1=acc[:, p, :] if k else pso[p][:], op0=ALU.mult,
                                                   op1=ALU.add).then_inc(o_done if last else acc_done, 1)

            loop(dve, step)


def build(nc, x, fs, cond, w1, u1, wq, bq, wk, bk, wv, bv, wo, bo, w2, u2,
          gate_w, w_gate, w_up, w_down, sw_gate, sw_up, sw_down, out, stages=9):
    top = ExitStack()
    dram = lambda n, s, d=F32: nc.dram_tensor(n, s, d, kind="Internal").ap()
    dr = dict(
        cT=dram("cT_split", [B, P, 2 * KC * S]),
        q=dram("q_T", [B, NG, P, H * P]),
        f2=dram("f2_T", [B * KC, P, S]),
        x2=dram("x2_rows", [T, C]),
        xs=dram("slots_in", [NBLK_ROOM * P, C]),
        ys=dram("slots_out", [NBLK * P, C]),
    )
    with top:
        sb = lambda n, s, d=F32: top.enter_context(nc.sbuf_tensor(n, s, d))
        keep = dict(
            xT=sb("xT", [P, B, KC, S]),
            ident=sb("ident", [P, P]),
            cols=sb("cols", [P, V_N]),
            bqs=sb("bqs", [P, H]),
            par1=sb("par1", [P, B, KC, 3]),
            par2=sb("par2", [P, B, KC, 3]),
        )
        with ExitStack() as two:
            s2 = lambda n, s, d=F32: two.enter_context(nc.sbuf_tensor(n, s, d))
            keep["cTh"] = s2("cTh", [P, B, KC, S], F32R)
            keep["cTl"] = s2("cTl", [P, B, KC, S], F32R)
            keep["kT"] = s2("kT", [P, B, KC, S])
            first_gate(nc, keep, dr, x, fs, cond, w1, u1, bq, bk, bv, bo, w2, u2)
            if stages >= 2:
                queries_and_second_gate(nc, keep, dr, wq)
        if stages >= 3:
            attention(nc, keep, dr, wk, wv, wo)
        if stages >= 4:
            with ExitStack() as moe:
                s3 = lambda n, s, d=F32: moe.enter_context(nc.sbuf_tensor(n, s, d))
                keep["hsh"] = s3("hsh", [P, len(SCH), T])
                keep["wts"] = s3("wts", [P, NT, 8])
                keep["slot"] = s3("slot", [P, NT, 8], I32)
                keep["tab"] = s3("tab", [1, 2 * P], I32)
                keep["blocks"] = s3("blocks", [1, E], I32)
                route_and_shared_up(nc, keep, dr, gate_w, sw_gate, sw_up)
                if stages >= 5:
                    experts(nc, keep, dr, w_gate, w_up, w_down)
                if stages >= 6:
                    combine(nc, keep, dr, sw_down, out)


_INS = ['x', 'fside_BxSxS_0', 'cond_512', 'L0_cond_w', 'L0_cond_u', 'L0_attn_Wq', 'L0_attn_bq', 'L0_attn_Wk',
        'L0_attn_bk', 'L0_attn_Wv', 'L0_attn_bv', 'L0_attn_Wo', 'L0_attn_bo', 'L0_cond2_w', 'L0_cond2_u',
        'L0_ffn_gate_w', 'L0_ffn_w_gate', 'L0_ffn_w_up', 'L0_ffn_w_down', 'L0_ffn_sw_gate', 'L0_ffn_sw_up',
        'L0_ffn_sw_down']


def kernel(**inputs):
    import concourse.bacc as bacc
    from concourse.bass_utils import run_bass_kernel_spmd

    nc = bacc.Bacc("TRN2", target_bir_lowering=False, num_devices=1)
    arrays, args = {}, []
    for name in _INS:
        a = np.ascontiguousarray(inputs[name])
        arrays[name] = a
        args.append(nc.dram_tensor(name, a.shape, mybir.dt.from_np(a.dtype), kind="ExternalInput").ap())
    args.append(nc.dram_tensor("out", (B, S, C), F32, kind="ExternalOutput").ap())
    build(nc, *args)
    r = run_bass_kernel_spmd(nc, [arrays], core_ids=[0])
    return r.results[0]["out"]
```

```python
import numpy as np
import concourse.bass as bass
from concourse import mybir
from contextlib import ExitStack

F32 = mybir.dt.float32
F32R = mybir.dt.float32r
BF16 = mybir.dt.bfloat16
I32 = mybir.dt.int32
U32 = mybir.dt.uint32
ALU = mybir.AluOpType
ACT = mybir.ActivationFunctionType
AX = mybir.AxisListType

P = 128
B, S, C = 4, 512, 512
KC = C // P
TC = S // P
T = B * S
NT = T // P
H, D = 16, 128
HG = 4
NG = H // HG
TD = 128
E, M = 32, 352
SH = 2 * M
NGRP, GSEL, TOPK = 4, 2, 6
EPG = E // NGRP
MCH = [(0, 128), (128, 128), (256, 96)]
SCH = [(128 * i, min(128, SH - 128 * i)) for i in range(-(-SH // P))]
NBLK = (T * TOPK + E * P - 1) // P
NBLK_ROOM = NBLK + 3
SCALE = 1.0 / float(np.sqrt(np.float32(D)))
NEG = -1.0e30
V_BQ, V_BK, V_BV, V_W1, V_W2, V_U1, V_U2, V_BO, V_N = 0, 16, 32, 48, 52, 56, 60, 64, 68


CREDIT = 2


def done(n):
    return n + (1 + CREDIT)


def pipeline(eng, total, unroll, depth, step):
    ahead = -(-depth // unroll) * unroll

    def peeled(n):
        def tile(k):
            m = n - k
            return (m, m % 2, m // 2, m % unroll) if 0 <= m < total else None
        return tile

    def looped(i, u):
        def tile(k):
            m = u - k
            return unroll * i + m, m % 2, (unroll // 2) * i + m // 2, m % unroll
        return tile

    for n in range(ahead):
        step(peeled(n))
    with eng.Fori(ahead // unroll, total // unroll) as i:
        for u in range(unroll):
            step(looped(i, u))
    for n in range(total // unroll * unroll, total + depth):
        step(peeled(n))


def chunk(tensor, n):
    return tensor[:].rearrange("p b k s -> p (b k) s")[:, bass.ds(n, 1), :].rearrange("p o s -> p (o s)")


class GateMath:

    def __init__(self, nc, ctx, name):
        sb = lambda n: ctx.enter_context(nc.sbuf_tensor(f"{name}_{n}", [P, 2, S], F32))
        sem = lambda n: ctx.enter_context(nc.semaphore(f"{name}_{n}"))
        self.nc = nc
        self.kt = sb("kt")
        self.ek, self.eu = sb("ek"), sb("eu")
        self.ekv, self.dl, self.dk = sb("ekv"), sb("dl"), sb("dk")
        self.nf, self.df = sb("nf"), sb("df")
        self.nb, self.db = sb("nb"), sb("db")
        self.min_done = sem("min_done")
        self.exp_done = sem("exp_done")
        self.ekv_done = sem("ekv_done")
        self.dl_done = sem("dl_done")
        self.dk_done = sem("dk_done")
        self.scan_done = sem("scan_done")
        self.sum_done = sem("sum_done")
        self.frac_done = sem("frac_done")

    def minima(self, dve, n, p, ucol):
        dve.wait_ge(self.scan_done, done(n - 2))
        dve.wait_ge(self.dl_done, done(n - 2))
        self.nc.vector.tensor_scalar(self.ek[:, p, :], self.kt[:, p, :], 30.0, None, ALU.min)
        self.nc.vector.tensor_scalar(self.eu[:, p, :], self.kt[:, p, :], ucol, 30.0, ALU.add, ALU.min).then_inc(self.min_done, 1)

    def exponentials(self, act, n, p):
        act.wait_ge(self.min_done, done(n))
        self.nc.scalar.activation(self.ek[:, p, :], self.ek[:, p, :], ACT.Exp)
        self.nc.scalar.activation(self.eu[:, p, :], self.eu[:, p, :], ACT.Exp).then_inc(self.exp_done, 1)

    def products(self, pool, n, p):
        pool.wait_ge(self.exp_done, done(n))
        pool.wait_ge(self.scan_done, done(n - 2))
        pool.wait_ge(self.frac_done, done(n - 2))
        self.nc.gpsimd.tensor_tensor(self.ekv[:, p, :], self.ek[:, p, :], self.kt[:, p, :], ALU.mult).then_inc(self.ekv_done, 1)
        self.nc.gpsimd.tensor_tensor(self.dl[:, p, :], self.eu[:, p, :], self.ek[:, p, :],
                                     ALU.subtract).then_inc(self.dl_done, 1)
        pool.wait_ge(self.dl_done, done(n))
        self.nc.gpsimd.tensor_tensor(self.dk[:, p, :], self.dl[:, p, :], self.kt[:, p, :], ALU.mult).then_inc(self.dk_done, 1)

    def scans(self, dve, n, p, decay, used):
        dve.wait_ge(used, done(n - 2))
        dve.wait_ge(self.ekv_done, done(n))
        dec = decay.broadcast_to([P, S])
        for f, b, src in ((self.nf, self.nb, self.ekv), (self.df, self.db, self.ek)):
            self.nc.vector.tensor_tensor_scan(f[:, p, :], dec, src[:, p, :], 0.0, ALU.mult, ALU.add)
            last = self.nc.vector.tensor_tensor_scan(b[:, p, ::-1], dec, src[:, p, ::-1], 0.0, ALU.mult, ALU.add)
        last.then_inc(self.scan_done, 1)

    def fraction(self, pool, n, p):
        tt = self.nc.gpsimd.tensor_tensor
        pool.wait_ge(self.scan_done, done(n))
        pool.wait_ge(self.dk_done, done(n))
        tt(self.nb[:, p, :], self.nf[:, p, :], self.nb[:, p, :], ALU.add)
        tt(self.db[:, p, :], self.df[:, p, :], self.db[:, p, :], ALU.add).then_inc(self.sum_done, 1)
        pool.wait_ge(self.sum_done, done(n))
        tt(self.nf[:, p, :], self.nb[:, p, :], self.dk[:, p, :], ALU.add)
        tt(self.df[:, p, :], self.db[:, p, :], self.dl[:, p, :], ALU.add).then_inc(self.frac_done, 1)

    def credit_dve(self, dve):
        dve.sem_inc(self.min_done, CREDIT)
        dve.sem_inc(self.scan_done, CREDIT)

    def credit_act(self, act):
        act.sem_inc(self.exp_done, CREDIT)

    def credit_pool(self, pool):
        for s in (self.ekv_done, self.dl_done, self.dk_done, self.sum_done, self.frac_done):
            pool.sem_inc(s, CREDIT)


def first_gate(nc, keep, dr, x, fs, cond, w1, u1, bq, bk, bv, bo, w2, u2):
    xT, ident, cols, bqs, par1, par2 = (keep[k] for k in ("xT", "ident", "cols", "bqs", "par1", "par2"))
    cTh, cTl, kT = keep["cTh"], keep["cTl"], keep["kT"]
    with ExitStack() as ctx:
        sb = lambda n, s, d=F32: ctx.enter_context(nc.sbuf_tensor(n, s, d))
        sem = lambda n: ctx.enter_context(nc.semaphore(n))
        kin = sb("kin", [P, TC, C])
        xin = sb("xin", [P, TC, C])
        rows = sb("rows", [V_N, P])
        te = sb("te", [P, B, TD])
        small = sb("small", [P, 64])
        cur = sb("cur1", [P, 2, 3])
        ex = sb("ex", [P, 2, S])
        rec = sb("rec1", [P, 2, S])
        cc_out = sb("c_out", [P, 2, S])
        psk = [ctx.enter_context(nc.psum_tensor(f"psk{i}", [P, S], F32)) for i in range(2)]
        psx = [ctx.enter_context(nc.psum_tensor(f"psx{i}", [P, S], F32)) for i in range(2)]
        psv = ctx.enter_context(nc.psum_tensor("psv", [P, V_N], F32))
        g = GateMath(nc, ctx, "g1")
        k_in, x_in, v_in, te_in = (sem(n) for n in ("k_in", "x_in", "v_in", "te_in"))
        c_out_sem = keep["cT_stored"]
        ident_zero, ident_done, v_T, cols_done = (sem(n) for n in ("ident_zero", "ident_done", "v_T", "cols_done"))
        k_T, x_T = sem("k_T"), sem("x_T")
        kt_done, x_done = sem("kt_done"), sem("x_done")
        t_chain, s_chain = sem("time_steps"), sem("decay_steps")
        cur_done, par_done = sem("cur_done1"), sem("par_done")
        max_done, den_done, rec_done, c_done, hi_done, lo_done = (sem(n) for n in ("max1_done", "den1_done", "rec1_done", "c_done", "c_hi", "c_lo"))
        block = ctx.enter_context(nc.Block())
        vec = [(V_BQ, bq, 16), (V_BK, bk, 16), (V_BV, bv, 16), (V_W1, w1, 4), (V_W2, w2, 4), (V_U1, u1, 4),
               (V_U2, u2, 4), (V_BO, bo, 4)]

        @block.sync
        def _(sp):
            for at, v, n in vec:
                sp.dma_start(rows[at:at + n, :], v.rearrange("(r p) -> r p", p=P)).then_inc(v_in, 16)
            sp.dma_start(te[:], cond.partition_broadcast(P)).then_inc(te_in, 16)
            with sp.Fori(0, B) as b:
                sp.wait_ge(k_T, KC * b + CREDIT)
                sp.dma_start(kin[:], fs[bass.ds(b, 1)].rearrange("o (t p) c -> p (o t) c", p=P)).then_inc(k_in, 16)
                sp.wait_ge(x_T, KC * b + CREDIT)
                sp.dma_start(xin[:], x[bass.ds(b, 1)].rearrange("o (t p) c -> p (o t) c", p=P)).then_inc(x_in, 16)
            with sp.Fori(0, B) as b:
                sp.wait_ge(lo_done, KC * b + (KC + CREDIT))
                for h, part in enumerate((cTh, cTl)):
                    dst = dr["cT"][bass.ds(b, 1), :, h * KC * S:(h + 1) * KC * S].rearrange("o p n -> p (o n)")
                    src = part[:, bass.ds(b, 1), :, :].rearrange("p o k s -> p (o k s)").bitcast(F32)
                    sp.dma_start(dst, src).then_inc(c_out_sem, 16)

        @block.gpsimd
        def _(pool):
            g.credit_pool(pool)
            nc.gpsimd.memset(ident[:], 0.0).then_inc(ident_zero, 1)
            pool.wait_ge(ident_zero, 1)
            nc.gpsimd.affine_select(out=ident[:], in_=ident[:], compare_op=ALU.not_equal, fill=1.0, base=0,
                                    pattern=[[-1, P]], channel_multiplier=1).then_inc(ident_done, 1)

            def step(tile):
                if t := tile(0):
                    g.products(pool, t[0], t[1])
                if t := tile(1):
                    g.fraction(pool, t[0], t[1])

            pipeline(pool, B * KC, KC, 1, step)

        @block.tensor
        def _(pe):
            pe.sem_inc(k_T, CREDIT)
            pe.sem_inc(x_T, CREDIT)
            pe.wait_ge(ident_done, 1)
            pe.wait_ge(v_in, 16 * len(vec))
            nc.tensor.transpose(psv[:], rows[:], ident[0:V_N, 0:V_N]).then_inc(v_T, 1)
            with pe.Fori(0, B) as b:
                for i in range(KC):
                    n = KC * b + i
                    if i == 0:
                        pe.wait_ge(k_in, 16 * b + 16)
                        pe.wait_ge(x_in, 16 * b + 16)
                    pe.wait_ge(kt_done, done(n - 2))
                    for t in range(TC):
                        last = nc.tensor.transpose(psk[i % 2][:, t * P:(t + 1) * P], kin[:, t, i * P:(i + 1) * P], ident[:])
                    last.then_inc(k_T, 1)
                    pe.wait_ge(x_done, done(n - 2))
                    for t in range(TC):
                        last = nc.tensor.transpose(psx[i % 2][:, t * P:(t + 1) * P], xin[:, t, i * P:(i + 1) * P], ident[:])
                    last.then_inc(x_T, 1)

        @block.scalar
        def _(act):
            g.credit_act(act)
            for s in (kt_done, x_done, hi_done):
                act.sem_inc(s, CREDIT)
            act.wait_ge(v_T, 1)
            nc.scalar.activation(cols[:], psv[:], ACT.Copy).then_inc(cols_done, 1)
            act.wait_ge(cols_done, 1)
            nc.scalar.activation(small[:, 0:8], cols[:, V_W1:V_W1 + 8], ACT.Exp).then_inc(s_chain, 1)
            act.wait_ge(s_chain, 1)
            nc.scalar.activation(small[:, 8:16], small[:, 0:8], ACT.Exp, scale=-1.0).then_inc(s_chain, 1)
            act.wait_ge(t_chain, 1)
            nc.scalar.activation(small[:, 20:24], small[:, 16:20], ACT.Exp, scale=-1.0).then_inc(s_chain, 1)

            def step(tile):
                if t := tile(0):
                    n, p = t[:2]
                    act.wait_ge(k_T, done(n))
                    act.wait_ge(g.dk_done, done(n - 2))
                    nc.scalar.activation(g.kt[:, p, :], psk[p][:], ACT.Copy)
                    nc.scalar.activation(chunk(kT, n), psk[p][:], ACT.Copy).then_inc(kt_done, 1)
                if t := tile(1):
                    n, p = t[:2]
                    g.exponentials(act, n, p)
                    act.wait_ge(x_T, done(n))
                    nc.scalar.activation(chunk(xT, n), psx[p][:], ACT.Copy)
                    act.wait_ge(den_done, done(n - 2))
                    nc.scalar.activation(ex[:, p, :], psx[p][:], ACT.Exp, scale=-1.0).then_inc(x_done, 1)
                if t := tile(3):
                    n, p = t[:2]
                    act.wait_ge(c_done, done(n))
                    nc.scalar.activation(chunk(cTh, n), cc_out[:, p, :], ACT.Copy).then_inc(hi_done, 1)

            pipeline(act, B * KC, KC, 3, step)

        @block.vector
        def _(dve):
            g.credit_dve(dve)
            for s in (cur_done, max_done, den_done, rec_done, c_done, lo_done):
                dve.sem_inc(s, CREDIT)
            dve.wait_ge(te_in, 16)
            nc.vector.tensor_reduce(small[:, 16:20], te[:], AX.X, ALU.add).then_inc(t_chain, 1)
            dve.wait_ge(s_chain, 3)
            nc.vector.tensor_scalar(small[:, 24:28], small[:, 20:24], 1.0, None, ALU.add).then_inc(t_chain, 1)
            dve.wait_ge(t_chain, 2)
            nc.vector.reciprocal(small[:, 28:32], small[:, 24:28]).then_inc(t_chain, 1)
            dve.wait_ge(t_chain, 3)
            nc.vector.tensor_scalar(small[:, 32:36], small[:, 28:32], 0.5, 0.5, ALU.mult, ALU.add)
            nc.vector.tensor_scalar(small[:, 36:40], small[:, 28:32], 0.2, 0.8, ALU.mult, ALU.add).then_inc(t_chain, 1)
            dve.wait_ge(t_chain, 4)
            for l, par in enumerate((par1, par2)):
                nc.vector.tensor_tensor(par[:, :, :, 0], small[:, 32:36].unsqueeze(2).broadcast_to([P, B, KC]),
                                        small[:, 8 + 4 * l:12 + 4 * l].unsqueeze(1).broadcast_to([P, B, KC]), ALU.mult)
                u_row = (V_U1, V_U2)[l]
                nc.vector.tensor_copy(par[:, :, :, 1], cols[:, u_row:u_row + KC].unsqueeze(1).broadcast_to([P, B, KC]))
                nc.vector.tensor_copy(par[:, :, :, 2], small[:, 36:40].unsqueeze(2).broadcast_to([P, B, KC]))
            nc.vector.tensor_scalar(bqs[:], cols[:, V_BQ:V_BQ + H], SCALE, None, ALU.mult).then_inc(par_done, 1)
            dve.wait_ge(par_done, 1)

            def step(tile):
                if t := tile(0):
                    n, p, _, i = t
                    dve.wait_ge(kt_done, done(n))
                    g.minima(dve, n, p, cols[:, V_U1 + i:V_U1 + i + 1])
                if t := tile(1):
                    n, p = t[:2]
                    dve.wait_ge(c_done, done(n - 2))
                    nc.vector.tensor_copy(cur[:, p, :], chunk(par1, n)).then_inc(cur_done, 1)
                    dve.wait_ge(cur_done, done(n))
                    g.scans(dve, n, p, cur[:, p, 0:1], c_done)
                if t := tile(3):
                    n, p = t[:2]
                    dve.wait_ge(hi_done, done(n))
                    nc.vector.tensor_tensor(chunk(cTl, n), cc_out[:, p, :], chunk(cTh, n).bitcast(F32),
                                            ALU.subtract).then_inc(lo_done, 1)
                if t := tile(2):
                    n, p = t[:2]
                    dve.wait_ge(g.frac_done, done(n))
                    nc.vector.tensor_scalar(g.db[:, p, :], g.df[:, p, :], 1e-8, None, ALU.max).then_inc(max_done, 1)
                    dve.wait_ge(max_done, done(n))
                    dve.wait_ge(x_done, done(n))
                    nc.vector.scalar_tensor_tensor(out=g.df[:, p, :], in0=ex[:, p, :], scalar=1.0,
                                                   in1=g.db[:, p, :], op0=ALU.add, op1=ALU.mult).then_inc(den_done, 1)
                    dve.wait_ge(den_done, done(n))
                    nc.vector.reciprocal(rec[:, p, :], g.df[:, p, :]).then_inc(rec_done, 1)
                    dve.wait_ge(rec_done, done(n))
                    dve.wait_ge(lo_done, done(n - 2))
                    nc.vector.scalar_tensor_tensor(out=cc_out[:, p, :], in0=g.nf[:, p, :], scalar=cur[:, p, 2:3],
                                                   in1=rec[:, p, :], op0=ALU.mult, op1=ALU.mult).then_inc(c_done, 1)

            pipeline(dve, B * KC, KC, 3, step)


def queries_and_second_gate(nc, keep, dr, wq):
    cTh, cTl, kT, par2, bqs, cols = (keep[k] for k in ("cTh", "cTl", "kT", "par2", "bqs", "cols"))
    with ExitStack() as ctx:
        sb = lambda n, s, d=F32: ctx.enter_context(nc.sbuf_tensor(n, s, d))
        sem = lambda n: ctx.enter_context(nc.semaphore(n))
        wraw = sb("wq_raw", [P, 2, KC, P])
        wh = sb("wq_high", [P, 2, KC, P], F32R)
        wl = sb("wq_low", [P, 2, KC, P], F32R)
        qo = sb("q_out", [P, 2, B, S])
        cur = sb("cur2", [P, 2, 3])
        bqc = sb("bq_cur", [P, 2])
        rec = sb("rec2", [P, 2, S])
        fo = sb("f_out", [P, 2, S])
        psq = [ctx.enter_context(nc.psum_tensor(f"psq{i}", [P, S], F32)) for i in range(B)]
        g = GateMath(nc, ctx, "g2")
        wq_in = [sem("wq_in0"), sem("wq_in1")]
        q_out = [sem("q_stored0"), sem("q_stored1")]
        f_out = [sem("f_stored0"), sem("f_stored1")]
        wh_done, wl_done = sem("wq_high_done"), sem("wq_low_done")
        q_done = sem("q_done")
        q_ev = sem("q_left_psum")
        kt_done, cur_done, max_done, rec_done, f_done = (
            sem(n) for n in ("kt2_done", "cur2_done", "max2_done", "rec2_done", "f_done"))
        block = ctx.enter_context(nc.Block())

        @block.sync
        def _(sp):
            def step(tile):
                if t := tile(0):
                    n, p = t[:2]
                    sp.wait_ge(wl_done, done(n - 2))
                    sp.dma_start(wraw[:, p, :, :], wq[:, bass.ds(P * n, P)].rearrange("(k p) m -> p k m", p=P)).then_inc(wq_in[p], 16)
                if t := tile(2):
                    n, p = t[:2]
                    sp.wait_ge(q_ev, B * n + 2 * B)
                    for b in range(B):
                        sp.dma_start(dr["q"][b, :, :, bass.ds(P * n, P)].rearrange("g p m -> p g m"),
                                     qo[:, p, b, :].rearrange("p (g m) -> p g m", g=NG)).then_inc(q_out[p], 16)
                    sp.wait_ge(f_done, done(n))
                    sp.dma_start(dr["f2"][bass.ds(n, 1)].rearrange("o p s -> p (o s)"), fo[:, p, :]).then_inc(f_out[p], 16)

            pipeline(sp, H, 2, 2, step)
            sp.wait_ge(keep["cT_stored"], 16 * 2 * B)
            for p in range(2):
                sp.wait_ge(q_out[p], 16 * B * H // 2)
                sp.wait_ge(f_out[p], 16 * H // 2)

        @block.gpsimd
        def _(pool):
            g.credit_pool(pool)

            def step(tile):
                if t := tile(0):
                    g.products(pool, t[0], t[1])
                if t := tile(1):
                    g.fraction(pool, t[0], t[1])

            pipeline(pool, B * KC, 2, 1, step)

        @block.tensor
        def _(pe):
            pe.sem_inc(q_done, B)

            def step(tile):
                n, p = tile(0)[:2]
                pe.wait_ge(wl_done, done(n))
                for b in range(B):
                    pe.wait_ge(q_ev, B * n + (b + 1))
                    i = 0
                    for a, m in ((wh, cTh), (wh, cTl), (wl, cTh)):
                        for k in range(KC):
                            last = nc.tensor.matmul(psq[b][:], a[:, p, k, :], m[:, b, k, :], start=i == 0, stop=i == 3 * KC - 1)
                            i += 1
                    last.then_inc(q_done, 1)

            pipeline(pe, H, 2, 0, step)

        @block.scalar
        def _(act):
            g.credit_act(act)
            act.sem_inc(wh_done, CREDIT)
            act.sem_inc(q_ev, B)

            def step(tile):
                if t := tile(0):
                    n, p, half = t[:3]
                    act.wait_ge(wq_in[p], 16 * half + 16)
                    act.wait_ge(q_done, B * n)
                    nc.scalar.activation(wh[:, p, :, :], wraw[:, p, :, :], ACT.Copy).then_inc(wh_done, 1)
                    g.exponentials(act, n, p)
                if t := tile(1):
                    n, p, half = t[:3]
                    act.wait_ge(q_out[p], 16 * B * half)
                    act.wait_ge(cur_done, done(n))
                    for b in range(B):
                        act.wait_ge(q_done, B * n + (B + b + 1))
                        nc.scalar.activation(qo[:, p, b, :], psq[b][:], ACT.Identity, bias=bqc[:, p:p + 1],
                                             scale=SCALE).then_inc(q_ev, 1)

            pipeline(act, H, 2, 1, step)

        @block.vector
        def _(dve):
            g.credit_dve(dve)
            for s in (kt_done, wl_done, cur_done, max_done, rec_done, f_done):
                dve.sem_inc(s, CREDIT)

            def step(tile):
                if t := tile(0):
                    n, p, _, i = t
                    dve.wait_ge(g.dk_done, done(n - 2))
                    nc.vector.tensor_scalar(g.kt[:, p, :], chunk(kT, n), 1.0, None, ALU.mult).then_inc(kt_done, 1)
                    dve.wait_ge(kt_done, done(n))
                    g.minima(dve, n, p, cols[:, V_U2 + i:V_U2 + i + 1])
                if t := tile(1):
                    n, p = t[:2]
                    dve.wait_ge(q_ev, B * n)
                    nc.vector.tensor_scalar(bqc[:, p:p + 1], bqs[:, bass.ds(n, 1)], 1.0, None, ALU.mult)
                    dve.wait_ge(f_done, done(n - 2))
                    nc.vector.tensor_copy(cur[:, p, :], chunk(par2, n)).then_inc(cur_done, 1)
                    dve.wait_ge(cur_done, done(n))
                    g.scans(dve, n, p, cur[:, p, 0:1], f_done)
                if t := tile(0):
                    n, p = t[:2]
                    dve.wait_ge(wh_done, done(n))
                    nc.vector.tensor_tensor(wl[:, p, :, :], wraw[:, p, :, :], wh[:, p, :, :].bitcast(F32),
                                            ALU.subtract).then_inc(wl_done, 1)
                if t := tile(2):
                    n, p, half = t[:3]
                    dve.wait_ge(g.frac_done, done(n))
                    nc.vector.tensor_scalar(g.db[:, p, :], g.df[:, p, :], 1e-8, None, ALU.max).then_inc(max_done, 1)
                    dve.wait_ge(max_done, done(n))
                    nc.vector.reciprocal(rec[:, p, :], g.db[:, p, :]).then_inc(rec_done, 1)
                    dve.wait_ge(rec_done, done(n))
                    dve.wait_ge(f_out[p], 16 * half)
                    nc.vector.scalar_tensor_tensor(out=fo[:, p, :], in0=g.nf[:, p, :], scalar=cur[:, p, 2:3],
                                                   in1=rec[:, p, :], op0=ALU.mult, op1=ALU.mult).then_inc(f_done, 1)

            pipeline(dve, H, 4, 2, step)


S_BANKS = ((0, 2), (3,), (1,))
P_AT = [0, 128, 384, 768]
P_N = 1280
T_BANKS = ((0,), (1, 3), (2,))
T_AT = {0: 0, 1: 512, 3: 896, 2: 1024}
PE_ORDER = ("K0 K1 S0 V0 K2 S1 V1 V2 S2 a0 V3 b0 K3 A0 a1 S3 b1 P0 A1 a2 Q0 b2 P1 A2 a3 Q1 b3 "
            "P2 A3 Q2 P3 Q3").split()
ACT_ORDER = "K0 K1 S0 V0 K2 S1 V1 V2 a0 S2 V3 b0 K3 A0 a1 b1 S3 A1 a2 b2 A2 a3 b3 A3".split()
DVE_ORDER = ("K0 K1 M0 N0 V0 K2 M1 N1 V1 V2 M2 a0 V3 b0 N2 K3 A0 a1 M3 b1 A1 a2 b2 N3 A2 a3 b3 A3 "
             "O0 O1 O2 O3").split()
TURNS = {"a": (0, 1), "b": (2,)}
PROJ = [e for e in PE_ORDER if e[0] in "KV"] + [f"O{i}" for i in range(KC)]
NPROJ = len(PROJ)
NPB = 3


def split_products(nc, out, highs_lows, start, stop):
    terms = [(a, b) for (ah, al), (bh, bl) in highs_lows for a, b in ((ah, bh), (ah, bl), (al, bh))]
    for i, (a, b) in enumerate(terms):
        last = nc.tensor.matmul(out, a, b, start=start and i == 0, stop=stop and i == len(terms) - 1)
    return last


def attention(nc, keep, dr, wk, wv, wo):
    xT, ident, cols = keep["xT"], keep["ident"], keep["cols"]
    with ExitStack() as ctx:
        sb = lambda n, s, d=F32: ctx.enter_context(nc.sbuf_tensor(n, s, d))
        sem = lambda n: ctx.enter_context(nc.semaphore(n))
        ps = lambda n: ctx.enter_context(nc.psum_tensor(n, [P, S], F32))
        wraw = sb("w_raw", [P, KC, HG * D])
        wsplit = {w: (sb(f"w{w}_high", [P, KC, HG * D], F32R), sb(f"w{w}_low", [P, KC, HG * D], F32R)) for w in "kvo"}
        cT = sb("cT", [P, 2, KC, S], F32R)
        qraw = sb("q_raw", [P, H, P])
        qh, ql = sb("q_high", [P, HG, S], F32R), sb("q_low", [P, HG, S], F32R)
        kh, kl = sb("k_high", [P, 2, S], F32R), sb("k_low", [P, 2, S], F32R)
        vh, vl = sb("v_high", [P, TC, HG * D], F32R), sb("v_low", [P, TC, HG * D], F32R)
        prob = sb("prob", [P, NPB, P_N])
        pth, ptl = sb("pT_high", [P, 2, P_N], F32R), sb("pT_low", [P, 2, P_N], F32R)
        oth, otl = sb("oT_high", [P, HG, S], F32R), sb("oT_low", [P, HG, S], F32R)
        nmax, rsum, rinv = sb("neg_max", [P, 2, TC]), sb("row_sum", [P, 2, TC]), sb("row_inv", [P, 2, TC])
        bias = sb("bias_kv", [P, 2 * HG])
        identb, maskb = sb("ident_b", [P, P], BF16), sb("mask_b", [P, P], BF16)
        zero = sb("zero_row", [P, C])
        pj = [ps("proj0"), ps("proj1")]
        pss = [ps(f"scores{i}") for i in range(3)]
        pst = [ps("weights_T0"), ps("weights_T1")]
        psa = ps("average_T")
        w_in, w_lo = sem("w_in"), sem("w_split")
        cT_in, q_in, q_hi, q_lo = sem("cT_in"), sem("q_in"), sem("q_high_done"), sem("q_split")
        w_hi = sem("w_high_done")
        mask0, mask_done, zero_done, filled = sem("mask_zero"), sem("mask_done"), sem("zero_done"), sem("slots_filled")
        proj_mm, proj_hi, proj_ev = sem("proj_mm"), sem("proj_high"), sem("proj_left")
        s_mm, s_max, s_exp, s_rec, s_norm = (sem(n) for n in ("scores_mm", "max_done", "exp_done", "rinv_done", "norm_done"))
        t_mm, t_hi, t_lo = sem("pT_mm"), sem("pT_high_done"), sem("pT_low_done")
        a_mm, a_hi, a_lo = sem("avg_mm"), sem("oT_high_done"), sem("oT_low_done")
        bias_done = sem("bias_done")
        pool_steps = keep["pool_steps"]
        block = ctx.enter_context(nc.Block())
        NIT = NG * B
        FILL = NBLK_ROOM * P // NIT
        FP = 104
        assert FILL * NIT == NBLK_ROOM * P and FILL % FP == 0

        def v_proj(it, e):
            return NPROJ * it + (PROJ.index(e) + 1 + NPROJ)

        def proj_bank(e):
            i = PROJ.index(e)
            return pss[i - (NPROJ - 2)] if i >= NPROJ - 2 else pj[i % 2]

        def prob_before(it, h):
            return (it, h - NPB) if h >= NPB else (it - 1, max(x for x in range(HG) if x % NPB == h % NPB))

        def v_head(it, h):
            return HG * it + (h + 1 + HG)

        def v_bank(it, h, x):
            return 3 * HG * it + (3 * h + x + 1 + 3 * HG)

        @block.sync
        def _(sp):
            sp.wait_ge(zero_done, 1)
            with sp.Fori(0, NG) as g:
                cs = bass.ds(HG * D * g, HG * D)

                def load_weights(i, src):
                    sp.wait_ge(w_lo, 3 * g + (i + 1))
                    sp.dma_start(wraw[:], src.rearrange("(k p) m -> p k m", p=P)).then_inc(w_in, 16)

                def load_batch(b, it):
                    sp.wait_ge(proj_mm, v_proj(it - 1, "K3"))
                    sp.dma_start(cT[:].rearrange("p a k s -> p (a k s)").bitcast(F32),
                                 dr["cT"][bass.ds(b, 1)].rearrange("o p n -> p (o n)")).then_inc(cT_in, 16)
                    sp.wait_ge(q_lo, it + 1)
                    sp.dma_start(qraw[:], dr["q"][bass.ds(b, 1), bass.ds(g, 1)]
                                 .rearrange("o u p (j t) -> p (o u j) t", j=H)).then_inc(q_in, 16)
                    sp.dma_start(dr["xs"][bass.ds(FILL * it, FILL), :].rearrange("(p r) c -> p r c", p=FP),
                                 zero[0:FP, :].unsqueeze(1).broadcast_to([FP, FILL // FP, C])).then_inc(filled, 16)

                load_weights(0, wk[:, cs])
                load_batch(0, B * g)
                load_weights(1, wv[:, cs])
                load_weights(2, wo[cs, :])
                with sp.Fori(1, B) as b:
                    load_batch(b, B * g + b)
            sp.wait_ge(filled, 16 * NIT)

        @block.gpsimd
        def _(pool):
            nc.gpsimd.memset(zero[:], 0.0).then_inc(zero_done, 1)
            nc.gpsimd.memset(identb[:], 0.0).then_inc(mask0, 1)
            nc.gpsimd.memset(maskb[:], 0.0).then_inc(mask0, 1)
            pool.wait_ge(mask0, 2)
            nc.gpsimd.affine_select(out=identb[:], in_=identb[:], compare_op=ALU.not_equal, fill=1.0, base=0,
                                    pattern=[[-1, P]], channel_multiplier=1).then_inc(mask_done, 1)
            nc.gpsimd.affine_select(out=maskb[:], in_=maskb[:], compare_op=ALU.is_ge, fill=NEG, base=0,
                                    pattern=[[-1, P]], channel_multiplier=1).then_inc(mask_done, 1)
            pool.sem_inc(w_lo, 1)
            pool.sem_inc(q_lo, 1)

            def split_weights(g, i, w):
                pool.wait_ge(w_in, 48 * g + 16 * (i + 1))
                pool.wait_ge(proj_mm, proj_used(g, w))
                pool.sem_inc(pool_steps, 1)
                nc.gpsimd.tensor_scalar(wsplit[w][0][:], wraw[:], 1.0, 1.0, ALU.mult, ALU.mult).then_inc(w_hi, 1)
                pool.wait_ge(w_hi, 3 * g + (i + 1))
                nc.gpsimd.tensor_tensor(wsplit[w][1][:], wraw[:], wsplit[w][0][:].bitcast(F32), ALU.subtract).then_inc(w_lo, 1)

            def proj_used(g, w):
                last = {"k": "K3", "v": "V3", "o": "O3"}[w]
                return v_proj(B * g - 1, last)

            def split_queries(it):
                pool.wait_ge(q_in, 16 * it + 16)
                pool.wait_ge(s_mm, v_bank(it - 1, HG - 1, 2))
                src = qraw[:].rearrange("p j t -> p t j")
                dst = lambda t: t[:].rearrange("p h (t j) -> p (h t) j", j=H)
                pool.sem_inc(pool_steps, 1)
                nc.gpsimd.tensor_scalar(dst(qh), src, 1.0, 1.0, ALU.mult, ALU.mult).then_inc(q_hi, 1)
                pool.wait_ge(q_hi, it + 1)
                nc.gpsimd.tensor_tensor(dst(ql), src, dst(qh).bitcast(F32), ALU.subtract).then_inc(q_lo, 1)

            with pool.Fori(0, NG) as g:
                split_weights(g, 0, "k")
                split_queries(B * g)
                split_weights(g, 1, "v")
                split_weights(g, 2, "o")
                with pool.Fori(1, B) as b:
                    split_queries(B * g + b)

        @block.tensor
        def _(pe):
            pe.sem_inc(proj_mm, NPROJ)
            pe.sem_inc(s_mm, 3 * HG)
            pe.sem_inc(t_mm, 3 * HG)
            pe.sem_inc(a_mm, HG)
            pe.wait_ge(mask_done, 2)
            with pe.Fori(0, NG) as g, pe.Fori(0, B) as b:
                it = B * g + b
                for e in PE_ORDER:
                    kind, h = e[0], int(e[1])
                    if kind in "KV":
                        out = proj_bank(e)
                        pe.wait_ge(proj_ev, v_proj(it, e) - (4 if PROJ.index(e) < 2 else 2))
                    if e == "K0":
                        pe.wait_ge(cT_in, 16 * it + 16)
                        pe.wait_ge(w_lo, 3 * g + 2)
                    if e == "V0":
                        pe.wait_ge(w_lo, 3 * g + 3)
                    if e == "P0":
                        pe.wait_ge(w_lo, 3 * g + 4)
                    if kind == "K":
                        ws = slice(h * D, (h + 1) * D)
                        split_products(nc, out[:], [((wsplit["k"][0][:, k, ws], wsplit["k"][1][:, k, ws]),
                                                     (cT[:, 0, k, :], cT[:, 1, k, :])) for k in range(KC)],
                                       True, True).then_inc(proj_mm, 1)
                    elif kind == "V":
                        ts = slice(h * P, (h + 1) * P)
                        split_products(nc, out[:], [((cT[:, 0, k, ts], cT[:, 1, k, ts]),
                                                     (wsplit["v"][0][:, k, :], wsplit["v"][1][:, k, :])) for k in range(KC)],
                                       True, True).then_inc(proj_mm, 1)
                    elif kind in "PQ":
                        pe.wait_ge(a_lo, v_head(it, h))
                        for t in ((0, 1) if kind == "P" else (2, 3)):
                            out, cs = proj_bank(f"O{t}"), slice(t * P, (t + 1) * P)
                            if h == 0 and kind == "P":
                                pe.wait_ge(proj_ev, v_proj(it, f"O{t}") - 2)
                            elif h == 0:
                                pe.wait_ge(s_exp, v_bank(it, HG - 1, t - 2))
                            last = split_products(nc, out[:], [((wsplit["o"][0][:, h, cs], wsplit["o"][1][:, h, cs]),
                                                                (oth[:, h, :], otl[:, h, :]))], h == 0, h == HG - 1)
                            if h == HG - 1:
                                last.then_inc(proj_mm, 1)
                    elif kind == "S":
                        if h == 0:
                            pe.wait_ge(q_lo, it + 2)
                        pe.wait_ge(proj_ev, v_proj(it, f"K{h}"))
                        for x, tiles in enumerate(S_BANKS):
                            pe.wait_ge(s_exp, v_bank(it, h - 1, x))
                            at = 0
                            for i in tiles:
                                n, ts = (i + 1) * P, slice(i * P, (i + 1) * P)
                                acc, kk = pss[x][:, at:at + n], slice(0, n)
                                nc.tensor.matmul(acc, qh[:, h, ts], kh[:, h % 2, kk], start=True, stop=False)
                                nc.tensor.matmul(acc[:, n - P:n], identb[:], maskb[:], start=False, stop=False)
                                nc.tensor.matmul(acc, qh[:, h, ts], kl[:, h % 2, kk], start=False, stop=False)
                                last = nc.tensor.matmul(acc, ql[:, h, ts], kh[:, h % 2, kk], start=False, stop=True)
                                at += n
                            last.then_inc(s_mm, 1)
                    elif kind in TURNS:
                        pe.wait_ge(s_norm, v_head(it, h))
                        for x in TURNS[kind]:
                            tiles, turn = T_BANKS[x], 3 * h + x
                            pe.wait_ge(t_lo, v_bank(it, h, x - 2))
                            at = 0
                            for j in tiles:
                                for i in range(j, TC):
                                    last = nc.tensor.transpose(pst[turn % 2][:, at:at + P],
                                                               prob[:, h % NPB, P_AT[i] + j * P:P_AT[i] + (j + 1) * P], ident[:])
                                    at += P
                            last.then_inc(t_mm, 1)
                    elif kind == "A":
                        if h == 0:
                            pe.wait_ge(proj_ev, v_proj(it, "V3"))
                        pe.wait_ge(t_lo, v_bank(it, h, 2))
                        pe.wait_ge(a_lo, v_head(it, h - 1))
                        for j in range(TC):
                            n, ds = (TC - j) * P, slice(h * D, (h + 1) * D)
                            pt = slice(T_AT[j], T_AT[j] + n)
                            last = split_products(nc, psa[:, j * P:], [((vh[:, j, ds], vl[:, j, ds]),
                                                                        (pth[:, h % 2, pt], ptl[:, h % 2, pt]))],
                                                  j == 0, j == TC - 1)
                        last.then_inc(a_mm, 1)

        @block.scalar
        def _(act):
            act.sem_inc(s_exp, 3 * HG)
            act.sem_inc(t_hi, 3 * HG)
            act.sem_inc(a_hi, HG)
            with act.Fori(0, NG) as g, act.Fori(0, B) as b:
                it = B * g + b
                for e in ACT_ORDER:
                    kind, h = e[0], int(e[1])
                    if kind == "K":
                        if h == 0:
                            act.wait_ge(bias_done, it + 1)
                        act.wait_ge(s_mm, v_bank(it, h - 2, 2))
                        act.wait_ge(proj_mm, v_proj(it, e))
                        nc.scalar.activation(kh[:, h % 2, :], proj_bank(e)[:], ACT.Identity,
                                             bias=bias[:, h:h + 1]).then_inc(proj_hi, 1)
                    elif kind == "V":
                        if h == 0:
                            act.wait_ge(a_mm, v_head(it - 1, HG - 1))
                        act.wait_ge(proj_mm, v_proj(it, e))
                        nc.scalar.activation(vh[:, h, :], proj_bank(e)[:], ACT.Copy).then_inc(proj_hi, 1)
                    elif kind == "S":
                        act.wait_ge(t_mm, v_bank(*prob_before(it, h), 2))
                        act.wait_ge(s_norm, v_head(it, h - 2))
                        for x, tiles in enumerate(S_BANKS):
                            act.wait_ge(s_max, v_bank(it, h, x))
                            at = 0
                            for i in tiles:
                                n = (i + 1) * P
                                last = nc.scalar.activation(prob[:, h % NPB, P_AT[i]:P_AT[i] + n], pss[x][:, at:at + n], ACT.Exp,
                                                            bias=nmax[:, h % 2, i:i + 1], accum_out=rsum[:, h % 2, i:i + 1])
                                at += n
                            last.then_inc(s_exp, 1)
                    elif kind in TURNS:
                        act.wait_ge(a_mm, v_head(it, h - 2))
                        for x in TURNS[kind]:
                            tiles = T_BANKS[x]
                            at, n = T_AT[tiles[0]], sum((TC - j) * P for j in tiles)
                            act.wait_ge(t_mm, v_bank(it, h, x))
                            nc.scalar.activation(pth[:, h % 2, at:at + n], pst[(3 * h + x) % 2][:, 0:n], ACT.Copy).then_inc(t_hi, 1)
                    elif kind == "A":
                        if h == 0:
                            act.wait_ge(proj_mm, v_proj(it - 1, "O3"))
                        act.wait_ge(a_mm, v_head(it, h))
                        nc.scalar.activation(oth[:, h, :], psa[:], ACT.Identity, bias=bias[:, HG + h:HG + h + 1]).then_inc(a_hi, 1)

        @block.vector
        def _(dve):
            dve.sem_inc(proj_ev, NPROJ)
            dve.sem_inc(s_max, 3 * HG)
            dve.sem_inc(s_norm, HG)
            dve.sem_inc(t_lo, 3 * HG)
            dve.sem_inc(a_lo, HG)
            with dve.Fori(0, NG) as g, dve.Fori(0, B) as b:
                it = B * g + b
                dve.wait_ge(a_lo, v_head(it - 1, HG - 1))
                nc.vector.tensor_scalar(bias[:, 0:HG], cols[:, bass.ds(HG * g + V_BK, HG)], 1.0, None, ALU.mult)
                nc.vector.tensor_scalar(bias[:, HG:], cols[:, bass.ds(HG * g + V_BV, HG)], 1.0, None, ALU.mult).then_inc(bias_done, 1)
                dve.wait_ge(bias_done, it + 1)
                for e in DVE_ORDER:
                    kind, h = e[0], int(e[1])
                    if kind in "KVO":
                        bank = proj_bank(e)
                    if kind in "KV":
                        kv = [x for x in PROJ if x[0] != "O"]
                        dve.wait_ge(proj_hi, len(kv) * it + (kv.index(e) + 1))
                    if kind == "K":
                        nc.vector.scalar_tensor_tensor(out=kl[:, h % 2, :], in0=bank[:], scalar=bias[:, h:h + 1],
                                                       in1=kh[:, h % 2, :].bitcast(F32), op0=ALU.add,
                                                       op1=ALU.subtract).then_inc(proj_ev, 1)
                    elif kind == "V":
                        nc.vector.tensor_tensor(vl[:, h, :], bank[:], vh[:, h, :].bitcast(F32), ALU.subtract).then_inc(proj_ev, 1)
                    elif kind == "O":
                        dve.wait_ge(proj_mm, v_proj(it, e))
                        acc = xT[:, bass.ds(b, 1), h, :].rearrange("p o s -> p (o s)")
                        nc.vector.tensor_tensor(acc, bank[:], acc, ALU.add).then_inc(proj_ev, 1)
                    elif kind == "M":
                        dve.wait_ge(s_exp, v_bank(it, h - 2, 2))
                        for x, tiles in enumerate(S_BANKS):
                            dve.wait_ge(s_mm, v_bank(it, h, x))
                            at = 0
                            for i in tiles:
                                last = nc.vector.tensor_reduce(nmax[:, h % 2, i:i + 1], pss[x][:, at:at + (i + 1) * P], AX.X,
                                                               ALU.max, negate=True)
                                at += (i + 1) * P
                            last.then_inc(s_max, 1)
                    elif kind == "N":
                        dve.wait_ge(s_norm, v_head(it, h - 2))
                        dve.wait_ge(s_exp, v_bank(it, h, 2))
                        nc.vector.reciprocal(rinv[:, h % 2, :], rsum[:, h % 2, :]).then_inc(s_rec, 1)
                        dve.wait_ge(s_rec, HG * it + (h + 1))
                        for i in range(TC):
                            w = prob[:, h % NPB, P_AT[i]:P_AT[i] + (i + 1) * P]
                            last = nc.vector.tensor_scalar(w, w, rinv[:, h % 2, i:i + 1], None, ALU.mult)
                        last.then_inc(s_norm, 1)
                    elif kind in TURNS:
                        for x in TURNS[kind]:
                            tiles = T_BANKS[x]
                            at, n = T_AT[tiles[0]], sum((TC - j) * P for j in tiles)
                            dve.wait_ge(t_hi, v_bank(it, h, x))
                            nc.vector.tensor_tensor(ptl[:, h % 2, at:at + n], pst[(3 * h + x) % 2][:, 0:n],
                                                    pth[:, h % 2, at:at + n].bitcast(F32), ALU.subtract).then_inc(t_lo, 1)
                    elif kind == "A":
                        dve.wait_ge(a_hi, v_head(it, h))
                        nc.vector.scalar_tensor_tensor(out=otl[:, h, :], in0=psa[:], scalar=bias[:, HG + h:HG + h + 1],
                                                       in1=oth[:, h, :].bitcast(F32), op0=ALU.add,
                                                       op1=ALU.subtract).then_inc(a_lo, 1)


POOL_ITEMS = 2


def route_and_shared_up(nc, keep, dr, gate_w, sw_gate, sw_up):
    xT, ident, cols, hsh, wts, slot, tab, blocks = (
        keep[k] for k in ("xT", "ident", "cols", "hsh", "wts", "slot", "tab", "blocks"))
    with ExitStack() as ctx:
        sb = lambda n, s, d=F32: ctx.enter_context(nc.sbuf_tensor(n, s, d))
        sem = lambda n: ctx.enter_context(nc.semaphore(n))
        ps = lambda n, s=(P, S): ctx.enter_context(nc.psum_tensor(n, list(s), F32))
        x2h, x2l = sb("x2_high", [P, B, KC, S], F32R), sb("x2_low", [P, B, KC, S], F32R)
        gw = sb("gate_raw", [P, KC, E])
        gwh, gwl = sb("gate_high", [P, KC, E], F32R), sb("gate_low", [P, KC, E], F32R)
        wraw = sb("sw_raw", [P, 2, 2, KC, P])
        wh, wl = sb("sw_high", [P, 2, 2, KC, P], F32R), sb("sw_low", [P, 2, 2, KC, P], F32R)
        sc = sb("scores", [P, NT, E])
        identb, onesb, before = sb("identb4", [P, P], BF16), sb("onesb", [P, P], BF16), sb("before", [P, P], BF16)
        iota_e, iota_g, iota_q, iota_p = sb("iota_e", [P, E]), sb("iota_g", [P, NGRP]), sb("iota_q", [P, NT]), sb("iota_p", [P, 1])
        sg, us = sb("silu_g", [P, 2, S]), sb("up_out", [P, 2, S])
        with ExitStack() as first:
            sf = lambda n, s, d=F32: first.enter_context(nc.sbuf_tensor(n, s, d))
            f2 = sf("f2", [P, KC, S])
            x2 = sf("x2", [P, 2, KC, S])
        tok = sg
        lt = us[0:E, 0, :]
        with ExitStack() as second:
            sf = lambda n, s, d=F32: second.enter_context(nc.sbuf_tensor(n, s, d))
            gm = sf("group_max", [P, NT, 8])
            gv, gi = sf("group_top", [P, NT, 8]), sf("group_at", [P, NT, 8], U32)
            gif = sf("group_at_f", [P, NT, GSEL])
            gk, gk1 = sf("group_kept", [P, 2, NT, NGRP]), sf("group_off", [P, NT, NGRP])
            wv, ei = sf("expert_top", [P, NT, 8]), sf("expert_at", [P, NT, 8], U32)
            eif, wsum, winv = sf("expert_at_f", [P, NT, 8]), sf("weight_sum", [P, NT]), sf("weight_inv", [P, NT])
            oh = sf("one_hot", [P, TOPK, NT * E])
            chosen = sf("chosen", [P, NT * E], BF16)
            more, nb, incl, base = sf("more", [P, E, NT]), sf("n_blocks", [P, E]), sf("blocks_to", [P, E]), sf("base", [P, E])
            pos, slotf = sf("position", [P, NT, E]), sf("slot_f", [P, TOPK, NT])
            eb, ebb, ebi = sf("block_expert", [P, 2]), sf("block_expert_b", [P, 1], BF16), sf("block_expert_i", [1, 2, P], I32)
            ones_e = sf("ones_e", [P, E])
        with ExitStack() as third:
            sf = lambda n, s, d=F32: third.enter_context(nc.sbuf_tensor(n, s, d))
            stage, sidx = sf("row_stage", [P, 2, C]), sf("slot_stage", [P, 2, 8], I32)
        psl, pslg, psr = ps("logits_ps", (E, S)), ps("scores_ps", (P, TC * E)), ps("route_ps")
        pst = ps("tok_ps")
        psg, psu = [ps("gate_ps0"), ps("gate_ps1")], [ps("up_ps0"), ps("up_ps1")]
        gw_in, gw_hi, gw_lo, consts, masks = sem("gate_in"), sem("gate_hi"), sem("gate_lo"), sem("iotas"), sem("masks")
        f2_in, tok_st = sem("f2_in"), [sem("tok_stored0"), sem("tok_stored1")]
        sg_done, x2_done, x2_hi, x2_lo = (sem(n) for n in ("sig_done", "x2_done", "x2_hi", "x2_lo"))
        l_mm, l_ev, l_T, sc_done = sem("logits_mm"), sem("logits_left"), sem("logits_T_done"), sem("scores_done")
        tok_T, tok_ev = sem("tok_T"), sem("tok_left")
        act_steps = keep["act_steps"]
        w_in, w_hi, w_lo = [sem("sw_in0"), sem("sw_in1")], sem("sw_hi"), sem("sw_lo")
        u_mm, s_done, h_pool, h_dve = sem("up_mm"), sem("silu_done"), sem("hidden_pool"), sem("hidden_dve")
        pool_steps, pe_steps = keep["pool_steps"], sem("pe_steps4")
        r, chosen_done, pos_mm, row_done, row_mm, slot_done = (
            sem(n) for n in ("route_steps", "chosen_done", "pos_mm", "row_done", "row_mm", "slot_done"))
        st_in, sidx_done, sent = [sem("stage_in0"), sem("stage_in1")], sem("slot_stage_done"), [sem("sent0"), sem("sent1")]
        block = ctx.enter_context(nc.Block())

        def wait_hidden(eng, m, i, p):
            if m < POOL_ITEMS:
                eng.wait_ge(h_pool, B * m + 2 * i + (p + 1))
            else:
                eng.wait_ge(h_pool, B * POOL_ITEMS + 2)
                eng.wait_ge(h_dve, B * (m - POOL_ITEMS) + 2 * i + (p + 1))

        @block.sync
        def _(sp):
            for q in range(2):
                sp.sem_inc(tok_st[q], 16)
            sp.dma_start(gw[:], gate_w.rearrange("(k p) e -> p k e", p=P)).then_inc(gw_in, 16)
            def load_shared(m):
                at, n = SCH[m]
                if m >= 2:
                    sp.wait_ge(w_lo, m - 1)
                for i, w in enumerate((sw_gate, sw_up)):
                    sp.dma_start(wraw[:, m % 2, i, :, 0:n], w[:, at:at + n].rearrange("(k p) m -> p k m", p=P)).then_inc(w_in[m % 2], 16)

            load_shared(0)
            load_shared(1)

            def step(tile):
                if t := tile(0):
                    b = t[0]
                    sp.wait_ge(x2_done, done(b - 1))
                    sp.dma_start(f2[:], dr["f2"][bass.ds(KC * b, KC)].rearrange("k p s -> p k s")).then_inc(f2_in, 16)
                if t := tile(1):
                    b = t[0]
                    for i in range(TC):
                        sp.wait_ge(tok_ev, TC * b + (i + 2))
                        sp.dma_start(dr["x2"][bass.ds(S * b + P * i, P), :], tok[:, i % 2, :]).then_inc(tok_st[i % 2], 16)

            pipeline(sp, B, 2, 1, step)
            for m in range(2, len(SCH)):
                load_shared(m)
            for q in range(2):
                sp.wait_ge(tok_st[q], 16 * NT // 2 + 16)
            sp.wait_ge(slot_done, 1)

            def stage_rows(i, first):
                for p in range(2):
                    if not first:
                        sp.wait_ge(sent[p], 16 * TOPK * i)
                    sp.dma_start(stage[:, p, :], dr["x2"][bass.ds(2 * P * i + p * P, P), :]).then_inc(st_in[p], 16)

            stage_rows(0, True)
            with sp.Fori(1, NT // 2) as i:
                stage_rows(i, False)
            for p in range(2):
                sp.wait_ge(sent[p], 16 * TOPK * NT // 2)

        @block.gpsimd
        def _(pool):
            nc.gpsimd.memset(identb[:], 0.0).then_inc(masks, 1)
            nc.gpsimd.memset(onesb[:], 1.0).then_inc(masks, 1)
            pool.wait_ge(masks, 2)
            nc.gpsimd.affine_select(out=identb[:], in_=identb[:], compare_op=ALU.not_equal, fill=1.0, base=0,
                                    pattern=[[-1, P]], channel_multiplier=1).then_inc(consts, 1)
            nc.gpsimd.affine_select(out=before[:], in_=onesb[:], compare_op=ALU.is_ge, fill=0.0, base=-1,
                                    pattern=[[1, P]], channel_multiplier=-1).then_inc(consts, 1)
            for tile, pattern, cm in ((iota_e, [[1, E]], 0), (iota_g, [[1, NGRP]], 0), (iota_q, [[P, NT]], 0), (iota_p, [[0, 1]], 1)):
                nc.gpsimd.iota(tile[:], pattern=pattern, base=0, channel_multiplier=cm,
                               allow_small_or_imprecise_dtypes=True).then_inc(consts, 1)
            pool.sem_inc(h_pool, 2)
            for m in range(POOL_ITEMS):
                with pool.Fori(0, B // 2) as i:
                    for p in range(2):
                        pool.wait_ge(s_done, B * m + 2 * i + (p + 1))
                        pool.sem_inc(pool_steps, 1)
                        nc.gpsimd.tensor_tensor(hsh[:, m, bass.ds(2 * S * i + p * S, S)], sg[:, p, :], us[:, p, :],
                                                ALU.mult).then_inc(h_pool, 1)
            pool.wait_ge(slot_done, 1)

            def send_rows(i, first):
                for p in range(2):
                    if not first:
                        pool.wait_ge(sent[p], 16 * TOPK * i)
                    pool.sem_inc(pool_steps, 1)
                    nc.gpsimd.tensor_copy(sidx[:, p, :], slot[:, bass.ds(2 * i + p, 1), :].rearrange("p o k -> p (o k)")).then_inc(sidx_done, 1)
                    pool.wait_ge(sidx_done, 2 * i + (p + 1))
                    pool.wait_ge(st_in[p], 16 * i + 16)
                    pool.sem_inc(pool_steps, 1)
                    for k in range(TOPK):
                        pool.indirect_dma_start(dr["xs"], bass.IndirectOffsetOnAxis(ap=sidx[:, p, k:k + 1], axis=0),
                                                stage[:, p, :], None).then_inc(sent[p], 16)

            send_rows(0, True)
            with pool.Fori(1, NT // 2) as i:
                send_rows(i, False)

        @block.tensor
        def _(pe):
            pe.sem_inc(tok_T, 2 * TC)
            pe.sem_inc(l_T, 1)
            pe.wait_ge(gw_lo, 1)

            def step(tile):
                if t := tile(1):
                    b = t[0]
                    pe.wait_ge(l_ev, b + 2)
                    pe.wait_ge(sc_done, b + 1)
                    pe.sem_inc(pe_steps, 1)
                    for i in range(TC):
                        last = nc.tensor.transpose(pslg[:, i * E:(i + 1) * E], lt[:, i * P:(i + 1) * P], ident[0:E, 0:E])
                    last.then_inc(l_T, 1)
                if t := tile(0):
                    b, q = t[:2]
                    pe.wait_ge(x2_lo, done(b))
                    pe.wait_ge(l_ev, b + 1)
                    both = lambda k: [v[:, bass.ds(b, 1), k, :].rearrange("p o s -> p (o s)") for v in (x2h, x2l)]
                    split_products(nc, psl[:], [((gwh[:, k, :], gwl[:, k, :]), both(k)) for k in range(KC)],
                                   True, True).then_inc(l_mm, 1)
                    for i in range(TC):
                        pe.wait_ge(tok_ev, TC * b + (i + 1))
                        for k in range(KC):
                            last = nc.tensor.transpose(pst[:, k * P:(k + 1) * P], x2[:, q, k, i * P:(i + 1) * P], ident[:])
                        last.then_inc(tok_T, 1)

            pipeline(pe, B, 2, 1, step)

            for m, (at, n) in enumerate(SCH):
                pe.wait_ge(w_lo, m + 1)
                with pe.Fori(0, B // 2) as i:
                    for p in range(2):
                        b = 2 * i + p
                        both = lambda k: [t[:, bass.ds(b, 1), k, :].rearrange("p o s -> p (o s)") for t in (x2h, x2l)]
                        wait_hidden(pe, m, i, p)
                        for j, bank in enumerate((psg[p], psu[p])):
                            last = split_products(nc, bank[0:n, :], [((wh[:, m % 2, j, k, 0:n], wl[:, m % 2, j, k, 0:n]), both(k))
                                                                     for k in range(KC)], True, True)
                        last.then_inc(u_mm, 1)
                if m == 1:
                    pe.wait_ge(chosen_done, 1)
                    pe.wait_ge(sc_done, B + 1)
                    nc.tensor.matmul(psr[:], before[:], chosen[:], start=True, stop=False)
                    for j in range(NT - 1):
                        rest = NT - 1 - j
                        rhs = chosen[:, j * E:(j + 1) * E].unsqueeze(1).broadcast_to([P, rest, E])
                        nc.tensor.matmul(psr[:, (j + 1) * E:], onesb[:], rhs, start=False, stop=j == NT - 2)
                    for j in range(NT):
                        last = nc.tensor.matmul(pslg[:, 0:E], onesb[:], chosen[:, j * E:(j + 1) * E], start=j == 0, stop=j == NT - 1)
                    last.then_inc(pos_mm, 1)
                if m == 3:
                    pe.wait_ge(row_done, 1)
                    nc.tensor.matmul(psl[0:1, 0:P], ebb[:], identb[:], start=True, stop=True).then_inc(row_mm, 1)

        @block.scalar
        def _(act):
            act.wait_ge(gw_in, 16)
            nc.scalar.activation(gwh[:], gw[:], ACT.Copy).then_inc(gw_hi, 1)
            act.sem_inc(l_ev, 1)
            act.sem_inc(sc_done, 1)

            def split_high(m):
                n = SCH[m][1]
                act.wait_ge(w_in[m % 2], 32 * (m // 2 + 1))
                if m >= 2:
                    act.wait_ge(u_mm, B * (m - 1))
                nc.scalar.activation(wh[:, m % 2, :, :, 0:n], wraw[:, m % 2, :, :, 0:n], ACT.Copy).then_inc(w_hi, 1)

            split_high(0)

            def step(tile):
                if t := tile(0):
                    b, q = t[:2]
                    act.wait_ge(tok_T, TC * b + TC)
                    act.wait_ge(x2_lo, done(b - 2))
                    act.sem_inc(act_steps, 1)
                    for k in range(KC):
                        last = nc.scalar.activation(x2[:, q, k, :], xT[:, bass.ds(b, 1), k, :].rearrange("p o s -> p (o s)"),
                                                    ACT.Sigmoid, bias=cols[:, V_BO + k:V_BO + k + 1])
                    last.then_inc(sg_done, 1)
                if t := tile(1):
                    b = t[0]
                    act.wait_ge(l_mm, b + 1)
                    act.wait_ge(l_T, b + 1)
                    nc.scalar.activation(lt, psl[:], ACT.Copy).then_inc(l_ev, 1)
                if t := tile(0):
                    b, q = t[:2]
                    act.wait_ge(x2_done, done(b))
                    act.sem_inc(act_steps, 1)
                    nc.scalar.activation(x2h[:, bass.ds(b, 1), :, :].rearrange("p o k s -> p (o k s)"),
                                         x2[:, q, :, :].rearrange("p k s -> p (k s)"), ACT.Copy).then_inc(x2_hi, 1)
                if t := tile(1):
                    b = t[0]
                    act.wait_ge(l_T, b + 2)
                    act.sem_inc(act_steps, 1)
                    nc.scalar.activation(sc[:, bass.ds(TC * b, TC), :].rearrange("p t e -> p (t e)"), pslg[:], ACT.Sigmoid).then_inc(sc_done, 1)

            pipeline(act, B, 2, 1, step)
            for q in range(2):
                act.wait_ge(tok_st[q], 16 * NT // 2 + 16)
            for m, (at, n) in enumerate(SCH):
                if m + 1 < len(SCH):
                    split_high(m + 1)
                with act.Fori(0, B // 2) as i:
                    for p in range(2):
                        wait_hidden(act, m, i, p)
                        act.wait_ge(u_mm, B * m + 2 * i + (p + 1))
                        last = nc.scalar.activation(sg[0:n, p, :], psg[p][0:n, :], ACT.Silu)
                        if m < POOL_ITEMS:
                            last = nc.scalar.activation(us[0:n, p, :], psu[p][0:n, :], ACT.Copy)
                        last.then_inc(s_done, 1)

        @block.vector
        def _(dve):
            steps = [0]

            def then(ins):
                steps[0] += 1
                ins.then_inc(r, 1)
                dve.wait_ge(r, steps[0])

            tt, ts, red = nc.vector.tensor_tensor, nc.vector.tensor_scalar, nc.vector.tensor_reduce
            dve.sem_inc(x2_done, CREDIT)
            dve.sem_inc(x2_lo, CREDIT)
            dve.sem_inc(tok_ev, 1)
            dve.sem_inc(h_dve, 2)
            dve.wait_ge(gw_hi, 1)
            tt(gwl[:], gw[:], gwh[:].bitcast(F32), ALU.subtract).then_inc(gw_lo, 1)

            def split_low(m):
                n = SCH[m][1]
                dve.wait_ge(w_hi, m + 1)
                for j in range(2):
                    last = tt(wl[:, m % 2, j, :, 0:n], wraw[:, m % 2, j, :, 0:n], wh[:, m % 2, j, :, 0:n].bitcast(F32), ALU.subtract)
                last.then_inc(w_lo, 1)

            split_low(0)

            def rows_out(b, half):
                for i in range(2 * half, 2 * half + 2):
                    dve.wait_ge(tok_st[i % 2], 32 * b + (16 * half + 16))
                    dve.wait_ge(tok_T, TC * b + (2 * TC + i + 1))
                    nc.vector.tensor_copy(tok[:, i % 2, :], pst[:]).then_inc(tok_ev, 1)

            def step(tile):
                if t := tile(0):
                    b, q = t[:2]
                    dve.wait_ge(sg_done, b + 1)
                    for k in range(KC):
                        x1 = xT[:, bass.ds(b, 1), k, :].rearrange("p o s -> p (o s)")
                        ts(x1, x1, cols[:, V_BO + k:V_BO + k + 1], None, ALU.add)
                    dve.wait_ge(f2_in, 16 * b + 16)
                    tt(x2[:, q, :, :], x2[:, q, :, :], f2[:], ALU.mult).then_inc(x2_done, 1)
                if t := tile(1):
                    rows_out(t[0], 0)
                if t := tile(0):
                    b, q = t[:2]
                    dve.wait_ge(x2_hi, b + 1)
                    tt(x2l[:, bass.ds(b, 1), :, :].rearrange("p o k s -> p (o k s)"), x2[:, q, :, :].rearrange("p k s -> p (k s)"),
                       x2h[:, bass.ds(b, 1), :, :].rearrange("p o k s -> p (o k s)").bitcast(F32), ALU.subtract).then_inc(x2_lo, 1)
                if t := tile(1):
                    rows_out(t[0], 1)

            pipeline(dve, B, 2, 1, step)

            for q in range(2):
                dve.wait_ge(tok_st[q], 16 * NT // 2 + 16)
            dve.wait_ge(l_T, B + 1)
            dve.wait_ge(sc_done, B + 1)
            dve.wait_ge(consts, 6)
            then(nc.vector.memset(gm[:], -1.0))
            then(red(gm[:, :, 0:NGRP], sc[:].rearrange("p t (g e) -> p t g e", g=NGRP), AX.X, ALU.max))
            for t in range(NT):
                last = nc.vector.max(gv[:, t, :], gm[:, t, :])
            then(last)
            for t in range(NT):
                last = nc.vector.max_index(gi[:, t, :], gv[:, t, :], gm[:, t, :])
            then(last)
            then(nc.vector.tensor_copy(gif[:], gi[:, :, 0:GSEL]))
            for c in range(GSEL):
                last = tt(gk[:, c, :, :], gif[:, :, c:c + 1].broadcast_to([P, NT, NGRP]),
                          iota_g[:].unsqueeze(1).broadcast_to([P, NT, NGRP]), ALU.is_equal)
            then(last)
            then(tt(gk[:, 0, :, :], gk[:, 0, :, :], gk[:, 1, :, :], ALU.add))
            then(ts(gk1[:], gk[:, 0, :, :], -1.0, None, ALU.add))
            spread = lambda g: g.rearrange("p t g -> p (t g)").unsqueeze(2).broadcast_to([P, NT * NGRP, EPG])
            sc3 = sc[:].rearrange("p t (g e) -> p (t g) e", g=NGRP)
            then(tt(sc3, sc3, spread(gk[:, 0, :, :]), ALU.mult))
            then(tt(sc3, sc3, spread(gk1[:]), ALU.add))
            for t in range(NT):
                last = nc.vector.max(wv[:, t, :], sc[:, t, :])
            then(last)
            for t in range(NT):
                last = nc.vector.max_index(ei[:, t, :], wv[:, t, :], sc[:, t, :])
            then(last)
            nc.vector.tensor_copy(eif[:], ei[:])
            then(red(wsum[:], wv[:, :, 0:TOPK], AX.X, ALU.add))
            then(nc.vector.reciprocal(winv[:], wsum[:]))
            tt(wts[:], wv[:], winv[:].unsqueeze(2).broadcast_to([P, NT, 8]), ALU.mult)
            for k in range(TOPK):
                last = tt(oh[:, k, :].rearrange("p (t e) -> p t e", e=E), eif[:, :, k:k + 1].broadcast_to([P, NT, E]),
                          iota_e[:].unsqueeze(1).broadcast_to([P, NT, E]), ALU.is_equal)
            then(last)
            with nc.allow_low_precision(reason="zeros and ones"):
                red(chosen[:], oh[:].rearrange("p k n -> p n k"), AX.X, ALU.add).then_inc(chosen_done, 1)
            split_low(1)
            split_low(2)
            dve.wait_ge(pos_mm, 1)
            then(tt(more[:], pslg[:, 0:E].unsqueeze(2).broadcast_to([P, E, NT]), iota_q[:].unsqueeze(1).broadcast_to([P, E, NT]), ALU.is_gt))
            then(red(nb[:], more[:], AX.X, ALU.add))
            nc.vector.memset(ones_e[:], 1.0)
            then(ts(nb[:], nb[:], 1.0, None, ALU.max))
            then(nc.vector.tensor_tensor_scan(incl[:], ones_e[:], nb[:], 0.0, ALU.mult, ALU.add))
            then(tt(base[:], incl[:], nb[:], ALU.subtract))
            then(ts(base[:], base[:], float(P), None, ALU.mult))
            then(tt(pos[:], psr[:].rearrange("p (t e) -> p t e", e=E), base[:].unsqueeze(1).broadcast_to([P, NT, E]), ALU.add))
            then(tt(oh[:], oh[:], pos[:].rearrange("p t e -> p (t e)").unsqueeze(1).broadcast_to([P, TOPK, NT * E]), ALU.mult))
            then(red(slotf[:].rearrange("p k t -> p (k t)"), oh[:].rearrange("p k (t e) -> p (k t) e", e=E), AX.X, ALU.add))
            nc.vector.memset(slot[:], 0)
            then(ts(more[:, :, 0], incl[:], iota_p[:, 0:1], None, ALU.is_le))
            nc.vector.tensor_copy(slot[:, :, 0:TOPK], slotf[:].rearrange("p k t -> p t k")).then_inc(slot_done, 1)
            then(red(eb[:, 0:1], more[:, :, 0], AX.X, ALU.add))
            then(ts(ebb[:], eb[:, 0:1], float(E - 1), None, ALU.min))
            dve.sem_inc(row_done, 1)
            split_low(3)
            nc.vector.tensor_copy(blocks[:], incl[0:1, :])
            for m in range(POOL_ITEMS, len(SCH)):
                if m == 4:
                    dve.wait_ge(row_mm, 1)
                    then(nc.vector.tensor_copy(ebi[:, 0, :], psl[0:1, 0:P]))
                    then(ts(ebi[:, 1, :], ebi[:, 0, :], 1, None, ALU.bitwise_and))
                    tab2 = tab[:].rearrange("o (b c) -> o b c", c=2)
                    ts(tab2[:, :, 0], psl[0:1, 0:P], 2.0, None, ALU.add)
                    nc.vector.tensor_copy(tab2[:, :, 1], ebi[:, 1, :])
                n = SCH[m][1]
                if 3 < m + 1 < len(SCH):
                    split_low(m + 1)
                with dve.Fori(0, B // 2) as i:
                    for p in range(2):
                        dve.wait_ge(s_done, B * m + 2 * i + (p + 1))
                        tt(hsh[0:n, m, bass.ds(2 * S * i + p * S, S)], sg[0:n, p, :], psu[p][0:n, :], ALU.mult).then_inc(h_dve, 1)


W_UP, W_DOWN, W_N = KC * M, 2 * KC * M, 2 * KC * M + len(MCH) * C
W_PARTS = ((0, W_UP, 1), (W_UP, W_DOWN, 1), (W_DOWN, W_N, 2))


def experts(nc, keep, dr, w_gate, w_up, w_down):
    ident, tab, blocks = keep["ident"], keep["tab"], keep["blocks"]
    with ExitStack() as ctx:
        sb = lambda n, s, d=F32: ctx.enter_context(nc.sbuf_tensor(n, s, d))
        sem = lambda n: ctx.enter_context(nc.semaphore(n))
        ps = lambda n, s=S: ctx.enter_context(nc.psum_tensor(n, [P, s], F32))
        raw = sb("we_raw", [P, W_N])
        wh, wl = sb("we_high", [P, 2, W_N], F32R), sb("we_low", [P, 2, W_N], F32R)
        xg = sb("rows_in", [P, 2, C])
        xth, xtl = sb("xT_high", [P, 2, KC, P], F32R), sb("xT_low", [P, 2, KC, P], F32R)
        sg, hb = sb("silu_e", [P, M]), sb("hidden_e", [P, M])
        hth, htl = sb("hT_high", [P, len(MCH), P], F32R), sb("hT_low", [P, len(MCH), P], F32R)
        yb = sb("rows_out", [P, 2, C])
        psx, psg, psu, psh = ps("xT_ps"), ps("gate_e", M), ps("up_e", M), ps("hT_ps", len(MCH) * P)
        psy = [ps("down_e0"), ps("down_e1")]
        w_in = [sem(f"we_in{i}") for i in range(len(W_PARTS))]
        w_hi, w_split, pad = sem("we_high_done"), sem("we_part_split"), sem("we_pad")
        xg_in, y_out = [sem("rows_in0"), sem("rows_in1")], [sem("rows_out0"), sem("rows_out1")]
        x_T, x_hi, x_lo = sem("x_T_e"), sem("x_hi_e"), sem("x_lo_e")
        gu_mm, s_done, h_done = sem("gate_up_mm"), sem("silu_e_done"), sem("hidden_e_done")
        h_T, h_hi, h_lo = sem("h_T_e"), sem("h_hi_e"), sem("h_lo_e")
        d_mm, y_ev, pool_steps = sem("down_mm"), sem("rows_left"), keep["pool_steps"]
        block = ctx.enter_context(nc.Block())

        @block.sync
        def _(sp):
            with sp.Fori(0, E) as e:
                one = lambda w: w[bass.ds(e, 1)]

                def free(i):
                    sp.wait_ge(w_split, len(W_PARTS) * e + (i + 2))

                for i, w in enumerate((w_gate, w_up)):
                    free(i)
                    at, to, _ = W_PARTS[i]
                    sp.dma_start(raw[:, at:to].rearrange("p (k m) -> p k m", k=KC),
                                 one(w).rearrange("o (k p) m -> p (o k) m", p=P)).then_inc(w_in[i], 16)
                free(2)
                sp.wait_ge(pad, 1)
                sp.dma_start(raw[:, W_DOWN:W_DOWN + 2 * C].rearrange("p (k c) -> p k c", k=2),
                             one(w_down)[:, 0:2 * P, :].rearrange("o (k p) c -> p (o k) c", p=P)).then_inc(w_in[2], 16)
                sp.dma_start(raw[0:M - 2 * P, W_DOWN + 2 * C:], one(w_down)[:, 2 * P:, :].rearrange("o p c -> p (o c)")).then_inc(w_in[2], 16)

        @block.gpsimd
        def _(pool):
            pool.sem_inc(w_split, len(W_PARTS) + 1)
            nc.gpsimd.memset(raw[M - 2 * P:, W_DOWN + 2 * C:], 0.0).then_inc(pad, 1)
            pool.wait_ge(pad, 1)

            def split(e, p, free):
                if free is not None:
                    used = pool.value_load(blocks[0:1, bass.ds(free, 1)], min_val=1, max_val=NBLK)
                for i, (at, to, dmas) in enumerate(W_PARTS):
                    if free is not None and i != 1:
                        pool.wait_ge(gu_mm if i == 0 else d_mm, used + CREDIT)
                    pool.wait_ge(w_in[i], 16 * dmas * e + 16 * dmas)
                    pool.sem_inc(pool_steps, 1)
                    nc.gpsimd.tensor_scalar(wh[:, p, at:to], raw[:, at:to], 1.0, 1.0, ALU.mult, ALU.mult).then_inc(w_hi, 1)
                    pool.wait_ge(w_hi, len(W_PARTS) * e + (i + 1))
                    nc.gpsimd.tensor_tensor(wl[:, p, at:to], raw[:, at:to], wh[:, p, at:to].bitcast(F32),
                                            ALU.subtract).then_inc(w_split, 1)

            split(0, 0, None)
            split(1, 1, None)
            with pool.Fori(1, E // 2) as i:
                for p in range(2):
                    split(2 * i + p, p, 2 * i + (p - 2))

        @block.tensor
        def _(pe):
            for s in (x_T, gu_mm, h_T, d_mm):
                pe.sem_inc(s, CREDIT)

            def step(tile):
                if t := tile(1):
                    expert_gu = pe.value_load(tab[0:1, bass.ds(2 * t[0], 1)], min_val=2, max_val=E + 1)
                    buf_gu = pe.value_load(tab[0:1, bass.ds(2 * t[0] + 1, 1)], min_val=0, max_val=1)
                if t := tile(2):
                    expert_d = pe.value_load(tab[0:1, bass.ds(2 * t[0], 1)], min_val=2, max_val=E + 1)
                    buf_d = pe.value_load(tab[0:1, bass.ds(2 * t[0] + 1, 1)], min_val=0, max_val=1)
                if t := tile(2):
                    n, p = t[:2]
                    pe.wait_ge(h_done, done(n))
                    pe.wait_ge(h_lo, done(n - 1))
                    for c, (at, w) in enumerate(MCH):
                        last = nc.tensor.transpose(psh[0:w, c * P:(c + 1) * P], hb[:, at:at + w], ident[:])
                    last.then_inc(h_T, 1)
                if t := tile(0):
                    n, p, half = t[:3]
                    pe.wait_ge(x_lo, done(n - 1))
                    pe.wait_ge(xg_in[p], 16 * half + 16)
                    for k in range(KC):
                        last = nc.tensor.transpose(psx[:, k * P:(k + 1) * P], xg[:, p, k * P:(k + 1) * P], ident[:])
                    last.then_inc(x_T, 1)
                if t := tile(1):
                    n, p = t[:2]
                    pe.wait_ge(w_split, len(W_PARTS) * expert_gu)
                    pe.wait_ge(x_lo, done(n))
                    pe.wait_ge(h_done, done(n - 1))
                    for bank, at in ((psg, 0), (psu, W_UP)):
                        part = lambda w, k: w[:, bass.ds(buf_gu, 1), at + k * M:at + (k + 1) * M].rearrange("p o m -> p (o m)")
                        last = split_products(nc, bank[:], [((xth[:, p, k, :], xtl[:, p, k, :]), (part(wh, k), part(wl, k)))
                                                            for k in range(KC)], True, True)
                    last.then_inc(gu_mm, 1)
                if t := tile(2):
                    n, p = t[:2]
                    pe.wait_ge(w_split, len(W_PARTS) * expert_d + 1)
                    pe.wait_ge(h_lo, done(n))
                    pe.wait_ge(y_ev, done(n - 2))
                    part = lambda w, c: w[0:MCH[c][1], bass.ds(buf_d, 1), W_DOWN + c * C:W_DOWN + (c + 1) * C].rearrange("p o m -> p (o m)")
                    split_products(nc, psy[p][:], [((hth[0:w, c, :], htl[0:w, c, :]), (part(wh, c), part(wl, c)))
                                                   for c, (at, w) in enumerate(MCH)], True, True).then_inc(d_mm, 1)

            pipeline(pe, NBLK, 4, 2, step)

        @block.scalar
        def _(act):
            for s in (x_hi, s_done, h_hi, y_ev):
                act.sem_inc(s, CREDIT)

            def load(n, p):
                act.dma_start(xg[:, p, :], dr["xs"][bass.ds(P * n, P), :]).then_inc(xg_in[p], 16)

            load(0, 0)
            load(1, 1)

            def step(tile):
                if t := tile(2):
                    n, p = t[:2]
                    act.wait_ge(h_T, done(n))
                    act.wait_ge(d_mm, done(n - 1))
                    nc.scalar.activation(hth[:, 0:2, :], psh[:, 0:2 * P].rearrange("p (c t) -> p c t", c=2), ACT.Copy)
                    nc.scalar.activation(hth[0:M - 2 * P, 2, :], psh[0:M - 2 * P, 2 * P:], ACT.Copy).then_inc(h_hi, 1)
                if t := tile(0):
                    n, p = t[:2]
                    act.wait_ge(x_T, done(n))
                    act.wait_ge(gu_mm, done(n - 2))
                    nc.scalar.activation(xth[:, p, :, :], psx[:].rearrange("p (k t) -> p k t", k=KC), ACT.Copy).then_inc(x_hi, 1)
                    load(n + 2, p)
                if t := tile(1):
                    n, p = t[:2]
                    act.wait_ge(gu_mm, done(n))
                    act.wait_ge(h_done, done(n - 1))
                    nc.scalar.activation(sg[:], psg[:], ACT.Silu).then_inc(s_done, 1)
                if t := tile(2):
                    n, p, half = t[:3]
                    act.wait_ge(y_out[p], 16 * half)
                    act.wait_ge(d_mm, done(n))
                    nc.scalar.activation(yb[:, p, :], psy[p][:], ACT.Copy).then_inc(y_ev, 1)
                    act.wait_ge(y_ev, done(n))
                    act.dma_start(dr["ys"][bass.ds(P * n, P), :], yb[:, p, :]).then_inc(y_out[p], 16)

            pipeline(act, NBLK, 2, 2, step)
            for p in range(2):
                act.wait_ge(y_out[p], 16 * ((NBLK + 1 - p) // 2))
                act.wait_ge(xg_in[p], 16 * ((NBLK + 3 - p) // 2))

        @block.vector
        def _(dve):
            for s in (x_lo, h_done, h_lo):
                dve.sem_inc(s, CREDIT)

            def step(tile):
                if t := tile(2):
                    n, p = t[:2]
                    dve.wait_ge(h_hi, done(n))
                    nc.vector.tensor_tensor(htl[:, 0:2, :], psh[:, 0:2 * P].rearrange("p (c t) -> p c t", c=2),
                                            hth[:, 0:2, :].bitcast(F32), ALU.subtract)
                    nc.vector.tensor_tensor(htl[0:M - 2 * P, 2, :], psh[0:M - 2 * P, 2 * P:],
                                            hth[0:M - 2 * P, 2, :].bitcast(F32), ALU.subtract).then_inc(h_lo, 1)
                if t := tile(0):
                    n, p = t[:2]
                    dve.wait_ge(x_hi, done(n))
                    nc.vector.tensor_tensor(xtl[:, p, :, :], psx[:].rearrange("p (k t) -> p k t", k=KC),
                                            xth[:, p, :, :].bitcast(F32), ALU.subtract).then_inc(x_lo, 1)
                if t := tile(1):
                    n, p = t[:2]
                    dve.wait_ge(s_done, done(n))
                    dve.wait_ge(h_T, done(n - 1))
                    nc.vector.tensor_tensor(hb[:], sg[:], psu[:], ALU.mult).then_inc(h_done, 1)

            pipeline(dve, NBLK, 2, 2, step)


def combine(nc, keep, dr, sw_down, out):
    xT, ident, hsh, wts, slot = (keep[k] for k in ("xT", "ident", "hsh", "wts", "slot"))
    NS = len(SCH)
    with ExitStack() as ctx:
        sb = lambda n, s, d=F32: ctx.enter_context(nc.sbuf_tensor(n, s, d))
        sem = lambda n: ctx.enter_context(nc.semaphore(n))
        raw, wh, wl = sb("sd_raw", [P, NS, C]), sb("sd_high", [P, NS, C], F32R), sb("sd_low", [P, NS, C], F32R)
        hh, hl = sb("h_high", [P, 2, NS, P], F32R), sb("h_low", [P, 2, NS, P], F32R)
        xc = sb("x1_tile", [P, 2, KC, P])
        wt = sb("wts_tile", [P, 2, 8])
        sidx = sb("slot_tile", [P, 2, 8], I32)
        yk = sb("expert_rows", [P, 2, TOPK, C])
        acc, ob = sb("acc", [P, 2, C]), sb("out_rows", [P, 2, C])
        pso = [ctx.enter_context(nc.psum_tensor(f"out_ps{i}", [P, S], F32)) for i in range(2)]
        w_in, w_hi, w_lo = sem("sd_in"), sem("sd_hi"), sem("sd_lo")
        hi, lo, x_c, o_mm = sem("h_hi6"), sem("h_lo6"), sem("x1_copied"), sem("out_mm")
        idx_done, y_in, acc_done, o_done, o_out = (sem("slot6"), [sem("y_in0"), sem("y_in1")], sem("acc_steps"), sem("out_done"),
                                                   [sem("out0"), sem("out1")])
        pool_steps, act_steps = keep["pool_steps"], keep["act_steps"]
        block = ctx.enter_context(nc.Block())
        tail = SCH[-1][1]

        def loop(eng, step):
            with eng.Fori(0, B) as b:
                for t in range(TC):
                    step(TC * b + t, t % 2, (TC // 2) * b + t // 2, b, t)

        @block.sync
        def _(sp):
            for p in range(2):
                sp.sem_inc(o_out[p], 16)
            sp.dma_start(raw[:, 0:NS - 1, :], sw_down[0:(NS - 1) * P, :].rearrange("(k p) c -> p k c", p=P)).then_inc(w_in, 16)
            sp.dma_start(raw[0:tail, NS - 1, :], sw_down[(NS - 1) * P:, :]).then_inc(w_in, 16)

            def step(n, p, half, b, t):
                sp.wait_ge(o_done, done(n))
                sp.dma_start(out[bass.ds(b, 1), t * P:(t + 1) * P, :].rearrange("o p c -> p (o c)"), ob[:, p, :]).then_inc(o_out[p], 16)

            loop(sp, step)
            for p in range(2):
                sp.wait_ge(o_out[p], 16 * NT // 2 + 16)

        @block.gpsimd
        def _(pool):
            def step(n, p, half, b, t):
                pool.wait_ge(o_done, done(n - 2))
                if not (isinstance(half, int) and half == 0):
                    pool.wait_ge(y_in[p], 16 * TOPK * half)
                pool.sem_inc(pool_steps, 1)
                nc.gpsimd.tensor_copy(sidx[:, p, :], slot[:, bass.ds(n, 1), :].rearrange("p o k -> p (o k)")).then_inc(idx_done, 1)
                pool.wait_ge(idx_done, n + 1)
                pool.sem_inc(pool_steps, 1)
                for k in range(TOPK):
                    pool.indirect_dma_start(yk[:, p, k, :], None, dr["ys"],
                                            bass.IndirectOffsetOnAxis(ap=sidx[:, p, k:k + 1], axis=0)).then_inc(y_in[p], 16)

            for t in range(TC):
                step(t, t % 2, t // 2, 0, t)
            with pool.Fori(1, B) as b:
                for t in range(TC):
                    step(TC * b + t, t % 2, (TC // 2) * b + t // 2, b, t)

        @block.tensor
        def _(pe):
            pe.sem_inc(o_mm, CREDIT)
            pe.wait_ge(w_lo, 1)

            def step(n, p, half, b, t):
                pe.wait_ge(lo, done(n))
                pe.wait_ge(o_done, done(n - 2))
                parts = [((hh[0:w, p, c, :], hl[0:w, p, c, :]), (wh[0:w, c, :], wl[0:w, c, :])) for c, (at, w) in enumerate(SCH)]
                split_products(nc, pso[p][:], parts[:1], True, False)
                pe.wait_ge(x_c, done(n))
                for k in range(KC):
                    nc.tensor.matmul(pso[p][:, k * P:(k + 1) * P], xc[:, p, k, :], ident[:], start=False, stop=False)
                split_products(nc, pso[p][:], parts[1:], False, True).then_inc(o_mm, 1)

            loop(pe, step)

        @block.scalar
        def _(act):
            act.sem_inc(hi, CREDIT)
            act.sem_inc(x_c, CREDIT)
            act.wait_ge(w_in, 32)
            nc.scalar.activation(wh[:, 0:NS - 1, :], raw[:, 0:NS - 1, :], ACT.Copy)
            nc.scalar.activation(wh[0:tail, NS - 1, :], raw[0:tail, NS - 1, :], ACT.Copy).then_inc(w_hi, 1)

            def step(n, p, half, b, t):
                act.wait_ge(o_mm, done(n - 2))
                act.sem_inc(act_steps, 1)
                ts = bass.ds(S * b + t * P, P)
                nc.scalar.activation(hh[:, p, 0:NS - 1, :], hsh[:, 0:NS - 1, ts], ACT.Copy)
                nc.scalar.activation(hh[0:tail, p, NS - 1, :], hsh[0:tail, NS - 1, ts], ACT.Copy).then_inc(hi, 1)
                nc.scalar.activation(xc[:, p, :, :], xT[:, bass.ds(b, 1), :, t * P:(t + 1) * P].rearrange("p o k s -> p (o k) s"),
                                     ACT.Copy).then_inc(x_c, 1)

            loop(act, step)

        @block.vector
        def _(dve):
            dve.sem_inc(lo, CREDIT)
            dve.sem_inc(o_done, CREDIT)
            dve.wait_ge(w_hi, 1)
            nc.vector.tensor_tensor(wl[:, 0:NS - 1, :], raw[:, 0:NS - 1, :], wh[:, 0:NS - 1, :].bitcast(F32), ALU.subtract)
            nc.vector.tensor_tensor(wl[0:tail, NS - 1, :], raw[0:tail, NS - 1, :], wh[0:tail, NS - 1, :].bitcast(F32),
                                    ALU.subtract).then_inc(w_lo, 1)

            def step(tile):
                if t := tile(0):
                    n, p = t[:2]
                    dve.wait_ge(hi, done(n))
                    ts = bass.ds(P * n, P)
                    nc.vector.tensor_tensor(hl[:, p, 0:NS - 1, :], hsh[:, 0:NS - 1, ts], hh[:, p, 0:NS - 1, :].bitcast(F32), ALU.subtract)
                    nc.vector.tensor_tensor(hl[0:tail, p, NS - 1, :], hsh[0:tail, NS - 1, ts], hh[0:tail, p, NS - 1, :].bitcast(F32),
                                            ALU.subtract).then_inc(lo, 1)
                if t := tile(1):
                    n, p, half = t[:3]
                    dve.wait_ge(o_done, done(n - 2))
                    dve.wait_ge(o_out[p], 16 * half + 16)
                    nc.vector.tensor_scalar(wt[:, p, :], wts[:, bass.ds(n, 1), :].rearrange("p o k -> p (o k)"), 1.0, None,
                                            ALU.mult).then_inc(acc_done, 1)
                    dve.wait_ge(y_in[p], 16 * TOPK * half + 16 * TOPK)
                    dve.wait_ge(o_mm, done(n))
                    for k in range(TOPK):
                        dve.wait_ge(acc_done, TOPK * n + (k + 1))
                        last = k == TOPK - 1
                        nc.vector.scalar_tensor_tensor(out=(ob if last else acc)[:, p, :], in0=yk[:, p, k, :], scalar=wt[:, p, k:k + 1],
                                                       in1=acc[:, p, :] if k else pso[p][:], op0=ALU.mult,
                                                       op1=ALU.add).then_inc(o_done if last else acc_done, 1)

            pipeline(dve, NT, 2, 1, step)


def build(nc, x, fs, cond, w1, u1, wq, bq, wk, bk, wv, bv, wo, bo, w2, u2,
          gate_w, w_gate, w_up, w_down, sw_gate, sw_up, sw_down, out, stages=9):
    top = ExitStack()
    dram = lambda n, s, d=F32: nc.dram_tensor(n, s, d, kind="Internal").ap()
    dr = dict(
        cT=dram("cT_split", [B, P, 2 * KC * S]),
        q=dram("q_T", [B, NG, P, H * P]),
        f2=dram("f2_T", [B * KC, P, S]),
        x2=dram("x2_rows", [T, C]),
        xs=dram("slots_in", [NBLK_ROOM * P, C]),
        ys=dram("slots_out", [NBLK * P, C]),
    )
    with top:
        sb = lambda n, s, d=F32: top.enter_context(nc.sbuf_tensor(n, s, d))
        keep = dict(
            xT=sb("xT", [P, B, KC, S]),
            ident=sb("ident", [P, P]),
            cols=sb("cols", [P, V_N]),
            bqs=sb("bqs", [P, H]),
            par1=sb("par1", [P, B, KC, 3]),
            par2=sb("par2", [P, B, KC, 3]),
            pool_steps=top.enter_context(nc.semaphore("pool_steps")),
            act_steps=top.enter_context(nc.semaphore("act_steps")),
            cT_stored=top.enter_context(nc.semaphore("cT_stored")),
        )
        with ExitStack() as two:
            s2 = lambda n, s, d=F32: two.enter_context(nc.sbuf_tensor(n, s, d))
            keep["cTh"] = s2("cTh", [P, B, KC, S], F32R)
            keep["cTl"] = s2("cTl", [P, B, KC, S], F32R)
            keep["kT"] = s2("kT", [P, B, KC, S])
            first_gate(nc, keep, dr, x, fs, cond, w1, u1, bq, bk, bv, bo, w2, u2)
            if stages >= 2:
                queries_and_second_gate(nc, keep, dr, wq)
        if stages >= 3:
            attention(nc, keep, dr, wk, wv, wo)
        if stages >= 4:
            with ExitStack() as moe:
                s3 = lambda n, s, d=F32: moe.enter_context(nc.sbuf_tensor(n, s, d))
                keep["hsh"] = s3("hsh", [P, len(SCH), T])
                keep["wts"] = s3("wts", [P, NT, 8])
                keep["slot"] = s3("slot", [P, NT, 8], I32)
                keep["tab"] = s3("tab", [1, 2 * P], I32)
                keep["blocks"] = s3("blocks", [1, E], I32)
                route_and_shared_up(nc, keep, dr, gate_w, sw_gate, sw_up)
                if stages >= 5:
                    experts(nc, keep, dr, w_gate, w_up, w_down)
                if stages >= 6:
                    combine(nc, keep, dr, sw_down, out)


_INS = ['x', 'fside_BxSxS_0', 'cond_512', 'L0_cond_w', 'L0_cond_u', 'L0_attn_Wq', 'L0_attn_bq', 'L0_attn_Wk',
        'L0_attn_bk', 'L0_attn_Wv', 'L0_attn_bv', 'L0_attn_Wo', 'L0_attn_bo', 'L0_cond2_w', 'L0_cond2_u',
        'L0_ffn_gate_w', 'L0_ffn_w_gate', 'L0_ffn_w_up', 'L0_ffn_w_down', 'L0_ffn_sw_gate', 'L0_ffn_sw_up',
        'L0_ffn_sw_down']


def kernel(**inputs):
    import concourse.bacc as bacc
    from concourse.bass_utils import run_bass_kernel_spmd

    nc = bacc.Bacc("TRN2", target_bir_lowering=False, num_devices=1)
    arrays, args = {}, []
    for name in _INS:
        a = np.ascontiguousarray(inputs[name])
        arrays[name] = a
        args.append(nc.dram_tensor(name, a.shape, mybir.dt.from_np(a.dtype), kind="ExternalInput").ap())
    args.append(nc.dram_tensor("out", (B, S, C), F32, kind="ExternalOutput").ap())
    build(nc, *args)
    r = run_bass_kernel_spmd(nc, [arrays], core_ids=[0])
    return r.results[0]["out"]
```
